# Optimizing a Trainium2 kernel written in Bass

```python
import numpy as np
import jax
import jax.numpy as jnp

def _softmax(x, axis=-1):
    return jax.nn.softmax(x, axis=axis)

def _gelu(x):
    return jax.nn.gelu(x, approximate=True)

def _silu(x):
    return jax.nn.silu(x)

def _sigmoid(x):
    return jax.nn.sigmoid(x)

def _layernorm(x, axis=-1, eps=1e-05):
    m = jnp.mean(x, axis=axis, keepdims=True)
    v = jnp.var(x, axis=axis, keepdims=True)
    return (x - m) / jnp.sqrt(v + eps)

def _scatter_add(tgt, idx, src, axis=0):
    return tgt.at[idx].add(src)

def _segment_sum(src, seg, n):
    return jax.ops.segment_sum(src, seg, n)
kernel_name = 'mk_gnn_preln_d4_gnn_r8_9f9e7b'

def setup_inputs(seed: int=0):
    np.random.seed(seed)
    _w = jnp.asarray

    def _rec_inputs():
        import jax
        import jax.numpy as jnp
        _gk = jax.random.key(seed)
        x = -0.0005207 + 1.001 * jax.random.normal(jax.random.fold_in(_gk, 1), (512, 512), jnp.float32)
        src = jax.random.randint(jax.random.fold_in(_gk, 2), (16384,), 0, 512, jnp.int32)
        dst = jnp.minimum((512 * jax.random.uniform(jax.random.fold_in(_gk, 3), (16384,)) ** 2.0).astype(jnp.int32), 4095)
        _o = jnp.argsort(dst, stable=True)
        src = src[_o]
        dst = dst[_o]
        return (x, src, dst)
    x, src, dst = _rec_inputs()

    def _L0_gnn_setup():
        import jax, jax.numpy as jnp
        import numpy as np
        N, E = (512, 16384)
        D_IN, D_OUT, H = (512, 512, 8)
        HEAD = D_OUT // H
        EPS = 1e-05

        def _layer_norm(x, g, b):
            m = jnp.mean(x, axis=-1, keepdims=True)
            v = jnp.mean(jnp.square(x - m), axis=-1, keepdims=True)
            return (x - m) * jax.lax.rsqrt(v + EPS) * g + b
        key = jax.random.key(seed)
        ks = jax.random.split(key, 16)
        s = 1.0 / np.sqrt(D_OUT)
        inp = {'x': jax.random.normal(ks[0], (N, D_IN), dtype=jnp.float32), 'edge_index': jax.random.randint(ks[1], (2, E), 0, N, dtype=jnp.int64), 'Wq': jax.random.normal(ks[2], (D_OUT, D_OUT), jnp.float32) * s, 'bq': jnp.zeros((D_OUT,), jnp.float32), 'Wk': jax.random.normal(ks[3], (D_OUT, D_OUT), jnp.float32) * s, 'bk': jnp.zeros((D_OUT,), jnp.float32), 'Wv': jax.random.normal(ks[4], (D_OUT, D_OUT), jnp.float32) * s, 'bv': jnp.zeros((D_OUT,), jnp.float32), 'Wo': jax.random.normal(ks[5], (D_OUT, D_OUT), jnp.float32) * s, 'bo': jnp.zeros((D_OUT,), jnp.float32), 'W1': jax.random.normal(ks[6], (D_OUT, 2 * D_OUT), jnp.float32) * s, 'b1': jnp.zeros((2 * D_OUT,), jnp.float32), 'W2': jax.random.normal(ks[7], (2 * D_OUT, D_OUT), jnp.float32) * (1.0 / np.sqrt(2 * D_OUT)), 'b2': jnp.zeros((D_OUT,), jnp.float32), 'g1': jnp.ones((D_OUT,), jnp.float32), 'be1': jnp.zeros((D_OUT,), jnp.float32), 'g2': jnp.ones((D_OUT,), jnp.float32), 'be2': jnp.zeros((D_OUT,), jnp.float32)}
        return inp
    _L0_gnn_all = _L0_gnn_setup()
    _L0_gnn_in = {k: v for k, v in _L0_gnn_all.items() if k in ('Wq', 'bq', 'Wk', 'bk', 'Wv', 'bv', 'Wo', 'bo', 'W1', 'b1', 'W2', 'b2', 'g1', 'be1', 'g2', 'be2')}
    del _L0_gnn_all

    def _L1_gnn_setup():
        import jax, jax.numpy as jnp
        import numpy as np
        N = 6250
        IN_CH = 512
        OUT_CH = 512
        DEG = 32
        E = N * DEG
        key = jax.random.key(seed)
        kx, kwc, kwn, kb, ke = jax.random.split(key, 5)
        x = jax.random.normal(kx, (N, IN_CH), dtype=jnp.float32)
        bound = 1.0 / np.sqrt(IN_CH)
        wc = jax.random.uniform(kwc, (IN_CH, OUT_CH), minval=-bound, maxval=bound, dtype=jnp.float32)
        wn = jax.random.uniform(kwn, (IN_CH, OUT_CH), minval=-bound, maxval=bound, dtype=jnp.float32)
        bias = jax.random.uniform(kb, (OUT_CH,), minval=-bound, maxval=bound, dtype=jnp.float32)
        src = jnp.repeat(jnp.arange(N, dtype=jnp.int64), DEG)
        dst = jax.random.randint(ke, (E,), 0, N, dtype=jnp.int64)
        edge_index = jnp.stack([src, dst], axis=0)
        return {'x': x, 'wc': wc, 'wn': wn, 'bias': bias, 'edge_index': edge_index}
    _L1_gnn_all = _L1_gnn_setup()
    _L1_gnn_in = {k: v for k, v in _L1_gnn_all.items() if k in ('wc', 'wn', 'bias')}
    del _L1_gnn_all

    def _L2_gnn_setup():
        import jax, jax.numpy as jnp
        import numpy as np
        N_NODES = 4096
        N_EDGES = 32768
        D = 512
        NUM_EXPERTS = 4
        TOP_K = 2
        LAYERS = 2
        key = jax.random.key(seed)
        ks = jax.random.split(key, 8)
        x = jax.random.normal(ks[0], (N_NODES, D), dtype=jnp.float32)
        edge_index = jax.random.randint(ks[1], (2, N_EDGES), 0, N_NODES, dtype=jnp.int64)
        s = 1.0 / np.sqrt(D)
        gate_W = jax.random.uniform(ks[2], (D, NUM_EXPERTS), jnp.float32, -s, s)
        gate_b = jax.random.uniform(ks[3], (NUM_EXPERTS,), jnp.float32, -s, s)
        Wl = jax.random.uniform(ks[4], (NUM_EXPERTS, LAYERS, D, D), jnp.float32, -s, s)
        bl = jax.random.uniform(ks[5], (NUM_EXPERTS, LAYERS, D), jnp.float32, -s, s)
        Wr = jax.random.uniform(ks[6], (NUM_EXPERTS, LAYERS, D, D), jnp.float32, -s, s)
        return {'x': x, 'gate_W': gate_W, 'gate_b': gate_b, 'Wl': Wl, 'bl': bl, 'Wr': Wr, 'edge_index': edge_index}
    _L2_gnn_all = _L2_gnn_setup()
    _L2_gnn_in = {k: v for k, v in _L2_gnn_all.items() if k in ('gate_W', 'gate_b', 'Wl', 'bl', 'Wr')}
    del _L2_gnn_all

    def _L3_gnn_setup():
        import jax, jax.numpy as jnp
        import numpy as np
        N_NODES = 2500
        N_EDGES = 80000
        D_IN = 512
        D_OUT = 512
        key = jax.random.key(seed)
        kx, ke, kw, kb = jax.random.split(key, 4)
        X = jax.random.normal(kx, (N_NODES, D_IN), dtype=jnp.float32)
        edge_index = jax.random.randint(ke, (2, N_EDGES), 0, N_NODES, dtype=jnp.int32)
        W = jax.random.normal(kw, (D_IN, D_OUT), dtype=jnp.float32) / np.sqrt(D_IN)
        b = jax.random.normal(kb, (D_OUT,), dtype=jnp.float32) * 0.01
        return {'X': X, 'edge_index': edge_index, 'W': W, 'b': b}
    _L3_gnn_all = _L3_gnn_setup()
    _L3_gnn_in = {k: v for k, v in _L3_gnn_all.items() if k in ('W', 'b')}
    del _L3_gnn_all
    return {'x': x, 'src': src, 'dst': dst, 'L0_gnn_Wq': _L0_gnn_in['Wq'], 'L0_gnn_bq': _L0_gnn_in['bq'], 'L0_gnn_Wk': _L0_gnn_in['Wk'], 'L0_gnn_bk': _L0_gnn_in['bk'], 'L0_gnn_Wv': _L0_gnn_in['Wv'], 'L0_gnn_bv': _L0_gnn_in['bv'], 'L0_gnn_Wo': _L0_gnn_in['Wo'], 'L0_gnn_bo': _L0_gnn_in['bo'], 'L0_gnn_W1': _L0_gnn_in['W1'], 'L0_gnn_b1': _L0_gnn_in['b1'], 'L0_gnn_W2': _L0_gnn_in['W2'], 'L0_gnn_b2': _L0_gnn_in['b2'], 'L0_gnn_g1': _L0_gnn_in['g1'], 'L0_gnn_be1': _L0_gnn_in['be1'], 'L0_gnn_g2': _L0_gnn_in['g2'], 'L0_gnn_be2': _L0_gnn_in['be2'], 'L1_gnn_wc': _L1_gnn_in['wc'], 'L1_gnn_wn': _L1_gnn_in['wn'], 'L1_gnn_bias': _L1_gnn_in['bias'], 'L2_gnn_gate_W': _L2_gnn_in['gate_W'], 'L2_gnn_gate_b': _L2_gnn_in['gate_b'], 'L2_gnn_Wl': _L2_gnn_in['Wl'], 'L2_gnn_bl': _L2_gnn_in['bl'], 'L2_gnn_Wr': _L2_gnn_in['Wr'], 'L3_gnn_W': _L3_gnn_in['W'], 'L3_gnn_b': _L3_gnn_in['b']}

def reference(x, src, dst, L0_gnn_Wq, L0_gnn_bq, L0_gnn_Wk, L0_gnn_bk, L0_gnn_Wv, L0_gnn_bv, L0_gnn_Wo, L0_gnn_bo, L0_gnn_W1, L0_gnn_b1, L0_gnn_W2, L0_gnn_b2, L0_gnn_g1, L0_gnn_be1, L0_gnn_g2, L0_gnn_be2, L1_gnn_wc, L1_gnn_wn, L1_gnn_bias, L2_gnn_gate_W, L2_gnn_gate_b, L2_gnn_Wl, L2_gnn_bl, L2_gnn_Wr, L3_gnn_W, L3_gnn_b):
    import jax
    import jax.numpy as jnp

    def _L0_gnn_ref(x, edge_index, Wq, bq, Wk, bk, Wv, bv, Wo, bo, W1, b1, W2, b2, g1, be1, g2, be2):
        import jax, jax.numpy as jnp
        import numpy as np
        N, E = (512, 16384)
        D_IN, D_OUT, H = (512, 512, 8)
        HEAD = D_OUT // H
        EPS = 1e-05

        def _layer_norm(x, g, b):
            m = jnp.mean(x, axis=-1, keepdims=True)
            v = jnp.mean(jnp.square(x - m), axis=-1, keepdims=True)
            return (x - m) * jax.lax.rsqrt(v + EPS) * g + b
        q = (x @ Wq + bq).reshape(N, H, HEAD)
        k = (x @ Wk + bk).reshape(N, H, HEAD)
        v = (x @ Wv + bv).reshape(N, H, HEAD)
        scores = jnp.einsum('nhd,mhd->nhm', q, k) / np.sqrt(HEAD)
        adj = jnp.zeros((N, N), jnp.float32).at[edge_index[0], edge_index[1]].set(1.0)
        scores = jnp.where(adj[:, None, :] == 0, -1000000000.0, scores)
        attn = jax.nn.softmax(scores, axis=1)
        attn_out = jnp.einsum('nhm,mhd->nhd', attn, v).reshape(N, D_OUT)
        attn_out = attn_out @ Wo + bo
        h1 = _layer_norm(x + attn_out, g1, be1)
        ff = jax.nn.relu(h1 @ W1 + b1) @ W2 + b2
        return _layer_norm(h1 + ff, g2, be2)

    def _L1_gnn_ref(x, wc, wn, bias, edge_index):
        import jax, jax.numpy as jnp
        import numpy as np
        N = 6250
        IN_CH = 512
        OUT_CH = 512
        DEG = 32
        E = N * DEG
        alpha = x @ wc
        beta = x @ wn
        src, dst = (edge_index[0], edge_index[1])
        sums = jax.ops.segment_sum(beta[dst], src, num_segments=x.shape[0])
        counts = jax.ops.segment_sum(jnp.ones_like(src, dtype=beta.dtype), src, num_segments=x.shape[0])
        gamma = sums / counts[:, None]
        return alpha + gamma + bias

    def _L2_gnn_ref(x, gate_W, gate_b, Wl, bl, Wr, edge_index):
        import jax, jax.numpy as jnp
        import numpy as np
        N_NODES = 4096
        N_EDGES = 32768
        D = 512
        NUM_EXPERTS = 4
        TOP_K = 2
        LAYERS = 2
        n = x.shape[0]
        src, dst = (edge_index[0], edge_index[1])
        gates = jax.nn.softmax(x @ gate_W + gate_b, axis=-1)
        top_v, top_i = jax.lax.top_k(gates, TOP_K)
        deg = jax.ops.segment_sum(jnp.ones((src.shape[0],), x.dtype), dst, num_segments=n)
        inv_deg = jnp.where(deg > 0, 1.0 / jnp.maximum(deg, 1.0), 0.0)[:, None]

        def sage_conv(h, W_l, b_l, W_r):
            aggr = jax.ops.segment_sum(h[src], dst, num_segments=n) * inv_deg
            return aggr @ W_l + b_l + h @ W_r
        expert_outs = []
        for e in range(NUM_EXPERTS):
            h = x
            for l in range(LAYERS):
                h = sage_conv(h, Wl[e, l], bl[e, l], Wr[e, l])
                h = jax.nn.relu(h)
            expert_outs.append(h)
        expert_outputs = jnp.stack(expert_outs, axis=1)
        sel = jnp.take_along_axis(expert_outputs, top_i[:, :, None], axis=1)
        out = jnp.sum(sel * top_v[:, :, None], axis=1)
        return out

    def _L3_gnn_ref(X, edge_index, W, b):
        import jax, jax.numpy as jnp
        import numpy as np
        N_NODES = 2500
        N_EDGES = 80000
        D_IN = 512
        D_OUT = 512
        n = X.shape[0]
        H = X @ W + b
        src, dst = (edge_index[0], edge_index[1])
        loops = jnp.arange(n, dtype=src.dtype)
        src_f = jnp.concatenate([src, loops])
        dst_f = jnp.concatenate([dst, loops])
        deg = jax.ops.segment_sum(jnp.ones_like(dst_f, dtype=H.dtype), dst_f, num_segments=n)
        inv_sqrt_deg = jax.lax.rsqrt(jnp.maximum(deg, 1.0))
        coef = inv_sqrt_deg[src_f] * inv_sqrt_deg[dst_f]
        msgs = H[src_f] * coef[:, None]
        out = jax.ops.segment_sum(msgs, dst_f, num_segments=n)
        return jax.nn.relu(out)
    edge_index = jnp.stack([src, dst])
    h = jnp.maximum(_layernorm(x, axis=-1), 0.0)
    x = x + _L0_gnn_ref(h, edge_index, L0_gnn_Wq, L0_gnn_bq, L0_gnn_Wk, L0_gnn_bk, L0_gnn_Wv, L0_gnn_bv, L0_gnn_Wo, L0_gnn_bo, L0_gnn_W1, L0_gnn_b1, L0_gnn_W2, L0_gnn_b2, L0_gnn_g1, L0_gnn_be1, L0_gnn_g2, L0_gnn_be2)
    h = jnp.maximum(_layernorm(x, axis=-1), 0.0)
    x = x + _L1_gnn_ref(h, L1_gnn_wc, L1_gnn_wn, L1_gnn_bias, edge_index)
    h = jnp.maximum(_layernorm(x, axis=-1), 0.0)
    x = x + _L2_gnn_ref(h, L2_gnn_gate_W, L2_gnn_gate_b, L2_gnn_Wl, L2_gnn_bl, L2_gnn_Wr, edge_index)
    h = jnp.maximum(_layernorm(x, axis=-1), 0.0)
    x = x + _L3_gnn_ref(h, edge_index, L3_gnn_W, L3_gnn_b)
    return x

_drawn_inputs = setup_inputs


def setup_inputs(seed=0):
    import zlib

    import numpy as np

    out = dict(_drawn_inputs(seed))
    spreads = {'L0_gnn_bq': (0.0, 2.0),
     'L0_gnn_bk': (0.0, 2.0),
     'L0_gnn_bv': (0.0, 0.1),
     'L0_gnn_bo': (0.0, 2.0),
     'L0_gnn_b1': (0.0, 0.1),
     'L0_gnn_b2': (0.0, 0.1),
     'L0_gnn_g1': (1.0, 0.2),
     'L0_gnn_be1': (0.0, 0.1),
     'L0_gnn_g2': (1.0, 0.2),
     'L0_gnn_be2': (0.0, 0.1)}
    factors = {'L0_gnn_Wq': 4.5,
     'L0_gnn_Wk': 4.985,
     'L1_gnn_bias': 3.891,
     'L2_gnn_gate_b': 6.155,
     'L2_gnn_bl': 8.0,
     'L3_gnn_b': 8.0}
    for name, (base, spread) in spreads.items():
        noise = np.random.default_rng([zlib.crc32(name.encode()), seed]).standard_normal(out[name].shape)
        drawn = base * np.exp(spread * noise) if base else spread * noise
        out[name] = jnp.asarray(drawn.astype(out[name].dtype))
    for name, factor in factors.items():
        out[name] = (out[name] * factor).astype(out[name].dtype)
    return out
```

```python
from contextlib import ExitStack

import numpy as np

import concourse.bass as bass
from concourse import mybir
from concourse.alu_op_type import AluOpType as ALU

ACT = mybir.ActivationFunctionType
F32 = mybir.dt.float32
F32R = mybir.dt.float32r
F16 = mybir.dt.float16
BF16 = mybir.dt.bfloat16
I32 = mybir.dt.int32
AX_X = mybir.AxisListType.X

P = 128
EPS = 1e-5
TOP_K = 2


def build(nc, d, out):
    N, D = d["x"].shape
    E = d["src"].shape[0]
    NT = N // P
    DT = D // P
    FT = 2 * D // P
    CH = E // P
    HEADS = 8
    HD = D // HEADS
    PAIRS = HEADS // 2
    EXPERTS = d["L2_gnn_gate_W"].shape[1]
    SCALE = float(HD) ** -0.5
    HN = N // 2
    STEPS = 2 * NT
    OH = 4
    assert N == D == 512 and NT == DT == 4 and HD == 64 and CH % OH == 0

    at = [-(-nc.sbuf_base // 32) * 32]

    def region(size):
        start = at[0]
        at[0] += size
        return start

    def place(name, shape, dt, offset):
        return nc.alloc_sbuf_tensor_at(name, shape, dt, offset=offset)

    MAT = NT * D * 4
    rW, rX, rH, rT, rCT, rQK, rVZ, rEP, rM = (region(k * MAT) for k in (6, 1, 1, 2, 2, 4, 4, 3, 1))
    rB, rBL, rS = region(4 * D * 4), region(2 * D * 4), region(2048 + 1280)

    stage = [place(f"w_stage{i}", [P, 4, D], F32, rW + i * MAT) for i in range(2)]
    w_hi = [place(f"w_hi{i}", [P, 4, D], F32R, rW + (2 + i) * MAT) for i in range(2)]
    w_lo = [place(f"w_lo{i}", [P, 4, D], F32R, rW + (4 + i) * MAT) for i in range(2)]
    x_sb = place("x_sb", [P, NT, D], F32, rX)
    h_sb = place("h_sb", [P, NT, D], F32, rH)
    T_hi = place("T_hi", [P, DT, N], F32R, rT)
    T_lo = place("T_lo", [P, DT, N], F32R, rT + MAT)
    ct_hi = place("ct_hi", [P, NT, N], F32R, rCT)
    ct_lo = place("ct_lo", [P, NT, N], F32R, rCT + MAT)
    q_hi = place("q_hi", [P, PAIRS, N], F32R, rQK)
    q_lo = place("q_lo", [P, PAIRS, N], F32R, rQK + MAT)
    k_hi = place("k_hi", [P, PAIRS, N], F32R, rQK + 2 * MAT)
    k_lo = place("k_lo", [P, PAIRS, N], F32R, rQK + 3 * MAT)
    ff_hi = place("ff_hi", [P, FT, N], F32R, rQK)
    ff_lo = place("ff_lo", [P, FT, N], F32R, rQK + 2 * MAT)
    R_hi = place("R_hi", [P, NT, D], F32R, rQK)
    R_lo = place("R_lo", [P, NT, D], F32R, rQK + MAT)
    agg_hi = place("agg_hi", [P, DT, N], F32R, rQK + 2 * MAT)
    agg_lo = place("agg_lo", [P, DT, N], F32R, rQK + 3 * MAT)
    vz_hi = place("vz_hi", [P, NT, HEADS, P], F32R, rVZ)
    vz_lo = place("vz_lo", [P, NT, HEADS, P], F32R, rVZ + 2 * MAT)
    c_hi = place("c_hi", [P, NT, N], F32R, rVZ)
    c_lo = place("c_lo", [P, NT, N], F32R, rVZ + MAT)
    hid_hi = place("hid_hi", [P, DT, N], F32R, rVZ + 2 * MAT)
    hid_lo = place("hid_lo", [P, DT, N], F32R, rVZ + 3 * MAT)
    tmp = place("tmp", [P, NT, D], F32, rEP)
    e_sb = place("e_sb", [P, HEADS, HN], F32, rEP)
    p_hi = place("p_hi", [P, HEADS, HN], F32R, rEP + MAT)
    p_lo = place("p_lo", [P, HEADS, HN], F32R, rEP + 2 * MAT)
    z_hi = place("z_hi", [P, NT, D], F32R, rEP + MAT)
    z_lo = place("z_lo", [P, NT, D], F32R, rEP + 2 * MAT)
    maskc = place("maskc", [P, NT, N], F32R, rM)
    part = place("part", [P, NT, D], F32, rM)
    one_dst = place("one_dst", [P, OH, N], F16, rEP)
    one_src = place("one_src", [P, OH, N], F16, rEP + OH * N * 2)
    edge_i = place("edge_i", [P, 2, CH], I32, rQK)
    edge_f = place("edge_f", [P, 2, CH], F32, rQK + 2 * CH * 4)
    iota_n = place("iota_n", [P, N], F16, rQK + 4 * CH * 4)
    row = [place(f"row{i}", [P, D], F32, rB + i * D * 4) for i in range(4)]
    row_bl = [place(f"row_bl{i}", [P, D], F32, rBL + i * D * 4) for i in range(2)]
    inv_in_row = place("inv_in_row", [P, N], F32, rS)
    rsum = place("rsum", [P, HN], F32, rS)
    rmask = place("rmask", [P, HN], F32, rS + HN * 4)
    small = [rS + 2048]

    def little(name, shape, dt=F32):
        start = small[0]
        size = int(np.prod(shape[1:])) * (2 if dt == BF16 else 4)
        small[0] += -(-size // 32) * 32
        return place(name, shape, dt, start)

    bq = little("bq", [P, DT])
    bk = little("bk", [P, DT])
    b1 = little("b1", [P, FT])
    bl0 = little("bl0", [P, EXPERTS, DT])
    gate_b = little("gate_b", [P, EXPERTS])
    gate_w = little("gate_w", [P, DT, EXPERTS])
    gw_hi = little("gw_hi", [P, DT, EXPERTS], F32R)
    gw_lo = little("gw_lo", [P, DT, EXPERTS], F32R)
    half_neg = little("half_neg", [P, 1])
    stats = little("stats", [P, 6])
    moments = little("moments", [P, 2])
    vareps = little("vareps", [P, 1])
    rstd = little("rstd", [P, 6 * NT])
    shift = little("shift", [P, 6 * NT])
    in_deg = little("in_deg", [P, NT])
    inv_in = little("inv_in", [P, NT])
    isd = little("isd", [P, NT])
    out_deg = little("out_deg", [P, NT])
    inv_out = little("inv_out", [P, NT])
    no_edge_nan = little("no_edge_nan", [P, NT])
    G1 = [P, NT, EXPERTS]
    logit = little("logit", G1)
    gmax = little("gmax", [P, NT])
    gate = little("gate", G1)
    gsum = little("gsum", [P, NT])
    rank = little("rank", G1)
    beats = little("beats", [P, NT])
    sbuf_end = small[0]
    at[0] = -(-sbuf_end // 32) * 32
    ident = place("ident", [P, P], F32, region(P * 4))
    m_bf = place("m_bf", [P, HN], BF16, rBL)
    neg_ident = place("neg_ident", [P, P], BF16, rBL + HN * 2)
    ones = place("ones", [P, P], F32R, rM)
    assert at[0] <= nc.sbuf_usable_end, (at[0], nc.sbuf_usable_end)

    def matrix(a, rows=slice(0, D), cols=slice(0, D)):
        return a[rows, cols].rearrange("(t p) n -> p t n", p=P)

    w1, w2 = d["L0_gnn_W1"], d["L0_gnn_W2"]
    units = [matrix(d[f"L0_gnn_{n}"]) for n in ("Wq", "Wk", "Wv", "Wo")]
    units += [matrix(w1, cols=slice(j * D, (j + 1) * D)) for j in range(2)]
    units += [matrix(w2, rows=slice(j * D, (j + 1) * D)) for j in range(2)]
    units += [matrix(d["L1_gnn_wn"]), matrix(d["L1_gnn_wc"])]
    FIRST_EXPERT = len(units)
    for e in range(EXPERTS):
        wl, wr = d["L2_gnn_Wl"], d["L2_gnn_Wr"]
        units += [matrix(a[e, layer]) for a, layer in ((wr, 0), (wl, 0), (wl, 1), (wr, 1))]
    units.append(matrix(d["L3_gnn_W"]))
    (WQ, WK, WV, WO, W1A, W1B, W2A, W2B, WN, WC) = range(FIRST_EXPERT)
    W_LAST = len(units) - 1

    rows_in = [("L0_gnn_bv", 0), ("L0_gnn_bo", 1), ("L0_gnn_g1", 2), ("L0_gnn_be1", 3),
               ("L0_gnn_b2", 0), ("L0_gnn_g2", 1), ("L0_gnn_be2", 2), ("L1_gnn_bias", 3),
               ("L3_gnn_b", 0)]
    BV, BO, GAMMA1, BETA1, B2, GAMMA2, BETA2, BIAS1, B3 = range(len(rows_in))

    LN0, LN1, LN2, LN3, LN4, LN5 = range(6)
    ln_order = [(LN0, t) for t in range(NT)] + [(LN1, t) for t in range(NT)]
    ln_order += [(k, t) for t in range(NT) for k in (LN2, LN3)]
    ln_order += [(k, t) for k in (LN4, LN5) for t in range(NT)]

    def ln_no(k, t):
        return ln_order.index((k, t)) + 1

    T0, T1, T3, T4, T5 = range(5)

    def tr_no(k, t):
        return NT * k + t + 1

    ctx = ExitStack()
    with ctx:
        ps = ctx.enter_context(nc.psum_tensor("ps", [P, 8, 512], F32))

        def sem(name):
            return ctx.enter_context(nc.semaphore(name))

        x_in = sem("x_in")
        edges_in = sem("edges_in")
        cols_in = sem("cols_in")
        row_in = [sem(f"row_in{i}") for i in range(4)]
        bl_in = [sem(f"bl_in{i}") for i in range(2)]
        stage_in = [sem(f"stage_in{i}") for i in range(2)]
        hi_made = sem("hi_made")
        lo_made = sem("lo_made")
        consts = sem("consts")
        neg_made = sem("neg_made")
        edges_made = sem("edges_made")
        onehot = sem("onehot")
        onehot_used = sem("onehot_used")
        ct_hi_made = sem("ct_hi_made")
        ct_evac = sem("ct_evac")
        dve = sem("dve")
        pool = sem("pool")
        ln_var = sem("ln_var")
        ln_rstd = sem("ln_rstd")
        ln_scale = sem("ln_scale")
        ln_out = sem("ln_out")
        h_ready = sem("h_ready")
        tr_done = sem("tr_done")
        tr_hi = sem("tr_hi")
        tr_lo = sem("tr_lo")
        q_done, q_hi_made, q_lo_made = sem("q_done"), sem("q_hi_made"), sem("q_lo_made")
        k_done, k_hi_made, k_lo_made = sem("k_done"), sem("k_hi_made"), sem("k_lo_made")
        v_done, v_sum, v_hi_made, v_lo_made = sem("v_done"), sem("v_sum"), sem("v_hi_made"), sem("v_lo_made")
        vz_zero = sem("vz_zero")
        ones_made = sem("ones_made")
        score_done, max_done, centred = sem("score_done"), sem("max_done"), sem("centred")
        exp_done, prob_done, p_hi_made, p_lo_made = sem("exp_done"), sem("prob_done"), sem("p_hi_made"), sem("p_lo_made")
        pv_done = sem("pv_done")
        att_hi_made, att_lo_made = sem("att_hi_made"), sem("att_lo_made")
        bo_added, b2_added, be2_added, bias1_added = sem("bo_added"), sem("b2_added"), sem("be2_added"), sem("bias1_added")
        wo_done, y1_made = sem("wo_done"), sem("y1_made")
        c_tr, c_hi_made, c_lo_tr, c_lo_made = sem("c_tr"), sem("c_hi_made"), sem("c_lo_tr"), sem("c_lo_made")
        ff_done, ff_sum, ff_hi_made, ff_lo_made = sem("ff_done"), sem("ff_sum"), sem("ff_hi_made"), sem("ff_lo_made")
        w2_half_done, w2_done = sem("w2_half_done"), sem("w2_done")
        x1_made = sem("x1_made")
        beta_done, beta_hi_made, beta_lo_made = sem("beta_done"), sem("beta_hi_made"), sem("beta_lo_made")
        alpha_done, alpha_added = sem("alpha_done"), sem("alpha_added")
        gamma_done, x2_made = sem("gamma_done"), sem("x2_made")
        deg_done, deg_made = sem("deg_done"), sem("deg_made")
        pow_ask, pow_made = sem("pow_ask"), sem("pow_made")
        hr_hi_made, hr_lo_made = sem("hr_hi_made"), sem("hr_lo_made")
        gate_split, logits_done, logits_out = sem("gate_split"), sem("logits_done"), sem("logits_out")
        gexp_ask, gexp_done = sem("gexp_ask"), sem("gexp_done")
        agg_done, agg_sum, agg_hi_made, agg_lo_made = sem("agg_done"), sem("agg_sum"), sem("agg_hi_made"), sem("agg_lo_made")
        hid_half_done = sem("hid_half_done")
        hid_done, hid_sum, hid_hi_made, hid_lo_made = sem("hid_done"), sem("hid_sum"), sem("hid_hi_made"), sem("hid_lo_made")
        z_done, z_hi_made, z_lo_made = sem("z_done"), sem("z_hi_made"), sem("z_lo_made")
        own_done, own_made = sem("own_done"), sem("own_made")
        near_done, expert_sum, expert_out = sem("near_done"), sem("expert_sum"), sem("expert_out")
        x3_made = sem("x3_made")
        H_done, H_made, H_hi_made, H_lo_made = sem("H_done"), sem("H_made"), sem("H_hi_made"), sem("H_lo_made")
        last_done, last_sum, last_relu, x4_made = sem("last_done"), sem("last_sum"), sem("last_relu"), sem("x4_made")
        stored = sem("stored")

        block = ctx.enter_context(nc.Block())

        w_spent = [(q_done, DT), (k_done, DT), (v_done, NT), (wo_done, NT), (ff_done, DT), (ff_done, FT),
                   (w2_half_done, NT), (w2_done, NT), (beta_done, NT), (alpha_done, NT)]
        for e in range(EXPERTS):
            w_spent += [(done, 4 * (e + 1)) for done in (hid_half_done, hid_done, z_done, own_done)]

        def f32(t):
            return t.bitcast(F32)

        def score_of(h):
            return ps[:, h % 4, (h // 4) * HN:(h // 4 + 1) * HN]

        def scores_view():
            return ps[:, 0:4, :].rearrange("p b (g n) -> p g b n", g=2)

        @block.sync
        def _(sp):
            sp.dma_start(edge_i[:, 0, :], d["src"].rearrange("(p c) -> p c", p=P)).then_inc(edges_in, 16)
            sp.dma_start(edge_i[:, 1, :], d["dst"].rearrange("(p c) -> p c", p=P)).then_inc(edges_in, 16)
            sp.dma_start(x_sb[:], d["x"].rearrange("(t p) n -> p t n", p=P)).then_inc(x_in, 16)

            row_free = {B2: (v_sum, NT), GAMMA2: (bo_added, NT), BETA2: (h_ready, NT), BIAS1: (h_ready, NT),
                        B3: (b2_added, NT)}

            def load_row(i):
                name, slot = rows_in[i]
                if i in row_free:
                    sp.wait_ge(*row_free[i])
                sp.dma_start(row[slot][:], d[name].unsqueeze(0).to_broadcast([P, D])).then_inc(row_in[slot], 16)

            def load_bl(e):
                if e >= 2:
                    sp.wait_ge(own_made, NT * (e - 1))
                sp.dma_start(row_bl[e % 2][:], d["L2_gnn_bl"][e, 1].unsqueeze(0).to_broadcast([P, D]))\
                  .then_inc(bl_in[e % 2], 16)

            ahead = {WQ: [BV], WK: [BO, GAMMA1], WV: [BETA1], W1B: [B2, GAMMA2], W2A: [BETA2, BIAS1],
                     FIRST_EXPERT + 1: [B3]}
            for u, src in enumerate(units):
                if u >= 2:
                    sp.wait_ge(lo_made, u - 1)
                sp.dma_start(stage[u % 2][:], src).then_inc(stage_in[u % 2], 16)
                for i in ahead.get(u, []):
                    load_row(i)
                if u in (WN, WC):
                    load_bl(u - WN)
                if u in (FIRST_EXPERT + 9, FIRST_EXPERT + 13):
                    load_bl((u - FIRST_EXPERT - 1) // 4)
            for t in range(NT):
                sp.wait_ge(x4_made, t + 1)
                sp.dma_start(out[t * P:(t + 1) * P, :], x_sb[:, t, :]).then_inc(stored, 16)
            sp.wait_ge(stored, 16 * NT)

        @block.gpsimd
        def _(gp):
            gp.iota(iota_n[:], pattern=[[1, N]], base=0, channel_multiplier=0,
                    allow_small_or_imprecise_dtypes=True).then_inc(consts, 1)
            gp.memset(ident[:], 0.0).then_inc(pool, 1)
            gp.memset(half_neg[:], -0.5).then_inc(consts, 1)
            gp.wait_ge(pool, 1)
            gp.affine_select(out=ident[:], in_=ident[:], compare_op=ALU.not_equal, fill=1.0, base=0,
                             pattern=[[-1, P]], channel_multiplier=1).then_inc(consts, 1)
            gp.memset(f32(vz_hi[:]), 0.0).then_inc(vz_zero, 1)
            gp.memset(f32(vz_lo[:]), 0.0).then_inc(vz_zero, 1)

            def split_lo(u):
                gp.wait_ge(hi_made, u + 1)
                if u >= 2:
                    gp.wait_ge(*w_spent[u - 2])
                s = u % 2
                gp.tensor_tensor(w_lo[s][:, 0:2], stage[s][:, 0:2], f32(w_hi[s][:, 0:2]), ALU.subtract)
                gp.tensor_tensor(w_lo[s][:, 2:4], stage[s][:, 2:4], f32(w_hi[s][:, 2:4]), ALU.subtract)\
                  .then_inc(lo_made, 1)

            def rstd_of(k):
                for t in range(NT):
                    power(ln_no(k, t))

            def power(n):
                gp.wait_ge(ln_var, n)
                gp.tensor_tensor(rstd[:, n - 1:n], vareps[:], half_neg[:], ALU.pow).then_inc(ln_rstd, 1)

            def add_row(i, t, target, done):
                slot = rows_in[i][1]
                if t == 0:
                    gp.wait_ge(row_in[slot], 16 * (1 + sum(s == slot for _, s in rows_in[:i])))
                ins = gp.tensor_tensor(target[:, t, :], target[:, t, :], row[slot][:], ALU.add)
                ins.then_inc(done, 1)

            rstd_of(LN0)
            split_lo(WQ)
            split_lo(WK)
            gp.wait_ge(tr_done, tr_no(T0, NT - 1))
            for t in range(NT):
                add_row(BO, t, h_sb, bo_added)
            split_lo(WV)
            split_lo(WO)
            split_lo(W1A)
            rstd_of(LN1)
            for t in range(NT):
                gp.wait_ge(tr_done, tr_no(T1, t))
                add_row(B2, t, h_sb, b2_added)
            gp.memset(f32(ones[:]), 1.0).then_inc(ones_made, 1)
            split_lo(W1B)
            for t in range(NT):
                add_row(BETA2, t, x_sb, be2_added)
            split_lo(W2A)
            split_lo(W2B)
            split_lo(WN)
            for t in range(NT):
                power(ln_no(LN2, t))
                power(ln_no(LN3, t))
            for t in range(NT):
                gp.wait_ge(ln_out, ln_no(LN3, t))
                add_row(BIAS1, t, x_sb, bias1_added)
            split_lo(WC)
            gp.wait_ge(pow_ask, 1)
            gp.tensor_tensor(isd[:], isd[:], half_neg[:].to_broadcast([P, NT]), ALU.pow).then_inc(pow_made, 1)
            split_lo(FIRST_EXPERT)
            rstd_of(LN4)
            for u in range(FIRST_EXPERT + 1, W_LAST + 1):
                split_lo(u)
            rstd_of(LN5)

        @block.scalar
        def _(act):
            with nc.allow_non_contiguous_dma("small per-partition vectors"):
                for dst, src in ((bq[:], d["L0_gnn_bq"].rearrange("(j p) -> p j", p=P)),
                                 (bk[:], d["L0_gnn_bk"].rearrange("(j p) -> p j", p=P)),
                                 (b1[:], d["L0_gnn_b1"].rearrange("(j p) -> p j", p=P)),
                                 (gate_w[:], d["L2_gnn_gate_W"].rearrange("(t p) e -> p t e", p=P)),
                                 (gate_b[:], d["L2_gnn_gate_b"].unsqueeze(0).to_broadcast([P, EXPERTS]))):
                    act.dma_start(dst, src).then_inc(cols_in, 16)
                for e in range(EXPERTS):
                    act.dma_start(bl0[:, e, :], d["L2_gnn_bl"][e, 0].rearrange("(j p) -> p j", p=P))\
                       .then_inc(cols_in, 16)

            def split_hi(u):
                act.wait_ge(stage_in[u % 2], 16 * (u // 2 + 1))
                if u >= 2:
                    act.wait_ge(*w_spent[u - 2])
                nc.scalar.activation(w_hi[u % 2][:], stage[u % 2][:], ACT.Copy).then_inc(hi_made, 1)

            def normalise(k, t, dst, src, func):
                n = ln_no(k, t)
                act.wait_ge(ln_scale, n)
                nc.scalar.activation(dst[:, t, :], src[:, t, :], func, scale=rstd[:, n - 1:n],
                                     bias=shift[:, n - 1:n]).then_inc(ln_out, 1)

            def transposed_hi(k, bank):
                for t in range(NT):
                    act.wait_ge(tr_done, tr_no(k, t))
                    nc.scalar.activation(T_hi[:, :, t * P:(t + 1) * P],
                                         ps[:, bank + t, :].rearrange("p (k n) -> p k n", k=DT),
                                         ACT.Copy).then_inc(tr_hi, 1)

            split_hi(WQ)
            split_hi(WK)
            for t in range(NT):
                normalise(LN0, t, h_sb, x_sb, ACT.Relu)
            transposed_hi(T0, 0)
            for t in range(NT):
                act.wait_ge(onehot_used, CH)
                nc.scalar.activation(ct_hi[:, t, :], ps[:, 4 + t, :], ACT.Copy).then_inc(ct_hi_made, 1)
            act.wait_ge(cols_in, 16 * (5 + EXPERTS))
            for j in range(PAIRS):
                act.wait_ge(q_done, j + 1)
                nc.scalar.activation(q_hi[:, j, :], ps[:, j, :], ACT.Identity, bias=bq[:, j:j + 1])\
                  .then_inc(q_hi_made, 1)
            split_hi(WV)
            for j in range(PAIRS):
                act.wait_ge(k_done, j + 1)
                nc.scalar.activation(k_hi[:, j, :], ps[:, 4 + j, :], ACT.Identity, bias=bk[:, j:j + 1])\
                  .then_inc(k_hi_made, 1)
            split_hi(WO)
            act.wait_ge(vz_zero, 2)
            for t in range(NT):
                act.wait_ge(v_sum, t + 1)
                v = tmp[:, t, :].rearrange("p (j two c) -> p j two c", j=PAIRS, two=2)
                for odd in range(2):
                    last = nc.scalar.activation(vz_hi[:, t, odd::2, odd * HD:(odd + 1) * HD], v[:, :, odd, :],
                                                ACT.Copy)
                last.then_inc(v_hi_made, 1)
            split_hi(W1A)
            def attended_hi(half):
                act.wait_ge(pv_done, NT * (half + 1))
                cols = slice(half * HN, (half + 1) * HN)
                for j in range(PAIRS):
                    nc.scalar.activation(T_hi[:, j, cols], ps[:, 4 + j, cols], ACT.Copy).then_inc(att_hi_made, 1)

            for i in range(STEPS):
                act.wait_ge(centred, i + 1)
                if i == 0:
                    act.wait_ge(v_lo_made, NT)
                else:
                    act.wait_ge(p_lo_made, i)
                nc.scalar.activation(e_sb[:].rearrange("p (g b) n -> p g b n", g=2), scores_view(), ACT.Exp, scale=SCALE).then_inc(exp_done, 1)
                if i == NT:
                    attended_hi(0)
                act.wait_ge(prob_done, i + 1)
                if i >= 1:
                    act.wait_ge(pv_done, i)
                nc.scalar.activation(p_hi[:], e_sb[:], ACT.Copy).then_inc(p_hi_made, 1)
            attended_hi(1)
            for t in range(NT):
                normalise(LN1, t, h_sb, h_sb, ACT.Identity)
            for t in range(NT):
                act.wait_ge(c_tr, t + 1)
                nc.scalar.activation(c_hi[:, t, :], ps[:, 4 + t, :], ACT.Copy).then_inc(c_hi_made, 1)
            split_hi(W1B)
            transposed_hi(T1, 0)
            for j in range(FT):
                act.wait_ge(ff_done, j + 1)
                nc.scalar.activation(ff_hi[:, j, :], ps[:, (4 + j) % 8, :], ACT.Relu, bias=b1[:, j:j + 1])\
                  .then_inc(ff_hi_made, 1)
                if j == DT:
                    split_hi(W2A)
            split_hi(W2B)
            split_hi(WN)
            for t in range(NT):
                act.wait_ge(c_lo_tr, t + 1)
                nc.scalar.activation(c_lo[:, t, :], ps[:, t, :], ACT.Copy).then_inc(c_lo_made, 1)
            for t in range(NT):
                normalise(LN2, t, h_sb, h_sb, ACT.Identity)
                normalise(LN3, t, h_sb, x_sb, ACT.Relu)
            split_hi(WC)
            transposed_hi(T3, 0)
            for t in range(NT):
                act.wait_ge(beta_done, t + 1)
                nc.scalar.activation(R_hi[:, t, :], ps[:, 4 + t, :], ACT.Copy).then_inc(beta_hi_made, 1)
            split_hi(FIRST_EXPERT)
            for t in range(NT):
                normalise(LN4, t, h_sb, x_sb, ACT.Relu)
                if t == 0:
                    act.wait_ge(gamma_done, NT)
                nc.scalar.wait_ge(ln_out, ln_no(LN4, t))
                nc.scalar.activation(R_hi[:, t, :], h_sb[:, t, :], ACT.Copy).then_inc(hr_hi_made, 1)
            split_hi(FIRST_EXPERT + 1)
            transposed_hi(T4, 4)
            act.wait_ge(gexp_ask, 1)
            nc.scalar.activation(gate[:], logit[:], ACT.Exp).then_inc(gexp_done, 1)
            for j in range(DT):
                act.wait_ge(agg_sum, j + 1)
                nc.scalar.activation(agg_hi[:, j, :], tmp[:, j, :], ACT.Copy).then_inc(agg_hi_made, 1)
            for e in range(EXPERTS):
                u = FIRST_EXPERT + 4 * e
                for j in range(DT):
                    act.wait_ge(hid_done, DT * e + j + 1)
                    nc.scalar.activation(hid_hi[:, j, :], ps[:, 4 + j, :], ACT.Relu, bias=bl0[:, e, j:j + 1])\
                      .then_inc(hid_hi_made, 1)
                split_hi(u + 2)
                split_hi(u + 3)
                for t in range(NT):
                    act.wait_ge(z_done, NT * e + t + 1)
                    nc.scalar.activation(z_hi[:, t, :], ps[:, t, :], ACT.Copy).then_inc(z_hi_made, 1)
                split_hi(u + 4)
                if e < EXPERTS - 1:
                    split_hi(u + 5)
                for t in range(NT):
                    act.wait_ge(expert_sum, NT * e + t + 1)
                    nc.scalar.activation(part[:, t, :], part[:, t, :], ACT.Relu, scale=gate[:, t, e:e + 1])\
                      .then_inc(expert_out, 1)
            for t in range(NT):
                normalise(LN5, t, h_sb, x_sb, ACT.Relu)
            transposed_hi(T5, 4)
            for t in range(NT):
                act.wait_ge(H_made, t + 1)
                nc.scalar.activation(R_hi[:, t, :], tmp[:, t, :], ACT.Copy).then_inc(H_hi_made, 1)
            for t in range(NT):
                act.wait_ge(last_sum, t + 1)
                nc.scalar.activation(tmp[:, t, :], tmp[:, t, :], ACT.Relu, scale=isd[:, t:t + 1])\
                  .then_inc(last_relu, 1)

        @block.vector
        def _(v):
            order = [0]

            def link(ins):
                order[0] += 1
                ins.then_inc(dve, 1)
                v.wait_ge(dve, order[0])

            def norm_scale(k, t, src):
                n = ln_no(k, t)
                link(nc.vector.bn_stats(stats[:], src[:, t, :]))
                link(nc.vector.bn_aggr(moments[:], stats[:]))
                nc.vector.tensor_scalar(vareps[:], moments[:, 1:2], EPS, None, ALU.add).then_inc(ln_var, 1)
                v.wait_ge(ln_rstd, n)
                nc.vector.scalar_tensor_tensor(shift[:, n - 1:n], moments[:, 0:1], -1.0,
                                               rstd[:, n - 1:n], ALU.mult, ALU.mult).then_inc(ln_scale, 1)

            def wait_row(i):
                slot = rows_in[i][1]
                v.wait_ge(row_in[slot], 16 * (1 + sum(s == slot for _, s in rows_in[:i])))
                return row[slot]

            def transposed_lo(k, bank):
                for t in range(NT):
                    v.wait_ge(tr_hi, tr_no(k, t))
                    cols = slice(t * P, (t + 1) * P)
                    nc.vector.tensor_tensor(T_lo[:, :, cols], ps[:, bank + t, :].rearrange("p (k n) -> p k n", k=DT),
                                            f32(T_hi[:, :, cols]), ALU.subtract).then_inc(tr_lo, 1)

            v.wait_ge(edges_in, 32)
            link(nc.vector.tensor_copy(edge_f[:], edge_i[:]))
            v.wait_ge(consts, 3)
            nc.vector.tensor_scalar(neg_ident[:], ident[:], -1.0, None, ALU.mult).then_inc(neg_made, 1)

            def one_hots(slot, c):
                nc.vector.tensor_scalar(one_dst[:, slot, :], iota_n[:], edge_f[:, 1, bass.ds(c, 1)], None,
                                        ALU.is_equal)
                nc.vector.tensor_scalar(one_src[:, slot, :], iota_n[:], edge_f[:, 0, bass.ds(c, 1)], None,
                                        ALU.is_equal).then_inc(onehot, 1)

            for s in range(OH):
                one_hots(s, s)
            with v.Fori(1, CH // OH) as g:
                for s in range(OH):
                    v.wait_ge(onehot_used, g * OH + (s + 1 - OH))
                    one_hots(s, g * OH + s)

            v.wait_ge(x_in, 16)
            for t in range(NT):
                norm_scale(LN0, t, x_sb)
            transposed_lo(T0, 0)
            for t in range(NT):
                v.wait_ge(ct_hi_made, t + 1)
                nc.vector.tensor_tensor(ct_lo[:, t, :], ps[:, 4 + t, :], f32(ct_hi[:, t, :]), ALU.subtract)
                nc.vector.tensor_reduce(in_deg[:, t:t + 1], ps[:, 4 + t, :], AX_X, ALU.add)
                nc.vector.tensor_scalar(maskc[:, t, :], ps[:, 4 + t, :], 0.0, 1.0 / HEADS, ALU.is_equal,
                                        ALU.mult).then_inc(ct_evac, 1)
            for j in range(PAIRS):
                v.wait_ge(q_hi_made, j + 1)
                nc.vector.scalar_tensor_tensor(q_lo[:, j, :], ps[:, j, :], bq[:, j:j + 1], f32(q_hi[:, j, :]),
                                               ALU.add, ALU.subtract).then_inc(q_lo_made, 1)
            for j in range(PAIRS):
                v.wait_ge(k_hi_made, j + 1)
                nc.vector.scalar_tensor_tensor(k_lo[:, j, :], ps[:, 4 + j, :], bk[:, j:j + 1], f32(k_hi[:, j, :]),
                                               ALU.add, ALU.subtract).then_inc(k_lo_made, 1)
            bv_row = wait_row(BV)
            for t in range(NT):
                v.wait_ge(v_done, t + 1)
                nc.vector.tensor_tensor(tmp[:, t, :], ps[:, t, :], bv_row[:], ALU.add).then_inc(v_sum, 1)
            for t in range(NT):
                v.wait_ge(v_hi_made, t + 1)
                if t == 0:
                    v.wait_ge(v_sum, NT)
                vals = tmp[:, t, :].rearrange("p (j two c) -> p j two c", j=PAIRS, two=2)
                for odd in range(2):
                    cols = slice(odd * HD, (odd + 1) * HD)
                    last = nc.vector.tensor_tensor(vz_lo[:, t, odd::2, cols], vals[:, :, odd, :],
                                                   f32(vz_hi[:, t, odd::2, cols]), ALU.subtract)
                last.then_inc(v_lo_made, 1)

            def attended_lo(half):
                cols = slice(half * HN, (half + 1) * HN)
                for j in range(PAIRS):
                    v.wait_ge(att_hi_made, PAIRS * half + j + 1)
                    nc.vector.tensor_tensor(T_lo[:, j, cols], ps[:, 4 + j, cols], f32(T_hi[:, j, cols]),
                                            ALU.subtract).then_inc(att_lo_made, 1)

            for i in range(STEPS):
                mt, half = i % NT, i // NT
                v.wait_ge(score_done, i + 1)
                if i >= 1:
                    v.wait_ge(centred, i)
                nc.vector.tensor_reduce(m_bf[:], ps[:, 0:4, :].rearrange("p b (g n) -> p n g b", g=2),
                                        mybir.AxisListType.XY, ALU.max).then_inc(max_done, 1)
                if i == NT:
                    attended_lo(0)
                v.wait_ge(exp_done, i + 1)
                link(nc.vector.tensor_reduce(rsum[:], e_sb[:].rearrange("p h n -> p n h"), AX_X, ALU.add))
                link(nc.vector.reciprocal(rsum[:], rsum[:]))
                link(nc.vector.scalar_tensor_tensor(rmask[:], f32(ct_hi[:, mt, half * HN:(half + 1) * HN]), 0.0,
                                                    rsum[:], ALU.is_gt, ALU.mult))
                nc.vector.tensor_tensor(e_sb[:], e_sb[:], rmask[:].unsqueeze(1).to_broadcast([P, HEADS, HN]),
                                        ALU.mult).then_inc(prob_done, 1)
                v.wait_ge(p_hi_made, i + 1)
                nc.vector.tensor_tensor(p_lo[:], e_sb[:], f32(p_hi[:]), ALU.subtract).then_inc(p_lo_made, 1)
            attended_lo(1)

            g1_row, be1_row = wait_row(GAMMA1), wait_row(BETA1)
            for t in range(NT):
                v.wait_ge(wo_done, t + 1)
                v.wait_ge(bo_added, t + 1)
                link(nc.vector.tensor_tensor(h_sb[:, t, :], ps[:, t, :], h_sb[:, t, :], ALU.add))
                norm_scale(LN1, t, h_sb)
                v.wait_ge(ln_out, ln_no(LN1, t))
                link(nc.vector.tensor_tensor(h_sb[:, t, :], h_sb[:, t, :], g1_row[:], ALU.mult))
                ins = nc.vector.tensor_tensor(h_sb[:, t, :], h_sb[:, t, :], be1_row[:], ALU.add)
                ins.then_inc(h_ready, 1)
            v.wait_ge(h_ready, NT)
            transposed_lo(T1, 0)
            for j in range(FT):
                v.wait_ge(ff_hi_made, j + 1)
                if j >= NT:
                    v.wait_ge(ff_lo_made, j - NT + 1)
                link(nc.vector.tensor_scalar(tmp[:, j % NT, :], ps[:, (4 + j) % 8, :], b1[:, j:j + 1], 0.0,
                                             ALU.add, ALU.max))
                nc.vector.tensor_tensor(ff_lo[:, j, :], tmp[:, j % NT, :], f32(ff_hi[:, j, :]),
                                        ALU.subtract).then_inc(ff_lo_made, 1)

            g2_row = wait_row(GAMMA2)
            for t in range(NT):
                v.wait_ge(w2_done, t + 1)
                v.wait_ge(b2_added, t + 1)
                link(nc.vector.tensor_tensor(h_sb[:, t, :], ps[:, 4 + t, :], h_sb[:, t, :], ALU.add))
                norm_scale(LN2, t, h_sb)
                v.wait_ge(ln_out, ln_no(LN2, t))
                v.wait_ge(be2_added, t + 1)
                link(nc.vector.tensor_tensor(h_sb[:, t, :], h_sb[:, t, :], g2_row[:], ALU.mult))
                link(nc.vector.tensor_tensor(x_sb[:, t, :], x_sb[:, t, :], h_sb[:, t, :], ALU.add))
                norm_scale(LN3, t, x_sb)
            transposed_lo(T3, 0)

            v.wait_ge(c_hi_made, NT)
            v.wait_ge(c_lo_made, NT)
            link(nc.vector.tensor_reduce(out_deg[:], f32(c_hi[:]), AX_X, ALU.add))
            link(nc.vector.tensor_reduce(inv_out[:], f32(c_lo[:]), AX_X, ALU.add))
            link(nc.vector.tensor_tensor(out_deg[:], out_deg[:], inv_out[:], ALU.add))
            link(nc.vector.reciprocal(no_edge_nan[:], out_deg[:]))
            link(nc.vector.tensor_scalar(no_edge_nan[:], no_edge_nan[:], 0.0, None, ALU.mult))
            link(nc.vector.tensor_scalar(out_deg[:], out_deg[:], 1.0, None, ALU.max))
            link(nc.vector.reciprocal(inv_out[:], out_deg[:]))
            nc.vector.tensor_scalar(isd[:], in_deg[:], 1.0, None, ALU.add).then_inc(pow_ask, 1)
            link(nc.vector.tensor_scalar(inv_in[:], in_deg[:], 1.0, None, ALU.max))
            link(nc.vector.reciprocal(inv_in[:], inv_in[:]))

            for t in range(NT):
                v.wait_ge(beta_hi_made, t + 1)
                nc.vector.tensor_tensor(R_lo[:, t, :], ps[:, 4 + t, :], f32(R_hi[:, t, :]), ALU.subtract)\
                  .then_inc(beta_lo_made, 1)
            for t in range(NT):
                v.wait_ge(alpha_done, t + 1)
                v.wait_ge(bias1_added, t + 1)
                nc.vector.tensor_tensor(x_sb[:, t, :], ps[:, t, :], x_sb[:, t, :], ALU.add).then_inc(alpha_added, 1)
            v.wait_ge(alpha_added, NT)
            for t in range(NT):
                v.wait_ge(gamma_done, t + 1)
                ins = nc.vector.scalar_tensor_tensor(x_sb[:, t, :], ps[:, 4 + t, :], inv_out[:, t:t + 1],
                                                     x_sb[:, t, :], ALU.mult, ALU.add)
                ins.then_inc(x2_made, 1)
                v.wait_ge(x2_made, t + 1)
                norm_scale(LN4, t, x_sb)
            for t in range(NT):
                v.wait_ge(hr_hi_made, t + 1)
                nc.vector.tensor_tensor(R_lo[:, t, :], h_sb[:, t, :], f32(R_hi[:, t, :]), ALU.subtract)\
                  .then_inc(hr_lo_made, 1)
            transposed_lo(T4, 4)
            v.wait_ge(deg_done, 1)
            link(nc.vector.tensor_scalar(inv_in_row[:], ps[:, 0, :], 1.0, None, ALU.max))
            nc.vector.reciprocal(inv_in_row[:], inv_in_row[:]).then_inc(deg_made, 1)
            v.wait_ge(cols_in, 16 * (5 + EXPERTS))
            link(nc.vector.tensor_copy(gw_hi[:], gate_w[:]))
            nc.vector.tensor_tensor(gw_lo[:], gate_w[:], f32(gw_hi[:]), ALU.subtract).then_inc(gate_split, 1)

            def over_experts(a):
                return a[:].unsqueeze(2).to_broadcast([P, NT, EXPERTS])

            v.wait_ge(logits_done, 1)
            ins = nc.vector.tensor_tensor(logit[:], ps[:, 4, 0:NT * EXPERTS].rearrange("p (t e) -> p t e", t=NT),
                                          gate_b[:].unsqueeze(1).to_broadcast([P, NT, EXPERTS]), ALU.add)
            ins.then_inc(logits_out, 1)
            v.wait_ge(logits_out, 1)
            link(nc.vector.tensor_reduce(gmax[:], logit[:], AX_X, ALU.max))
            nc.vector.tensor_tensor(logit[:], logit[:], over_experts(gmax), ALU.subtract).then_inc(gexp_ask, 1)
            v.wait_ge(gexp_done, 1)
            link(nc.vector.tensor_reduce(gsum[:], gate[:], AX_X, ALU.add))
            link(nc.vector.reciprocal(gsum[:], gsum[:]))
            link(nc.vector.tensor_tensor(gate[:], gate[:], over_experts(gsum), ALU.mult))
            for e in range(EXPERTS):
                first = True
                for o in range(EXPERTS):
                    if o == e:
                        continue
                    goal = rank[:, :, e] if first else beats[:]
                    link(nc.vector.tensor_tensor(goal, gate[:, :, o], gate[:, :, e],
                                                 ALU.is_ge if o < e else ALU.is_gt))
                    if not first:
                        link(nc.vector.tensor_tensor(rank[:, :, e], rank[:, :, e], beats[:], ALU.add))
                    first = False
            link(nc.vector.scalar_tensor_tensor(gate[:], rank[:], TOP_K - 0.5, gate[:], ALU.is_lt, ALU.mult))

            v.wait_ge(deg_made, 1)
            for j in range(DT):
                v.wait_ge(agg_done, j + 1)
                nc.vector.tensor_tensor(tmp[:, j, :], ps[:, j, :], inv_in_row[:], ALU.mult).then_inc(agg_sum, 1)
                v.wait_ge(agg_hi_made, j + 1)
                nc.vector.tensor_tensor(agg_lo[:, j, :], tmp[:, j, :], f32(agg_hi[:, j, :]), ALU.subtract)\
                  .then_inc(agg_lo_made, 1)

            for e in range(EXPERTS):
                if e == 0:
                    v.wait_ge(agg_lo_made, DT)
                else:
                    v.wait_ge(hid_lo_made, DT * e)
                for j in range(DT):
                    v.wait_ge(hid_hi_made, DT * e + j + 1)
                    link(nc.vector.tensor_scalar(tmp[:, j, :], ps[:, 4 + j, :], bl0[:, e, j:j + 1], 0.0,
                                                 ALU.add, ALU.max))
                    nc.vector.tensor_tensor(hid_lo[:, j, :], tmp[:, j, :], f32(hid_hi[:, j, :]), ALU.subtract)\
                      .then_inc(hid_lo_made, 1)
                for t in range(NT):
                    v.wait_ge(z_hi_made, NT * e + t + 1)
                    nc.vector.tensor_tensor(z_lo[:, t, :], ps[:, t, :], f32(z_hi[:, t, :]), ALU.subtract)\
                      .then_inc(z_lo_made, 1)
                v.wait_ge(bl_in[e % 2], 16 * (e // 2 + 1))
                if e >= 1:
                    v.wait_ge(x3_made, NT * e)
                for t in range(NT):
                    v.wait_ge(own_done, NT * e + t + 1)
                    nc.vector.tensor_tensor(part[:, t, :], ps[:, 4 + t, :], row_bl[e % 2][:], ALU.add)\
                      .then_inc(own_made, 1)
                v.wait_ge(own_made, NT * (e + 1))
                for t in range(NT):
                    v.wait_ge(near_done, NT * e + t + 1)
                    nc.vector.scalar_tensor_tensor(part[:, t, :], ps[:, t, :], inv_in[:, t:t + 1], part[:, t, :],
                                                   ALU.mult, ALU.add).then_inc(expert_sum, 1)
                for t in range(NT):
                    v.wait_ge(expert_out, NT * e + t + 1)
                    nc.vector.tensor_tensor(x_sb[:, t, :], x_sb[:, t, :], part[:, t, :], ALU.add)\
                      .then_inc(x3_made, 1)
                    if e == EXPERTS - 1:
                        v.wait_ge(x3_made, NT * e + t + 1)
                        norm_scale(LN5, t, x_sb)

            transposed_lo(T5, 4)
            b3_row = wait_row(B3)
            for t in range(NT):
                v.wait_ge(H_done, t + 1)
                link(nc.vector.tensor_tensor(tmp[:, t, :], ps[:, t, :], b3_row[:], ALU.add))
                if t == 0:
                    v.wait_ge(pow_made, 1)
                nc.vector.tensor_scalar(tmp[:, t, :], tmp[:, t, :], isd[:, t:t + 1], None, ALU.mult)\
                  .then_inc(H_made, 1)
                v.wait_ge(H_hi_made, t + 1)
                nc.vector.tensor_tensor(R_lo[:, t, :], tmp[:, t, :], f32(R_hi[:, t, :]), ALU.subtract)\
                  .then_inc(H_lo_made, 1)
            v.wait_ge(H_lo_made, NT)
            for t in range(NT):
                v.wait_ge(last_done, t + 1)
                nc.vector.tensor_tensor(tmp[:, t, :], ps[:, 4 + t, :], tmp[:, t, :], ALU.add).then_inc(last_sum, 1)
            for t in range(NT):
                v.wait_ge(last_relu, t + 1)
                nc.vector.scalar_tensor_tensor(x_sb[:, t, :], tmp[:, t, :], no_edge_nan[:, t:t + 1], x_sb[:, t, :],
                                               ALU.add, ALU.add).then_inc(x4_made, 1)

        @block.tensor
        def _(pe):
            def mm3(goal, a_hi, a_lo, b_hi, b_lo, start, stop, **kw):
                nc.tensor.matmul(goal, a_hi, b_hi, start=start, stop=False, **kw)
                nc.tensor.matmul(goal, a_hi, b_lo, start=False, stop=False, **kw)
                return nc.tensor.matmul(goal, a_lo, b_hi, start=False, stop=stop, **kw)

            def weights(u):
                pe.wait_ge(lo_made, u + 1)
                return w_hi[u % 2], w_lo[u % 2]

            def transposes(k, bank, ready):
                for t in range(NT):
                    ready(t)
                    for j in range(DT):
                        last = nc.tensor.transpose(ps[:, bank + t, j * P:(j + 1) * P],
                                                   h_sb[:, t, j * P:(j + 1) * P], ident[:])
                    last.then_inc(tr_done, 1)

            def ln_ready(k):
                return lambda t: pe.wait_ge(ln_out, ln_no(k, t))

            def col(t):
                return slice(t * P, (t + 1) * P)

            def count(slot, value, start, stop):
                pe.wait_ge(onehot, value)
                for t in range(NT):
                    last = nc.tensor.matmul(ps[:, 4 + t, :], one_dst[:, slot, col(t)], one_src[:, slot, :],
                                            start=start, stop=stop, skip_group_check=True)
                return last

            count(0, 1, True, False).then_inc(onehot_used, 1)
            for s in range(1, OH):
                count(s, s + 1, False, False).then_inc(onehot_used, 1)
            with pe.Fori(1, CH // OH) as g:
                for s in range(OH):
                    count(s, g * OH + (s + 1), False, s == OH - 1).then_inc(onehot_used, 1)

            transposes(T0, 0, ln_ready(LN0))
            pe.wait_ge(tr_lo, tr_no(T0, NT - 1))
            hi, lo = weights(WQ)
            for j in range(DT):
                for k in range(DT):
                    last = mm3(ps[:, j, :], hi[:, k, col(j)], lo[:, k, col(j)], T_hi[:, k, :], T_lo[:, k, :],
                               k == 0, k == DT - 1)
                last.then_inc(q_done, 1)
            hi, lo = weights(WK)
            for j in range(DT):
                pe.wait_ge(ct_evac, j + 1)
                for k in range(DT):
                    last = mm3(ps[:, 4 + j, :], hi[:, k, col(j)], lo[:, k, col(j)], T_hi[:, k, :], T_lo[:, k, :],
                               k == 0, k == DT - 1)
                last.then_inc(k_done, 1)
            hi, lo = weights(WV)
            for t in range(NT):
                pe.wait_ge(q_lo_made, t + 1)
                for k in range(DT):
                    last = mm3(ps[:, t, :], T_hi[:, k, col(t)], T_lo[:, k, col(t)], hi[:, k, :], lo[:, k, :],
                               k == 0, k == DT - 1)
                last.then_inc(v_done, 1)

            def scores(i):
                mt, half = i % NT, i // NT
                if i == 0:
                    pe.wait_ge(v_sum, NT)
                    pe.wait_ge(k_lo_made, PAIRS)
                    pe.wait_ge(neg_made, 1)
                else:
                    pe.wait_ge(exp_done, i)
                for h in range(HEADS):
                    rows, j = slice(HD * (h % 2), HD * (h % 2 + 1)), h // 2
                    q = slice(half * HN, (half + 1) * HN)
                    last = mm3(score_of(h), k_hi[rows, j, col(mt)], k_lo[rows, j, col(mt)], q_hi[rows, j, q],
                               q_lo[rows, j, q], h < 4, False, skip_group_check=True)
                last.then_inc(score_done, 1)

            def centre(i):
                pe.wait_ge(max_done, i + 1)
                for h in range(HEADS):
                    last = nc.tensor.matmul(score_of(h), neg_ident[:], m_bf[:], start=False, stop=True,
                                            skip_group_check=True)
                last.then_inc(centred, 1)

            def values(i):
                mt, half = i % NT, i // NT
                if i == 0:
                    pe.wait_ge(v_lo_made, NT)
                pe.wait_ge(p_lo_made, i + 1)
                q = slice(half * HN, (half + 1) * HN)
                for j in range(PAIRS):
                    goal = ps[:, 4 + j, q]
                    for h in (2 * j, 2 * j + 1):
                        mm3(goal, vz_hi[:, mt, h, :], vz_lo[:, mt, h, :], p_hi[:, h, :], p_lo[:, h, :],
                            mt == 0 and h % 2 == 0, False)
                        for vz in (vz_hi, vz_lo):
                            last = nc.tensor.matmul(goal, vz[:, mt, h, :], maskc[:, mt, q], start=False,
                                                    stop=mt == NT - 1 and h % 2 == 1 and vz is vz_lo)
                last.then_inc(pv_done, 1)

            scores(0)
            centre(0)
            for i in range(1, STEPS):
                scores(i)
                centre(i)
                values(i - 1)
            values(STEPS - 1)

            pe.wait_ge(att_lo_made, 2 * PAIRS)
            hi, lo = weights(WO)
            for t in range(NT):
                for k in range(DT):
                    last = mm3(ps[:, t, :], T_hi[:, k, col(t)], T_lo[:, k, col(t)], hi[:, k, :], lo[:, k, :],
                               k == 0, k == DT - 1)
                last.then_inc(wo_done, 1)

            def count_transposes(src, bank, done):
                for s in range(NT):
                    for t in range(NT):
                        last = nc.tensor.transpose(ps[:, bank + s, col(t)], f32(src[:, t, col(s)]), ident[:])
                    last.then_inc(done, 1)

            count_transposes(ct_hi, 4, c_tr)
            transposes(T1, 0, lambda t: pe.wait_ge(h_ready, t + 1))

            pe.wait_ge(tr_lo, tr_no(T1, NT - 1))
            for j in range(FT):
                if j % DT == 0:
                    hi, lo = weights(W1A + j // DT)
                if j < DT:
                    pe.wait_ge(c_hi_made, j + 1)
                for k in range(DT):
                    last = mm3(ps[:, (4 + j) % 8, :], hi[:, k, col(j % DT)], lo[:, k, col(j % DT)],
                               T_hi[:, k, :], T_lo[:, k, :], k == 0, k == DT - 1)
                last.then_inc(ff_done, 1)
            for half in range(2):
                hi, lo = weights(W2A + half)
                for t in range(NT):
                    if t == 0:
                        pe.wait_ge(ff_lo_made, DT * (half + 1))
                    for k in range(DT):
                        f = half * DT + k
                        last = mm3(ps[:, 4 + t, :], ff_hi[:, f, col(t)], ff_lo[:, f, col(t)], hi[:, k, :],
                                   lo[:, k, :], f == 0, f == FT - 1)
                    last.then_inc(w2_done if half else w2_half_done, 1)
            count_transposes(ct_lo, 0, c_lo_tr)

            pe.wait_ge(c_lo_made, NT)
            transposes(T3, 0, ln_ready(LN3))
            pe.wait_ge(tr_lo, tr_no(T3, NT - 1))
            for u, bank, done in ((WN, 4, beta_done), (WC, 0, alpha_done)):
                hi, lo = weights(u)
                for t in range(NT):
                    for k in range(DT):
                        last = mm3(ps[:, bank + t, :], T_hi[:, k, col(t)], T_lo[:, k, col(t)], hi[:, k, :],
                                   lo[:, k, :], k == 0, k == DT - 1)
                    last.then_inc(done, 1)
            pe.wait_ge(beta_lo_made, NT)
            for t in range(NT):
                for k in range(NT):
                    last = mm3(ps[:, 4 + t, :], ct_hi[:, k, col(t)], ct_lo[:, k, col(t)], R_hi[:, k, :],
                               R_lo[:, k, :], k == 0, k == NT - 1)
                last.then_inc(gamma_done, 1)
            pe.wait_ge(alpha_added, NT)
            pe.wait_ge(ones_made, 1)
            for k in range(NT):
                nc.tensor.matmul(ps[:, 0, :], ones[:], c_hi[:, k, :], start=k == 0, stop=False)
                last = nc.tensor.matmul(ps[:, 0, :], ones[:], c_lo[:, k, :], start=False, stop=k == NT - 1)
            last.then_inc(deg_done, 1)

            def t4_ready(t):
                pe.wait_ge(x2_made, t + 1)
                pe.wait_ge(ln_out, ln_no(LN4, t))

            transposes(T4, 4, t4_ready)
            pe.wait_ge(tr_lo, tr_no(T4, NT - 1))
            pe.wait_ge(gate_split, 1)
            for t in range(NT):
                for k in range(DT):
                    last = mm3(ps[:, 4, t * EXPERTS:(t + 1) * EXPERTS], T_hi[:, k, col(t)], T_lo[:, k, col(t)],
                               gw_hi[:, k, :], gw_lo[:, k, :], k == 0, k == DT - 1)
            last.then_inc(logits_done, 1)
            pe.wait_ge(hr_lo_made, NT)
            pe.wait_ge(deg_made, 1)
            for j in range(DT):
                for k in range(NT):
                    last = mm3(ps[:, j, :], R_hi[:, k, col(j)], R_lo[:, k, col(j)], c_hi[:, k, :], c_lo[:, k, :],
                               k == 0, k == NT - 1)
                last.then_inc(agg_done, 1)

            for e in range(EXPERTS):
                for n, (a_hi, a_lo) in enumerate(((T_hi, T_lo), (agg_hi, agg_lo))):
                    hi, lo = weights(FIRST_EXPERT + 4 * e + n)
                    if n == 0:
                        if e == 0:
                            pe.wait_ge(logits_out, 1)
                        else:
                            pe.wait_ge(own_made, NT * e)
                    elif e == 0:
                        pe.wait_ge(agg_lo_made, DT)
                    for j in range(DT):
                        for k in range(DT):
                            last = mm3(ps[:, 4 + j, :], hi[:, k, col(j)], lo[:, k, col(j)], a_hi[:, k, :],
                                       a_lo[:, k, :], n == 0 and k == 0, n == 1 and k == DT - 1)
                        last.then_inc(hid_done if n else hid_half_done, 1)
                for n, (bank, done) in enumerate(((0, z_done), (4, own_done))):
                    hi, lo = weights(FIRST_EXPERT + 4 * e + 2 + n)
                    if n == 0:
                        if e == 0:
                            pe.wait_ge(agg_sum, DT)
                        else:
                            pe.wait_ge(expert_sum, NT * e)
                        for k in range(DT):
                            pe.wait_ge(hid_lo_made, DT * e + k + 1)
                            for t in range(NT):
                                last = mm3(ps[:, bank + t, :], hid_hi[:, k, col(t)], hid_lo[:, k, col(t)],
                                           hi[:, k, :], lo[:, k, :], k == 0, k == DT - 1)
                                if k == DT - 1:
                                    last.then_inc(done, 1)
                    else:
                        for t in range(NT):
                            for k in range(DT):
                                last = mm3(ps[:, bank + t, :], hid_hi[:, k, col(t)], hid_lo[:, k, col(t)],
                                           hi[:, k, :], lo[:, k, :], k == 0, k == DT - 1)
                            last.then_inc(done, 1)
                pe.wait_ge(z_lo_made, NT * (e + 1))
                for t in range(NT):
                    for k in range(NT):
                        last = mm3(ps[:, t, :], c_hi[:, k, col(t)], c_lo[:, k, col(t)], z_hi[:, k, :],
                                   z_lo[:, k, :], k == 0, k == NT - 1)
                    last.then_inc(near_done, 1)

            pe.wait_ge(own_made, NT * EXPERTS)
            transposes(T5, 4, ln_ready(LN5))
            pe.wait_ge(tr_lo, tr_no(T5, NT - 1))
            pe.wait_ge(expert_sum, NT * EXPERTS)
            hi, lo = weights(W_LAST)
            for t in range(NT):
                for k in range(DT):
                    last = mm3(ps[:, t, :], T_hi[:, k, col(t)], T_lo[:, k, col(t)], hi[:, k, :], lo[:, k, :],
                               k == 0, k == DT - 1)
                last.then_inc(H_done, 1)
            pe.wait_ge(H_lo_made, NT)
            for t in range(NT):
                for k in range(NT):
                    last = mm3(ps[:, 4 + t, :], c_hi[:, k, col(t)], c_lo[:, k, col(t)], R_hi[:, k, :], R_lo[:, k, :],
                               k == 0, k == NT - 1)
                last.then_inc(last_done, 1)


_INS = ["x", "src", "dst",
        *(f"L0_gnn_{n}" for n in ("Wq", "bq", "Wk", "bk", "Wv", "bv", "Wo", "bo", "W1", "b1", "W2", "b2", "g1",
                                  "be1", "g2", "be2")),
        "L1_gnn_wc", "L1_gnn_wn", "L1_gnn_bias",
        *(f"L2_gnn_{n}" for n in ("gate_W", "gate_b", "Wl", "bl", "Wr")), "L3_gnn_W", "L3_gnn_b"]


def kernel(**inputs):
    import concourse.bacc as bacc
    from concourse.bass_utils import run_bass_kernel_spmd

    nc = bacc.Bacc("TRN2", target_bir_lowering=False, num_devices=1)
    arrays, d = {}, {}
    for name in _INS:
        a = np.ascontiguousarray(inputs[name])
        arrays[f"in_{name}"] = a
        d[name] = nc.dram_tensor(f"in_{name}", a.shape, mybir.dt.from_np(a.dtype), kind="ExternalInput").ap()
    out = nc.dram_tensor("out", arrays["in_x"].shape, F32, kind="ExternalOutput").ap()
    build(nc, d, out)
    r = run_bass_kernel_spmd(nc, [arrays], core_ids=[0])
    return r.results[0]["out"]
```

```python
from contextlib import ExitStack

import numpy as np

import concourse.bass as bass
from concourse import mybir
from concourse.alu_op_type import AluOpType as ALU

ACT = mybir.ActivationFunctionType
F32 = mybir.dt.float32
F32R = mybir.dt.float32r
F16 = mybir.dt.float16
BF16 = mybir.dt.bfloat16
I32 = mybir.dt.int32
AX_X = mybir.AxisListType.X

P = 128
EPS = 1e-5
TOP_K = 2


def build(nc, d, out):
    N, D = d["x"].shape
    E = d["src"].shape[0]
    NT = N // P
    DT = D // P
    FT = 2 * D // P
    CH = E // P
    HEADS = 8
    HD = D // HEADS
    PAIRS = HEADS // 2
    EXPERTS = d["L2_gnn_gate_W"].shape[1]
    SCALE = float(HD) ** -0.5
    HN = N // 2
    STEPS = 2 * NT
    HALF = N // 2
    DIGIT = 6
    UN = 4
    RING = 32
    SEGMENTS = CH // RING
    W_SCALE = 2.0 ** 9
    assert N == D == 512 and NT == DT == 4 and HD == 64 and CH % RING == 0 and RING % UN == 0

    at = [-(-nc.sbuf_base // 32) * 32]

    def region(size):
        start = at[0]
        at[0] += size
        return start

    def place(name, shape, dt, offset):
        return nc.alloc_sbuf_tensor_at(name, shape, dt, offset=offset)

    MAT = NT * D * 4
    rW, rX, rH, rT, rCT, rQK, rVZ, rEP, rM = (region(k * MAT) for k in (6, 1, 1, 2, 2, 4, 4, 3, 1))
    rB, rBL, rS = region(4 * D * 4), region(2 * D * 4), region(2048 + 1280)

    stage = [place(f"w_stage{i}", [P, 4, D], F32, rW + i * MAT) for i in range(2)]
    w_hi = [place(f"w_hi{i}", [P, 4, D], F32R, rW + (2 + i) * MAT) for i in range(2)]
    w_lo = [place(f"w_lo{i}", [P, 4, D], F32R, rW + (4 + i) * MAT) for i in range(2)]
    x_sb = place("x_sb", [P, NT, D], F32, rX)
    h_sb = place("h_sb", [P, NT, D], F32, rH)
    T_hi = place("T_hi", [P, DT, N], F32R, rT)
    T_lo = place("T_lo", [P, DT, N], F32R, rT + MAT)
    ct_hi = place("ct_hi", [P, NT, N], F32R, rCT)
    ct_lo = place("ct_lo", [P, NT, N], F32R, rCT + MAT)
    q_hi = place("q_hi", [P, PAIRS, N], F32R, rQK)
    q_lo = place("q_lo", [P, PAIRS, N], F32R, rQK + MAT)
    k_hi = place("k_hi", [P, PAIRS, N], F32R, rQK + 2 * MAT)
    k_lo = place("k_lo", [P, PAIRS, N], F32R, rQK + 3 * MAT)
    ff_hi = place("ff_hi", [P, FT, N], F32R, rQK)
    ff_lo = place("ff_lo", [P, FT, N], F32R, rQK + 2 * MAT)
    R_hi = place("R_hi", [P, NT, D], F32R, rQK)
    R_lo = place("R_lo", [P, NT, D], F32R, rQK + MAT)
    agg_hi = place("agg_hi", [P, DT, N], F32R, rQK + 2 * MAT)
    agg_lo = place("agg_lo", [P, DT, N], F32R, rQK + 3 * MAT)
    vz_hi = place("vz_hi", [P, NT, HEADS, P], F32R, rVZ)
    vz_lo = place("vz_lo", [P, NT, HEADS, P], F32R, rVZ + 2 * MAT)
    c_hi = place("c_hi", [P, NT, N], F32R, rVZ)
    c_lo = place("c_lo", [P, NT, N], F32R, rVZ + MAT)
    hid_hi = place("hid_hi", [P, DT, N], F32R, rVZ + 2 * MAT)
    hid_lo = place("hid_lo", [P, DT, N], F32R, rVZ + 3 * MAT)
    tmp = place("tmp", [P, NT, D], F32, rEP)
    p_hi = place("p_hi", [P, HEADS, HN], F32R, rEP + MAT)
    p_lo = place("p_lo", [P, HEADS, HN], F32R, rEP + 2 * MAT)
    z_hi = place("z_hi", [P, NT, D], F32R, rEP + MAT)
    z_lo = place("z_lo", [P, NT, D], F32R, rEP + 2 * MAT)
    maskc = place("maskc", [P, NT, N], F32R, rM)
    part = place("part", [P, NT, D], F32, rM)
    e_two = [place("e_sb0", [P, HEADS, HN], F32, rX), place("e_sb1", [P, HEADS, HN], F32, rEP)]
    one_dst = place("one_dst", [P, RING, HALF], F16, rVZ)
    one_src = place("one_src", [P, RING, HALF], F16, rVZ + RING * HALF * 2)
    all_dst = place("all_dst", [P, UN, N], F16, rEP)
    all_src = place("all_src", [P, UN, N], F16, rEP + UN * N * 2)
    edge_i = place("edge_i", [P, 2, CH], I32, rEP + MAT)
    edge_f = place("edge_f", [P, 2, CH], F32, rEP + MAT + 1024)
    upper = place("upper", [P, 2, CH], F32, rEP + MAT + 2048)
    edge_m = place("edge_m", [P, 2, CH], F32, rEP + MAT + 3072)
    edge_w = place("edge_w", [P, CH], F32, rEP + MAT + 4096)
    iota_n = place("iota_n", [P, N], F16, rEP + MAT + 4608)
    packed = place("packed", [P, 2, HALF], I32, rEP + MAT + 5632)
    checked = place("checked", [P, 2], F32, rEP + MAT + 7680)
    slow_flag = place("slow_flag", [P, 1], I32, rEP + MAT + 7712)
    zeros = place("zeros", [P, N], F16, rEP)
    digits = place("digits", [P, NT, N], I32, rEP + 2 * MAT)
    row = [place(f"row{i}", [P, D], F32, rB + i * D * 4) for i in range(4)]
    row_bl = [place(f"row_bl{i}", [P, D], F32, rBL + i * D * 4) for i in range(2)]
    inv_in_row = place("inv_in_row", [P, N], F32, rS)
    rsum = place("rsum", [P, HN], F32, rS)
    rmask = place("rmask", [P, HN], F32, rS + HN * 4)
    small = [rS + 2048]

    def little(name, shape, dt=F32):
        start = small[0]
        size = int(np.prod(shape[1:])) * (2 if dt == BF16 else 4)
        small[0] += -(-size // 32) * 32
        return place(name, shape, dt, start)

    qk_bias = little("qk_bias", [P, 2, DT])
    bq, bk = qk_bias[:, 0, :], qk_bias[:, 1, :]
    b1 = little("b1", [P, FT])
    bl0 = little("bl0", [P, EXPERTS, DT])
    gate_b = little("gate_b", [P, EXPERTS])
    gate_w = little("gate_w", [P, DT, EXPERTS])
    gw_hi = little("gw_hi", [P, DT, EXPERTS], F32R)
    gw_lo = little("gw_lo", [P, DT, EXPERTS], F32R)
    scalars = little("scalars", [P, 2])
    one_col, half_neg = scalars[:, 0:1], scalars[:, 1:2]
    stats = little("stats", [P, 6])
    moments = little("moments", [P, 6 * NT, 2])
    vareps = little("vareps", [P, 6 * NT])
    rstd = little("rstd", [P, 6 * NT])
    shift = little("shift", [P, 6 * NT])
    in_deg = little("in_deg", [P, NT])
    inv_in = little("inv_in", [P, NT])
    isd = little("isd", [P, NT])
    out_deg = little("out_deg", [P, NT])
    inv_out = little("inv_out", [P, NT])
    no_edge_nan = little("no_edge_nan", [P, NT])
    G1 = [P, NT, EXPERTS]
    logit = little("logit", G1)
    gmax = little("gmax", [P, NT])
    gate = little("gate", G1)
    gsum = little("gsum", [P, NT])
    rank = little("rank", G1)
    beats = little("beats", [P, NT])
    sbuf_end = small[0]
    at[0] = -(-sbuf_end // 32) * 32
    ident = place("ident", [P, P], F32, region(P * 4))
    m_bf = place("m_bf", [P, HN], BF16, rBL)
    neg_ident = place("neg_ident", [P, P], BF16, rBL + HN * 2)
    ones = place("ones", [P, P], F32, rM)
    assert at[0] <= nc.sbuf_usable_end, (at[0], nc.sbuf_usable_end)

    def matrix(a, rows=slice(0, D), cols=slice(0, D)):
        return a[rows, cols].rearrange("(t p) n -> p t n", p=P)

    w1, w2 = d["L0_gnn_W1"], d["L0_gnn_W2"]
    units = [matrix(d[f"L0_gnn_{n}"]) for n in ("Wq", "Wk", "Wv", "Wo")]
    units += [matrix(w1, cols=slice(j * D, (j + 1) * D)) for j in range(2)]
    units += [matrix(w2, rows=slice(j * D, (j + 1) * D)) for j in range(2)]
    units += [matrix(d["L1_gnn_wn"]), matrix(d["L1_gnn_wc"])]
    FIRST_EXPERT = len(units)
    for e in range(EXPERTS):
        wl, wr = d["L2_gnn_Wl"], d["L2_gnn_Wr"]
        units += [matrix(a[e, layer]) for a, layer in ((wr, 0), (wl, 0), (wl, 1), (wr, 1))]
    units.append(matrix(d["L3_gnn_W"]))
    (WQ, WK, WV, WO, W1A, W1B, W2A, W2B, WN, WC) = range(FIRST_EXPERT)
    W_LAST = len(units) - 1

    rows_in = [("L0_gnn_bv", 0), ("L0_gnn_bo", 1), ("L0_gnn_g1", 2), ("L0_gnn_be1", 3),
               ("L0_gnn_b2", 0), ("L0_gnn_g2", 1), ("L0_gnn_be2", 2), ("L1_gnn_bias", 3),
               ("L3_gnn_b", 0)]
    BV, BO, GAMMA1, BETA1, B2, GAMMA2, BETA2, BIAS1, B3 = range(len(rows_in))

    LN0, LN1, LN2, LN3, LN4, LN5 = range(6)
    ln_order = [(LN0, t) for t in range(NT)] + [(LN1, t) for t in range(NT)]
    ln_order += [(LN2, 0)] + [x for t in range(1, NT) for x in ((LN2, t), (LN3, t - 1))] + [(LN3, NT - 1)]
    ln_order += [(k, t) for k in (LN4, LN5) for t in range(NT)]

    def ln_no(k, t):
        return ln_order.index((k, t)) + 1

    out_order = [(k, t) for k in (LN0, LN3, LN4, LN5) for t in range(NT)]

    def ln_out_no(k, t):
        return out_order.index((k, t)) + 1

    T0, T1, T3, T4, T5 = range(5)

    def tr_no(k, t):
        return NT * k + t + 1

    ctx = ExitStack()
    with ctx:
        ps = ctx.enter_context(nc.psum_tensor("ps", [P, 8, 512], F32))

        def sem(name):
            return ctx.enter_context(nc.semaphore(name))

        x_in = [sem(f"x_in{t}") for t in range(NT)]
        edges_in = sem("edges_in")
        cols_in = sem("cols_in")
        row_in = [sem(f"row_in{i}") for i in range(4)]
        bl_in = [sem(f"bl_in{i}") for i in range(2)]
        stage_in = [sem(f"stage_in{i}") for i in range(2)]
        hi_made = sem("hi_made")
        lo_made = sem("lo_made")
        consts = sem("consts")
        neg_made = sem("neg_made")
        onehot = sem("onehot")
        onehot_used = sem("onehot_used")
        digits_made = sem("digits_made")
        ct_hi_made = sem("ct_hi_made")
        total_ask = sem("total_ask")
        total_done = sem("total_done")
        flag_made = sem("flag_made")
        all_onehot = sem("all_onehot")
        all_used = sem("all_used")
        all_copied = sem("all_copied")
        ct_ready = sem("ct_ready")
        x_back = sem("x_back")
        dve = sem("dve")
        pool = sem("pool")
        ln_var = sem("ln_var")
        ln_rstd = sem("ln_rstd")
        ln_scale = sem("ln_scale")
        ln_out = sem("ln_out")
        h_ready = sem("h_ready")
        tr_done = sem("tr_done")
        tr_hi = sem("tr_hi")
        tr_lo = sem("tr_lo")
        q_done, q_hi_made, q_lo_made = sem("q_done"), sem("q_hi_made"), sem("q_lo_made")
        k_done, k_hi_made, k_lo_made = sem("k_done"), sem("k_hi_made"), sem("k_lo_made")
        v_done, v_sum, v_hi_made, v_lo_made = sem("v_done"), sem("v_sum"), sem("v_hi_made"), sem("v_lo_made")
        vz_zero = sem("vz_zero")
        ones_made = sem("ones_made")
        zero_made = sem("zero_made")
        diag_made = sem("diag_made")
        score_done, max_done, centred = sem("score_done"), sem("max_done"), sem("centred")
        exp_done, prob_done, p_hi_made, p_lo_made = sem("exp_done"), sem("prob_done"), sem("p_hi_made"), sem("p_lo_made")
        pv_done = sem("pv_done")
        att_hi_made, att_lo_made = sem("att_hi_made"), sem("att_lo_made")
        bo_added, b2_added, be2_added, bias1_added = sem("bo_added"), sem("b2_added"), sem("be2_added"), sem("bias1_added")
        wo_done = sem("wo_done")
        c_tr, c_hi_made, c_lo_tr, c_lo_made = sem("c_tr"), sem("c_hi_made"), sem("c_lo_tr"), sem("c_lo_made")
        ff_done, ff_hi_made, ff_lo_made = sem("ff_done"), sem("ff_hi_made"), sem("ff_lo_made")
        w2_half_done, w2_done = sem("w2_half_done"), sem("w2_done")
        y2_read = sem("y2_read")
        beta_done, beta_hi_made, beta_lo_made = sem("beta_done"), sem("beta_hi_made"), sem("beta_lo_made")
        alpha_done, alpha_added = sem("alpha_done"), sem("alpha_added")
        gamma_done, x2_made = sem("gamma_done"), sem("x2_made")
        deg_done, deg_made = sem("deg_done"), sem("deg_made")
        pow_ask, pow_made = sem("pow_ask"), sem("pow_made")
        hr_hi_made, hr_lo_made = sem("hr_hi_made"), sem("hr_lo_made")
        gate_split, logits_done, logits_out = sem("gate_split"), sem("logits_done"), sem("logits_out")
        gexp_ask, gexp_done = sem("gexp_ask"), sem("gexp_done")
        agg_done, agg_sum, agg_hi_made, agg_lo_made = sem("agg_done"), sem("agg_sum"), sem("agg_hi_made"), sem("agg_lo_made")
        hid_half_done = sem("hid_half_done")
        hid_done, hid_hi_made, hid_lo_made = sem("hid_done"), sem("hid_hi_made"), sem("hid_lo_made")
        z_done, z_hi_made, z_lo_made = sem("z_done"), sem("z_hi_made"), sem("z_lo_made")
        own_done, own_made = sem("own_done"), sem("own_made")
        near_done, expert_sum, expert_out = sem("near_done"), sem("expert_sum"), sem("expert_out")
        x3_made = sem("x3_made")
        H_done, H_made, H_hi_made, H_lo_made = sem("H_done"), sem("H_made"), sem("H_hi_made"), sem("H_lo_made")
        last_done, last_sum, last_relu, x4_made = sem("last_done"), sem("last_sum"), sem("last_relu"), sem("x4_made")
        stored = sem("stored")

        block = ctx.enter_context(nc.Block())

        w_spent = [(q_done, DT), (k_done, DT), (v_done, NT), (wo_done, NT), (ff_done, DT), (ff_done, FT),
                   (w2_half_done, NT), (w2_done, NT), (beta_done, NT), (alpha_done, NT)]
        for e in range(EXPERTS):
            w_spent += [(done, 4 * (e + 1)) for done in (hid_half_done, hid_done, z_done, own_done)]

        def k_bank(j):
            return (4, 5, 6, 0)[j]

        def f32(t):
            return t.bitcast(F32)

        def score_of(h):
            return ps[:, 4 + h % 4, (h // 4) * HN:(h // 4 + 1) * HN]

        def scores_view():
            return ps[:, 4:8, :].rearrange("p b (g n) -> p g b n", g=2)

        @block.sync
        def _(sp):
            for t in range(NT):
                sp.dma_start(x_sb[:, t, :], d["x"][t * P:(t + 1) * P, :]).then_inc(x_in[t], 16)
            sp.dma_start(edge_i[:, 0, :], d["src"].rearrange("(p c) -> p c", p=P)).then_inc(edges_in, 16)
            sp.dma_start(edge_i[:, 1, :], d["dst"].rearrange("(p c) -> p c", p=P)).then_inc(edges_in, 16)

            row_free = {B2: (v_sum, NT), GAMMA2: (bo_added, NT), BETA2: (h_ready, NT), BIAS1: (h_ready, NT),
                        B3: (b2_added, NT)}

            def load_row(i):
                name, slot = rows_in[i]
                if i in row_free:
                    sp.wait_ge(*row_free[i])
                sp.dma_start(row[slot][:], d[name].unsqueeze(0).to_broadcast([P, D])).then_inc(row_in[slot], 16)

            def load_bl(e):
                if e >= 2:
                    sp.wait_ge(own_made, NT * (e - 1))
                sp.dma_start(row_bl[e % 2][:], d["L2_gnn_bl"][e, 1].unsqueeze(0).to_broadcast([P, D]))\
                  .then_inc(bl_in[e % 2], 16)

            ahead = {WQ: [BV], WK: [BO, GAMMA1], WV: [BETA1], W1B: [B2, GAMMA2], W2A: [BETA2, BIAS1],
                     FIRST_EXPERT + 1: [B3]}
            for u, src in enumerate(units):
                if u >= 2:
                    sp.wait_ge(lo_made, u - 1)
                sp.dma_start(stage[u % 2][:], src).then_inc(stage_in[u % 2], 16)
                for i in ahead.get(u, []):
                    load_row(i)
                if u in (WN, WC):
                    load_bl(u - WN)
                if u in (FIRST_EXPERT + 9, FIRST_EXPERT + 13):
                    load_bl((u - FIRST_EXPERT - 1) // 4)
                if u == W2A:
                    sp.wait_ge(p_lo_made, 2 * STEPS)
                    sp.dma_start(x_sb[:], d["x"].rearrange("(t p) n -> p t n", p=P)).then_inc(x_back, 16)
            for t in range(NT):
                sp.wait_ge(x4_made, t + 1)
                sp.dma_start(out[t * P:(t + 1) * P, :], x_sb[:, t, :]).then_inc(stored, 16)
            sp.wait_ge(stored, 16 * NT)

        @block.gpsimd
        def _(gp):
            gp.iota(iota_n[:], pattern=[[1, N]], base=0, channel_multiplier=0,
                    allow_small_or_imprecise_dtypes=True).then_inc(consts, 1)
            gp.memset(ident[:], 0.0).then_inc(pool, 1)
            gp.memset(half_neg, -0.5).then_inc(consts, 1)
            gp.memset(one_col, 1.0).then_inc(consts, 1)
            gp.memset(zeros[:], 0.0).then_inc(zero_made, 1)
            gp.wait_ge(pool, 1)
            gp.affine_select(out=ident[:], in_=ident[:], compare_op=ALU.not_equal, fill=1.0, base=0,
                             pattern=[[-1, P]], channel_multiplier=1).then_inc(consts, 1)
            gp.wait_ge(consts, 4)

            def split_lo(u):
                gp.wait_ge(hi_made, u + 1)
                if u >= 2:
                    gp.wait_ge(*w_spent[u - 2])
                s = u % 2
                gp.tensor_tensor(w_lo[s][:, 0:2], stage[s][:, 0:2], f32(w_hi[s][:, 0:2]), ALU.subtract)
                gp.tensor_tensor(w_lo[s][:, 2:4], stage[s][:, 2:4], f32(w_hi[s][:, 2:4]), ALU.subtract)\
                  .then_inc(lo_made, 1)

            def rstd_of(k):
                for t in range(NT):
                    power(ln_no(k, t))

            def power(n):
                gp.wait_ge(ln_var, n)
                gp.tensor_tensor(rstd[:, n - 1:n], vareps[:, n - 1:n], half_neg, ALU.pow).then_inc(ln_rstd, 1)

            def add_row(i, t, target, done):
                slot = rows_in[i][1]
                if t == 0:
                    gp.wait_ge(row_in[slot], 16 * (1 + sum(s == slot for _, s in rows_in[:i])))
                ins = gp.tensor_tensor(target[:, t, :], target[:, t, :], row[slot][:], ALU.add)
                ins.then_inc(done, 1)

            def split_p_lo(i):
                for g in range(2):
                    gp.wait_ge(p_hi_made, 2 * i + g + 1)
                    if i >= 1:
                        gp.wait_ge(pv_done, 2 * i + g - 1)
                    heads = slice(g * HEADS // 2, (g + 1) * HEADS // 2)
                    gp.tensor_tensor(p_lo[:, heads], e_two[i % 2][:, heads], f32(p_hi[:, heads]),
                                     ALU.subtract).then_inc(p_lo_made, 1)

            rstd_of(LN0)
            split_lo(WQ)
            split_lo(WK)
            gp.wait_ge(tr_done, tr_no(T0, NT - 1))
            for t in range(NT):
                add_row(BO, t, h_sb, bo_added)
            split_lo(WV)
            gp.wait_ge(ct_ready, 1)
            gp.memset(f32(vz_hi[:]), 0.0).then_inc(vz_zero, 1)
            gp.memset(f32(vz_lo[:]), 0.0).then_inc(vz_zero, 1)
            split_lo(WO)
            for i in range(STEPS):
                split_p_lo(i)
                if i == 1:
                    split_lo(W1A)
            rstd_of(LN1)
            for t in range(NT):
                gp.wait_ge(tr_done, tr_no(T1, t))
                add_row(B2, t, h_sb, b2_added)
            gp.memset(ones[:], 1.0).then_inc(ones_made, 1)
            split_lo(W1B)
            gp.wait_ge(x_back, 16)
            for t in range(NT):
                add_row(BETA2, t, x_sb, be2_added)
            split_lo(W2A)
            split_lo(W2B)
            split_lo(WN)
            for k, t in ln_order[2 * NT:4 * NT]:
                power(ln_no(k, t))
            split_lo(WC)
            for t in range(NT):
                gp.wait_ge(ln_out, ln_out_no(LN3, t))
                add_row(BIAS1, t, x_sb, bias1_added)
            gp.wait_ge(pow_ask, 1)
            gp.tensor_tensor(isd[:], isd[:], half_neg.to_broadcast([P, NT]), ALU.pow).then_inc(pow_made, 1)
            split_lo(FIRST_EXPERT)
            rstd_of(LN4)
            for u in range(FIRST_EXPERT + 1, W_LAST + 1):
                split_lo(u)
            rstd_of(LN5)

        @block.scalar
        def _(act):
            with nc.allow_non_contiguous_dma("small per-partition vectors"):
                for dst, src in ((bq, d["L0_gnn_bq"].rearrange("(j p) -> p j", p=P)),
                                 (bk, d["L0_gnn_bk"].rearrange("(j p) -> p j", p=P)),
                                 (b1[:], d["L0_gnn_b1"].rearrange("(j p) -> p j", p=P)),
                                 (gate_w[:], d["L2_gnn_gate_W"].rearrange("(t p) e -> p t e", p=P)),
                                 (gate_b[:], d["L2_gnn_gate_b"].unsqueeze(0).to_broadcast([P, EXPERTS]))):
                    act.dma_start(dst, src).then_inc(cols_in, 16)
                for e in range(EXPERTS):
                    act.dma_start(bl0[:, e, :], d["L2_gnn_bl"][e, 0].rearrange("(j p) -> p j", p=P))\
                       .then_inc(cols_in, 16)

            def split_hi(u):
                act.wait_ge(stage_in[u % 2], 16 * (u // 2 + 1))
                if u >= 2:
                    act.wait_ge(*w_spent[u - 2])
                nc.scalar.activation(w_hi[u % 2][:], stage[u % 2][:], ACT.Copy).then_inc(hi_made, 1)

            def normalise(k, t, dst, src, func):
                n = ln_no(k, t)
                act.wait_ge(ln_scale, ln_out_no(k, t))
                nc.scalar.activation(dst[:, t, :], src[:, t, :], func, scale=rstd[:, n - 1:n],
                                     bias=shift[:, n - 1:n]).then_inc(ln_out, 1)

            def transposed_hi(k, bank, only=None):
                for t in range(NT) if only is None else [only]:
                    act.wait_ge(tr_done, tr_no(k, t))
                    nc.scalar.activation(T_hi[:, :, t * P:(t + 1) * P],
                                         ps[:, bank + t, :].rearrange("p (k n) -> p k n", k=DT),
                                         ACT.Copy).then_inc(tr_hi, 1)

            for t in range(NT):
                normalise(LN0, t, h_sb, x_sb, ACT.Relu)
                if t < 2:
                    split_hi(WQ + t)
            transposed_hi(T0, 0)
            act.wait_ge(cols_in, 16 * (5 + EXPERTS))
            for j in range(PAIRS):
                act.wait_ge(q_done, j + 1)
                nc.scalar.activation(q_hi[:, j, :], ps[:, j, :], ACT.Identity, bias=bq[:, j:j + 1])\
                  .then_inc(q_hi_made, 1)
            split_hi(WV)
            for j in range(PAIRS):
                act.wait_ge(k_done, j + 1)
                nc.scalar.activation(k_hi[:, j, :], ps[:, k_bank(j), :], ACT.Identity, bias=bk[:, j:j + 1])\
                  .then_inc(k_hi_made, 1)
            split_hi(WO)
            act.wait_ge(digits_made, 1)
            nc.scalar.activation(ct_hi[:], digits[:], ACT.Copy).then_inc(ct_hi_made, 1)
            act.wait_ge(vz_zero, 2)
            for t in range(NT):
                act.wait_ge(v_sum, t + 1)
                v = tmp[:, t, :].rearrange("p (j two c) -> p j two c", j=PAIRS, two=2)
                for odd in range(2):
                    last = nc.scalar.activation(vz_hi[:, t, odd::2, odd * HD:(odd + 1) * HD], v[:, :, odd, :],
                                                ACT.Copy)
                last.then_inc(v_hi_made, 1)
            split_hi(W1A)

            def exponentials(i):
                act.wait_ge(centred, i + 1)
                if i == 1:
                    act.wait_ge(v_lo_made, NT)
                if i >= 2:
                    act.wait_ge(p_lo_made, 2 * (i - 1))
                nc.scalar.activation(e_two[i % 2][:].rearrange("p (g b) n -> p g b n", g=2), scores_view(), ACT.Exp,
                                     scale=SCALE).then_inc(exp_done, 1)

            def attended_hi(half):
                act.wait_ge(pv_done, 2 * NT * (half + 1))
                cols = slice(half * HN, (half + 1) * HN)
                for j in range(PAIRS):
                    nc.scalar.activation(T_hi[:, j, cols], ps[:, j, cols], ACT.Copy).then_inc(att_hi_made, 1)

            exponentials(0)
            for i in range(STEPS):
                if i + 1 < STEPS:
                    exponentials(i + 1)
                if i == NT:
                    attended_hi(0)
                for g in range(2):
                    act.wait_ge(prob_done, 2 * i + g + 1)
                    if i >= 1:
                        act.wait_ge(pv_done, 2 * i + g - 1)
                    heads = slice(g * HEADS // 2, (g + 1) * HEADS // 2)
                    nc.scalar.activation(p_hi[:, heads], e_two[i % 2][:, heads], ACT.Copy).then_inc(p_hi_made, 1)
            attended_hi(1)
            for t in range(NT):
                act.wait_ge(c_tr, t + 1)
                nc.scalar.activation(c_hi[:, t, :], ps[:, t, :], ACT.Copy).then_inc(c_hi_made, 1)
            split_hi(W1B)
            transposed_hi(T1, 4)
            for j in range(FT):
                if j == DT:
                    split_hi(W2A)
                act.wait_ge(ff_done, j + 1)
                nc.scalar.activation(ff_hi[:, j, :], ps[:, j, :], ACT.Relu, bias=b1[:, j:j + 1])\
                  .then_inc(ff_hi_made, 1)
            split_hi(W2B)
            split_hi(WN)
            for t in range(NT):
                normalise(LN3, t, h_sb, x_sb, ACT.Relu)
                if t >= 1:
                    transposed_hi(T3, 4, t - 1)
            split_hi(WC)
            transposed_hi(T3, 4, NT - 1)
            for t in range(NT):
                act.wait_ge(beta_done, t + 1)
                nc.scalar.activation(R_hi[:, t, :], ps[:, t, :], ACT.Copy).then_inc(beta_hi_made, 1)
            split_hi(FIRST_EXPERT)
            split_hi(FIRST_EXPERT + 1)
            act.wait_ge(gamma_done, NT)
            for t in range(NT):
                normalise(LN4, t, h_sb, x_sb, ACT.Relu)
                act.wait_ge(ln_out, ln_out_no(LN4, t))
                nc.scalar.activation(R_hi[:, t, :], h_sb[:, t, :], ACT.Copy).then_inc(hr_hi_made, 1)
                if t >= 1:
                    transposed_hi(T4, 0, t - 1)
            transposed_hi(T4, 0, NT - 1)
            for j in range(DT):
                act.wait_ge(agg_sum, j + 1)
                nc.scalar.activation(agg_hi[:, j, :], tmp[:, j, :], ACT.Copy).then_inc(agg_hi_made, 1)
            act.wait_ge(gexp_ask, 1)
            nc.scalar.activation(gate[:], logit[:], ACT.Exp).then_inc(gexp_done, 1)
            for e in range(EXPERTS):
                u = FIRST_EXPERT + 4 * e
                split_hi(u + 2)
                for j in range(DT):
                    act.wait_ge(hid_done, DT * e + j + 1)
                    nc.scalar.activation(hid_hi[:, j, :], ps[:, j, :], ACT.Relu, bias=bl0[:, e, j:j + 1])\
                      .then_inc(hid_hi_made, 1)
                split_hi(u + 3)
                for t in range(NT):
                    act.wait_ge(z_done, NT * e + t + 1)
                    nc.scalar.activation(z_hi[:, t, :], ps[:, 4 + t, :], ACT.Copy).then_inc(z_hi_made, 1)
                split_hi(u + 4)
                if e < EXPERTS - 1:
                    split_hi(u + 5)
                for t in range(NT):
                    act.wait_ge(expert_sum, NT * e + t + 1)
                    nc.scalar.activation(part[:, t, :], part[:, t, :], ACT.Relu, scale=gate[:, t, e:e + 1])\
                      .then_inc(expert_out, 1)
            for t in range(NT):
                normalise(LN5, t, h_sb, x_sb, ACT.Relu)
                if t >= 1:
                    transposed_hi(T5, 0, t - 1)
            transposed_hi(T5, 0, NT - 1)
            for t in range(NT):
                act.wait_ge(H_made, t + 1)
                nc.scalar.activation(R_hi[:, t, :], tmp[:, t, :], ACT.Copy).then_inc(H_hi_made, 1)
            for t in range(NT):
                act.wait_ge(last_sum, t + 1)
                nc.scalar.activation(tmp[:, t, :], tmp[:, t, :], ACT.Relu, scale=isd[:, t:t + 1])\
                  .then_inc(last_relu, 1)

        @block.vector
        def _(v):
            order = [0]

            def link(ins):
                order[0] += 1
                ins.then_inc(dve, 1)
                v.wait_ge(dve, order[0])

            def norm_stats(k, t, src):
                n = ln_no(k, t)
                link(nc.vector.bn_stats(stats[:], src[:, t, :]))
                link(nc.vector.bn_aggr(moments[:, n - 1, :], stats[:]))
                nc.vector.tensor_scalar(vareps[:, n - 1:n], moments[:, n - 1, 1:2], EPS, None, ALU.add)\
                  .then_inc(ln_var, 1)

            def norm_shift(k, t):
                n = ln_no(k, t)
                v.wait_ge(ln_rstd, n)
                nc.vector.scalar_tensor_tensor(shift[:, n - 1:n], moments[:, n - 1, 0:1], -1.0, rstd[:, n - 1:n],
                                               ALU.mult, ALU.mult).then_inc(ln_scale, 1)

            def norm_scaled(k, t, gain):
                n = ln_no(k, t)
                v.wait_ge(ln_rstd, n)
                link(nc.vector.tensor_scalar(h_sb[:, t, :], h_sb[:, t, :], moments[:, n - 1, 0:1], rstd[:, n - 1:n],
                                             ALU.subtract, ALU.mult))
                link(nc.vector.tensor_tensor(h_sb[:, t, :], h_sb[:, t, :], gain[:], ALU.mult))

            def wait_row(i):
                slot = rows_in[i][1]
                v.wait_ge(row_in[slot], 16 * (1 + sum(s == slot for _, s in rows_in[:i])))
                return row[slot]

            def transposed_lo(k, bank, t):
                v.wait_ge(tr_hi, tr_no(k, t))
                cols = slice(t * P, (t + 1) * P)
                nc.vector.tensor_tensor(T_lo[:, :, cols], ps[:, bank + t, :].rearrange("p (k n) -> p k n", k=DT),
                                        f32(T_hi[:, :, cols]), ALU.subtract).then_inc(tr_lo, 1)

            for t in range(NT):
                v.wait_ge(x_in[t], 16)
                norm_stats(LN0, t, x_sb)
                if t >= 1:
                    norm_shift(LN0, t - 1)
            norm_shift(LN0, NT - 1)

            v.wait_ge(edges_in, 32)
            link(nc.vector.tensor_copy(edge_f[:], edge_i[:]))
            link(nc.vector.tensor_scalar(upper[:], edge_f[:], float(HALF), None, ALU.is_ge))
            link(nc.vector.scalar_tensor_tensor(edge_m[:], upper[:], -float(HALF), edge_f[:], ALU.mult, ALU.add))
            link(nc.vector.tensor_scalar(upper[:, 0, :], upper[:, 0, :], 4.0 ** DIGIT - 1, 1.0, ALU.mult, ALU.add))
            link(nc.vector.tensor_scalar(upper[:, 1, :], upper[:, 1, :], (2.0 ** DIGIT - 1) / W_SCALE, 1 / W_SCALE,
                                         ALU.mult, ALU.add))
            link(nc.vector.tensor_tensor(edge_w[:], upper[:, 0, :], upper[:, 1, :], ALU.mult))
            v.wait_ge(consts, 4)
            nc.vector.tensor_scalar(neg_ident[:], ident[:], -1.0, None, ALU.mult).then_inc(neg_made, 1)

            def packed_one_hots(first, count):
                with v.Fori(0, count // UN) as g:
                    if first >= RING:
                        v.wait_ge(onehot_used, g + (first - RING) // UN + 1)
                    for s in range(UN):
                        c = g * UN + (first + s)
                        slot = g * UN + (first % RING + s)
                        nc.vector.tensor_scalar(one_dst[:, bass.ds(slot, 1), :].squeeze(1), iota_n[:, 0:HALF],
                                                edge_m[:, 1, bass.ds(c, 1)], None, ALU.is_equal)
                        last = nc.vector.tensor_scalar(one_src[:, bass.ds(slot, 1), :].squeeze(1), iota_n[:, 0:HALF],
                                                       edge_m[:, 0, bass.ds(c, 1)], edge_w[:, bass.ds(c, 1)],
                                                       ALU.is_equal, ALU.mult)
                    last.then_inc(onehot, 1)

            packed_one_hots(0, RING // 2)
            for t in range(NT):
                transposed_lo(T0, 0, t)
            packed_one_hots(RING // 2, RING // 2)
            packed_one_hots(RING, RING)
            v.wait_ge(cols_in, 16 * (5 + EXPERTS))
            for j in range(PAIRS):
                v.wait_ge(q_hi_made, j + 1)
                nc.vector.scalar_tensor_tensor(q_lo[:, j, :], ps[:, j, :], bq[:, j:j + 1], f32(q_hi[:, j, :]),
                                               ALU.add, ALU.subtract).then_inc(q_lo_made, 1)
            packed_one_hots(2 * RING, RING)
            for j in range(PAIRS):
                v.wait_ge(k_hi_made, j + 1)
                nc.vector.scalar_tensor_tensor(k_lo[:, j, :], ps[:, k_bank(j), :], bk[:, j:j + 1],
                                               f32(k_hi[:, j, :]), ALU.add, ALU.subtract).then_inc(k_lo_made, 1)
            packed_one_hots(3 * RING, RING)

            v.wait_ge(onehot_used, CH // UN)
            link(nc.vector.tensor_scalar(packed[:], ps[:, 7, :].rearrange("p (m n) -> p m n", m=2), W_SCALE, 2.0 ** 24,
                                         ALU.mult, ALU.min))
            for src_up in range(2):
                for dst_up in range(2):
                    shift_by = DIGIT * (dst_up + 2 * src_up)
                    last = nc.vector.tensor_scalar(
                        digits[:, 2 * dst_up:2 * dst_up + 2, src_up * HALF:(src_up + 1) * HALF], packed[:], shift_by,
                        2 ** DIGIT - 1 if shift_by < 3 * DIGIT else 2 ** 24 - 1, ALU.logical_shift_right,
                        ALU.bitwise_and)
            last.then_inc(digits_made, 1)
            v.wait_ge(digits_made, 1)
            link(nc.vector.tensor_reduce(in_deg[:], digits[:], AX_X, ALU.add))
            link(nc.vector.tensor_reduce(checked[:, 0:1], in_deg[:], AX_X, ALU.add))
            link(nc.vector.tensor_reduce(checked[:, 1:2], ps[:, 7, :], AX_X, ALU.max))
            link(nc.vector.tensor_scalar(checked[:, 1:2], checked[:, 1:2], 2.0 ** 24 / W_SCALE, -(2.0 ** 24), ALU.is_ge,
                                         ALU.mult))
            nc.vector.tensor_tensor(checked[:, 0:1], checked[:, 0:1], checked[:, 1:2], ALU.add).then_inc(total_ask, 1)
            nc.vector.tensor_scalar(maskc[:], digits[:], 0.0, 1.0 / HEADS, ALU.is_equal, ALU.mult)
            v.wait_ge(total_done, 1)
            nc.vector.tensor_scalar(slow_flag[0:1, :], ps[0:1, 7, 0:1], float(E), None, ALU.not_equal)\
              .then_inc(flag_made, 1)
            v.wait_ge(flag_made, 1)
            slow = v.value_load(slow_flag[0:1, 0:1], min_val=0, max_val=1)
            v.wait_ge(ct_hi_made, 1)
            with v.If(slow > 0):
                def whole_one_hots(s, c):
                    nc.vector.tensor_scalar(all_dst[:, s, :], iota_n[:], edge_f[:, 1, bass.ds(c, 1)], None,
                                            ALU.is_equal)
                    nc.vector.tensor_scalar(all_src[:, s, :], iota_n[:], edge_f[:, 0, bass.ds(c, 1)], None,
                                            ALU.is_equal).then_inc(all_onehot, 1)

                for s in range(UN):
                    whole_one_hots(s, s)
                with v.Fori(1, CH // UN) as g:
                    for s in range(UN):
                        v.wait_ge(all_used, g * UN + (s + 1 - UN))
                        whole_one_hots(s, g * UN + s)
                v.wait_ge(all_used, CH)
                nc.vector.tensor_copy(ct_hi[:], ps[:, 4:8, :]).then_inc(all_copied, 1)
                v.wait_ge(all_copied, 1)
                nc.vector.tensor_tensor(ct_lo[:], ps[:, 4:8, :], f32(ct_hi[:]), ALU.subtract)
                nc.vector.tensor_reduce(in_deg[:], ps[:, 4:8, :], AX_X, ALU.add)
                nc.vector.tensor_scalar(maskc[:], ps[:, 4:8, :], 0.0, 1.0 / HEADS, ALU.is_equal, ALU.mult)\
                  .then_inc(all_copied, 1)
                v.wait_ge(all_copied, 2)
            link(nc.vector.tensor_scalar(inv_in[:], in_deg[:], 1.0, None, ALU.max))
            nc.vector.reciprocal(inv_in[:], inv_in[:]).then_inc(ct_ready, 1)

            bv_row = wait_row(BV)
            for t in range(NT):
                v.wait_ge(v_done, t + 1)
                nc.vector.tensor_tensor(tmp[:, t, :], ps[:, t, :], bv_row[:], ALU.add).then_inc(v_sum, 1)

            def maxima(i):
                v.wait_ge(score_done, i + 1)
                if i >= 1:
                    v.wait_ge(centred, i)
                nc.vector.tensor_reduce(m_bf[:], ps[:, 4:8, :].rearrange("p b (g n) -> p n g b", g=2),
                                        mybir.AxisListType.XY, ALU.max).then_inc(max_done, 1)

            def attended_lo(half):
                cols = slice(half * HN, (half + 1) * HN)
                for j in range(PAIRS):
                    v.wait_ge(att_hi_made, PAIRS * half + j + 1)
                    nc.vector.tensor_tensor(T_lo[:, j, cols], ps[:, j, cols], f32(T_hi[:, j, cols]),
                                            ALU.subtract).then_inc(att_lo_made, 1)

            maxima(0)
            for t in range(NT):
                v.wait_ge(v_hi_made, t + 1)
                if t == 0:
                    v.wait_ge(v_sum, NT)
                vals = tmp[:, t, :].rearrange("p (j two c) -> p j two c", j=PAIRS, two=2)
                for odd in range(2):
                    cols = slice(odd * HD, (odd + 1) * HD)
                    last = nc.vector.tensor_tensor(vz_lo[:, t, odd::2, cols], vals[:, :, odd, :],
                                                   f32(vz_hi[:, t, odd::2, cols]), ALU.subtract)
                last.then_inc(v_lo_made, 1)
            for i in range(STEPS):
                mt, half = i % NT, i // NT
                e = e_two[i % 2]
                v.wait_ge(exp_done, i + 1)
                link(nc.vector.tensor_reduce(rsum[:], e[:].rearrange("p h n -> p n h"), AX_X, ALU.add))
                if i + 1 < STEPS:
                    maxima(i + 1)
                if i == NT:
                    attended_lo(0)
                link(nc.vector.reciprocal(rsum[:], rsum[:]))
                link(nc.vector.scalar_tensor_tensor(rmask[:], f32(ct_hi[:, mt, half * HN:(half + 1) * HN]), 0.0,
                                                    rsum[:], ALU.is_gt, ALU.mult))
                for g in range(2):
                    heads = slice(g * HEADS // 2, (g + 1) * HEADS // 2)
                    nc.vector.tensor_tensor(e[:, heads], e[:, heads],
                                            rmask[:].unsqueeze(1).to_broadcast([P, HEADS // 2, HN]),
                                            ALU.mult).then_inc(prob_done, 1)
            attended_lo(1)

            g1_row, be1_row = wait_row(GAMMA1), wait_row(BETA1)

            def h1_finish(t):
                norm_scaled(LN1, t, g1_row)
                nc.vector.tensor_tensor(h_sb[:, t, :], h_sb[:, t, :], be1_row[:], ALU.add).then_inc(h_ready, 1)

            for t in range(NT):
                v.wait_ge(wo_done, t + 1)
                v.wait_ge(bo_added, t + 1)
                link(nc.vector.tensor_tensor(h_sb[:, t, :], ps[:, 4 + t, :], h_sb[:, t, :], ALU.add))
                norm_stats(LN1, t, h_sb)
                if t >= 1:
                    h1_finish(t - 1)
            h1_finish(NT - 1)
            for t in range(NT):
                transposed_lo(T1, 4, t)

            v.wait_ge(c_hi_made, NT)
            link(nc.vector.tensor_reduce(out_deg[:], f32(c_hi[:]), AX_X, ALU.add))
            for j in range(DT):
                v.wait_ge(ff_hi_made, j + 1)
                link(nc.vector.tensor_scalar(tmp[:, j, :], ps[:, j, :], b1[:, j:j + 1], 0.0, ALU.add, ALU.max))
                nc.vector.tensor_tensor(ff_lo[:, j, :], tmp[:, j, :], f32(ff_hi[:, j, :]),
                                        ALU.subtract).then_inc(ff_lo_made, 1)
            v.wait_ge(ff_lo_made, DT)
            for j in range(DT, FT):
                v.wait_ge(ff_hi_made, j + 1)
                link(nc.vector.tensor_scalar(tmp[:, j - DT, :], ps[:, j, :], b1[:, j:j + 1], 0.0, ALU.add, ALU.max))
                nc.vector.tensor_tensor(ff_lo[:, j, :], tmp[:, j - DT, :], f32(ff_hi[:, j, :]),
                                        ALU.subtract).then_inc(ff_lo_made, 1)
            with v.If(slow > 0):
                v.wait_ge(c_lo_tr, NT)
                nc.vector.tensor_copy(c_lo[:], ps[:, 4:8, :]).then_inc(c_lo_made, 1)
                v.wait_ge(c_lo_made, 1)
                nc.vector.tensor_reduce(inv_out[:], f32(c_lo[:]), AX_X, ALU.add).then_inc(c_lo_made, 1)
                v.wait_ge(c_lo_made, 2)
                nc.vector.tensor_tensor(out_deg[:], out_deg[:], inv_out[:], ALU.add).then_inc(c_lo_made, 1)
                v.wait_ge(c_lo_made, 3)
            link(nc.vector.reciprocal(no_edge_nan[:], out_deg[:]))
            link(nc.vector.tensor_scalar(no_edge_nan[:], no_edge_nan[:], 0.0, None, ALU.mult))
            link(nc.vector.tensor_scalar(out_deg[:], out_deg[:], 1.0, None, ALU.max))
            link(nc.vector.reciprocal(inv_out[:], out_deg[:]))
            nc.vector.tensor_scalar(isd[:], in_deg[:], 1.0, None, ALU.add).then_inc(pow_ask, 1)
            v.wait_ge(ff_lo_made, FT)
            for t in range(NT):
                nc.vector.tensor_scalar(tmp[:, t, 0:P], ident[:], inv_in[:, t:t + 1], None, ALU.mult)\
                  .then_inc(diag_made, 1)
            v.wait_ge(deg_done, 1)
            nc.vector.tensor_copy(inv_in_row[:], ps[:, 4, :]).then_inc(deg_made, 1)

            g2_row = wait_row(GAMMA2)

            def x1_finish(t):
                norm_scaled(LN2, t, g2_row)
                v.wait_ge(be2_added, t + 1)
                link(nc.vector.tensor_tensor(x_sb[:, t, :], x_sb[:, t, :], h_sb[:, t, :], ALU.add))
                norm_stats(LN3, t, x_sb)

            for t in range(NT):
                v.wait_ge(w2_done, t + 1)
                v.wait_ge(b2_added, t + 1)
                ins = nc.vector.tensor_tensor(h_sb[:, t, :], ps[:, t, :], h_sb[:, t, :], ALU.add)
                ins.then_inc(y2_read, 1)
                v.wait_ge(y2_read, t + 1)
                norm_stats(LN2, t, h_sb)
                if t >= 2:
                    norm_shift(LN3, t - 2)
                if t >= 1:
                    x1_finish(t - 1)
            norm_shift(LN3, NT - 2)
            transposed_lo(T3, 4, 0)
            x1_finish(NT - 1)
            norm_shift(LN3, NT - 1)
            for t in range(1, NT):
                transposed_lo(T3, 4, t)

            for t in range(NT):
                v.wait_ge(beta_hi_made, t + 1)
                nc.vector.tensor_tensor(R_lo[:, t, :], ps[:, t, :], f32(R_hi[:, t, :]), ALU.subtract)\
                  .then_inc(beta_lo_made, 1)
            v.wait_ge(cols_in, 16 * (5 + EXPERTS))
            link(nc.vector.tensor_copy(gw_hi[:], gate_w[:]))
            nc.vector.tensor_tensor(gw_lo[:], gate_w[:], f32(gw_hi[:]), ALU.subtract).then_inc(gate_split, 1)
            for t in range(NT):
                v.wait_ge(alpha_done, t + 1)
                v.wait_ge(bias1_added, t + 1)
                nc.vector.tensor_tensor(x_sb[:, t, :], ps[:, 4 + t, :], x_sb[:, t, :], ALU.add)\
                  .then_inc(alpha_added, 1)
            v.wait_ge(alpha_added, NT)

            def row_lo(t):
                v.wait_ge(hr_hi_made, t + 1)
                nc.vector.tensor_tensor(R_lo[:, t, :], h_sb[:, t, :], f32(R_hi[:, t, :]), ALU.subtract)\
                  .then_inc(hr_lo_made, 1)

            for t in range(NT + 3):
                if t < NT:
                    v.wait_ge(gamma_done, t + 1)
                    ins = nc.vector.scalar_tensor_tensor(x_sb[:, t, :], ps[:, t, :], inv_out[:, t:t + 1],
                                                         x_sb[:, t, :], ALU.mult, ALU.add)
                    ins.then_inc(x2_made, 1)
                    v.wait_ge(x2_made, t + 1)
                    norm_stats(LN4, t, x_sb)
                if 1 <= t <= NT:
                    norm_shift(LN4, t - 1)
                if 2 <= t < NT + 2:
                    row_lo(t - 2)
                if t >= 3:
                    transposed_lo(T4, 0, t - 3)

            for j in range(DT):
                v.wait_ge(agg_done, j + 1)
                nc.vector.tensor_tensor(tmp[:, j, :], ps[:, 4 + j, :], inv_in_row[:], ALU.mult).then_inc(agg_sum, 1)
                v.wait_ge(agg_hi_made, j + 1)
                nc.vector.tensor_tensor(agg_lo[:, j, :], tmp[:, j, :], f32(agg_hi[:, j, :]), ALU.subtract)\
                  .then_inc(agg_lo_made, 1)

            def over_experts(a):
                return a[:].unsqueeze(2).to_broadcast([P, NT, EXPERTS])

            v.wait_ge(logits_done, 1)
            ins = nc.vector.tensor_tensor(logit[:], ps[:, 3, 0:NT * EXPERTS].rearrange("p (t e) -> p t e", t=NT),
                                          gate_b[:].unsqueeze(1).to_broadcast([P, NT, EXPERTS]), ALU.add)
            ins.then_inc(logits_out, 1)
            v.wait_ge(logits_out, 1)
            link(nc.vector.tensor_reduce(gmax[:], logit[:], AX_X, ALU.max))
            nc.vector.tensor_tensor(logit[:], logit[:], over_experts(gmax), ALU.subtract).then_inc(gexp_ask, 1)
            v.wait_ge(gexp_done, 1)
            link(nc.vector.tensor_reduce(gsum[:], gate[:], AX_X, ALU.add))
            link(nc.vector.reciprocal(gsum[:], gsum[:]))
            link(nc.vector.tensor_tensor(gate[:], gate[:], over_experts(gsum), ALU.mult))
            for e in range(EXPERTS):
                others = [o for o in range(EXPERTS) if o != e]
                for o in others:
                    goal = rank[:, :, e] if o == others[0] else beats[:]
                    link(nc.vector.tensor_tensor(goal, gate[:, :, o], gate[:, :, e],
                                                 ALU.is_ge if o < e else ALU.is_gt))
                    if o != others[0]:
                        link(nc.vector.tensor_tensor(rank[:, :, e], rank[:, :, e], beats[:], ALU.add))
            link(nc.vector.scalar_tensor_tensor(gate[:], rank[:], TOP_K - 0.5, gate[:], ALU.is_lt, ALU.mult))

            for e in range(EXPERTS):
                if e == 0:
                    v.wait_ge(agg_lo_made, DT)
                else:
                    v.wait_ge(hid_lo_made, DT * e)
                for j in range(DT):
                    v.wait_ge(hid_hi_made, DT * e + j + 1)
                    link(nc.vector.tensor_scalar(tmp[:, j, :], ps[:, j, :], bl0[:, e, j:j + 1], 0.0,
                                                 ALU.add, ALU.max))
                    nc.vector.tensor_tensor(hid_lo[:, j, :], tmp[:, j, :], f32(hid_hi[:, j, :]), ALU.subtract)\
                      .then_inc(hid_lo_made, 1)
                for t in range(NT):
                    v.wait_ge(z_hi_made, NT * e + t + 1)
                    nc.vector.tensor_tensor(z_lo[:, t, :], ps[:, 4 + t, :], f32(z_hi[:, t, :]), ALU.subtract)\
                      .then_inc(z_lo_made, 1)
                v.wait_ge(bl_in[e % 2], 16 * (e // 2 + 1))
                if e >= 1:
                    v.wait_ge(x3_made, NT * e)
                for t in range(NT):
                    v.wait_ge(own_done, NT * e + t + 1)
                    nc.vector.tensor_tensor(part[:, t, :], ps[:, t, :], row_bl[e % 2][:], ALU.add)\
                      .then_inc(own_made, 1)
                v.wait_ge(own_made, NT * (e + 1))

                def add_expert(t):
                    v.wait_ge(expert_out, NT * e + t + 1)
                    ins = nc.vector.tensor_tensor(x_sb[:, t, :], x_sb[:, t, :], part[:, t, :], ALU.add)
                    ins.then_inc(x3_made, 1)
                    if e == EXPERTS - 1:
                        v.wait_ge(x3_made, NT * e + t + 1)
                        norm_stats(LN5, t, x_sb)

                for t in range(NT):
                    v.wait_ge(near_done, NT * e + t + 1)
                    nc.vector.scalar_tensor_tensor(part[:, t, :], ps[:, 4 + t, :], inv_in[:, t:t + 1], part[:, t, :],
                                                   ALU.mult, ALU.add).then_inc(expert_sum, 1)
                    if t >= 1:
                        add_expert(t - 1)
                    if e == EXPERTS - 1 and t >= 2:
                        norm_shift(LN5, t - 2)
                add_expert(NT - 1)
            norm_shift(LN5, NT - 2)
            norm_shift(LN5, NT - 1)
            for t in range(NT):
                transposed_lo(T5, 0, t)

            b3_row = wait_row(B3)
            v.wait_ge(pow_made, 1)
            for t in range(NT):
                v.wait_ge(H_done, t + 1)
                link(nc.vector.tensor_tensor(tmp[:, t, :], ps[:, 4 + t, :], b3_row[:], ALU.add))
                nc.vector.tensor_scalar(tmp[:, t, :], tmp[:, t, :], isd[:, t:t + 1], None, ALU.mult)\
                  .then_inc(H_made, 1)
                v.wait_ge(H_hi_made, t + 1)
                nc.vector.tensor_tensor(R_lo[:, t, :], tmp[:, t, :], f32(R_hi[:, t, :]), ALU.subtract)\
                  .then_inc(H_lo_made, 1)
            v.wait_ge(H_lo_made, NT)

            def finish(t):
                v.wait_ge(last_relu, t + 1)
                nc.vector.scalar_tensor_tensor(x_sb[:, t, :], tmp[:, t, :], no_edge_nan[:, t:t + 1], x_sb[:, t, :],
                                               ALU.add, ALU.add).then_inc(x4_made, 1)

            for t in range(NT):
                v.wait_ge(last_done, t + 1)
                nc.vector.tensor_tensor(tmp[:, t, :], ps[:, t, :], tmp[:, t, :], ALU.add).then_inc(last_sum, 1)
                if t >= 1:
                    finish(t - 1)
            finish(NT - 1)

        @block.tensor
        def _(pe):
            def mm3(goal, a_hi, a_lo, b_hi, b_lo, start, stop, **kw):
                nc.tensor.matmul(goal, a_hi, b_hi, start=start, stop=False, **kw)
                nc.tensor.matmul(goal, a_hi, b_lo, start=False, stop=False, **kw)
                return nc.tensor.matmul(goal, a_lo, b_hi, start=False, stop=stop, **kw)

            def weights(u):
                pe.wait_ge(lo_made, u + 1)
                return w_hi[u % 2], w_lo[u % 2]

            def col(t):
                return slice(t * P, (t + 1) * P)

            def transposes(bank, t):
                for j in range(DT):
                    last = nc.tensor.transpose(ps[:, bank + t, col(j)], h_sb[:, t, col(j)], ident[:])
                last.then_inc(tr_done, 1)

            def rows_tile(bank, t, w, done):
                for k in range(DT):
                    last = mm3(ps[:, bank + t, :], T_hi[:, k, col(t)], T_lo[:, k, col(t)], w[0][:, k, :],
                               w[1][:, k, :], k == 0, k == DT - 1)
                last.then_inc(done, 1)

            def sums_over_edges(bank, counts_hi, counts_lo, r_hi, r_lo, ready, value, done):
                for k in range(NT):
                    pe.wait_ge(ready, value + k + 1)
                    for t in range(NT):
                        goal = ps[:, bank + t, :]
                        nc.tensor.matmul(goal, counts_hi[:, k, col(t)], r_hi[:, k, :], start=k == 0, stop=False)
                        last = nc.tensor.matmul(goal, counts_hi[:, k, col(t)], r_lo[:, k, :], start=False,
                                                stop=k == NT - 1)
                        if k == NT - 1:
                            last.then_inc(done, 1)
                    if k == 0:
                        with pe.If(slow > 0):
                            pe.wait_ge(ready, value + NT)
                            for t in range(NT):
                                for kk in range(NT):
                                    nc.tensor.matmul(ps[:, bank + t, :], counts_lo[:, kk, col(t)], r_hi[:, kk, :],
                                                     start=False, stop=False, skip_group_check=True)

            def count_segment(n):
                with pe.Fori(0, RING // UN) as g:
                    pe.wait_ge(onehot, g + (n * (RING // UN) + 1))
                    for s in range(UN):
                        rows = one_src[:, bass.ds(g * UN + s, 1), :].squeeze(1)
                        for m in range(2):
                            cols = one_dst[:, bass.ds(g * UN + s, 1), m * P:(m + 1) * P].squeeze(1)
                            last = nc.tensor.matmul(ps[:, 7, m * HALF:(m + 1) * HALF], cols, rows,
                                                    start=False, stop=False, skip_group_check=True)
                    last.then_inc(onehot_used, 1)

            for t in range(NT):
                pe.wait_ge(ln_out, ln_out_no(LN0, t))
                pe.wait_ge(consts, 4)
                transposes(0, t)
            pe.wait_ge(zero_made, 1)
            nc.tensor.matmul(ps[:, 7, :], zeros[:, 0:P], zeros[:], start=True, stop=False, skip_group_check=True)
            pe.wait_ge(tr_lo, tr_no(T0, NT - 1))
            hi, lo = weights(WQ)
            for j in range(DT):
                for k in range(DT):
                    last = mm3(ps[:, j, :], hi[:, k, col(j)], lo[:, k, col(j)], T_hi[:, k, :], T_lo[:, k, :],
                               k == 0, k == DT - 1)
                last.then_inc(q_done, 1)
            count_segment(0)
            hi, lo = weights(WK)
            for j in range(DT):
                if k_bank(j) == 0:
                    pe.wait_ge(q_lo_made, 1)
                for k in range(DT):
                    last = mm3(ps[:, k_bank(j), :], hi[:, k, col(j)], lo[:, k, col(j)], T_hi[:, k, :], T_lo[:, k, :],
                               k == 0, k == DT - 1)
                last.then_inc(k_done, 1)
            count_segment(1)
            count_segment(2)
            pe.wait_ge(k_lo_made, PAIRS)
            pe.wait_ge(q_lo_made, PAIRS)
            w = weights(WV)
            for t in range(NT):
                rows_tile(0, t, w, v_done)
            count_segment(3)
            pe.wait_ge(total_ask, 1)
            nc.tensor.matmul(ps[0:1, 7, 0:1], checked[:, 0:1], one_col, start=True, stop=True).then_inc(total_done, 1)
            pe.wait_ge(flag_made, 1)
            slow = pe.value_load(slow_flag[0:1, 0:1], min_val=0, max_val=1)
            with pe.If(slow > 0):
                def count(slot, value, start):
                    pe.wait_ge(all_onehot, value)
                    for t in range(NT):
                        last = nc.tensor.matmul(ps[:, 4 + t, :], all_dst[:, slot, col(t)], all_src[:, slot, :],
                                                start=start, stop=False, skip_group_check=True)
                    last.then_inc(all_used, 1)

                for s in range(UN):
                    count(s, s + 1, s == 0)
                with pe.Fori(1, CH // UN) as g:
                    for s in range(UN):
                        count(s, g * UN + (s + 1), False)
                pe.wait_ge(all_copied, 2)

            def scores(i):
                mt, half = i % NT, i // NT
                if i == 0:
                    pe.wait_ge(neg_made, 1)
                else:
                    pe.wait_ge(exp_done, i)
                for h in range(HEADS):
                    rows, j = slice(HD * (h % 2), HD * (h % 2 + 1)), h // 2
                    q = slice(half * HN, (half + 1) * HN)
                    last = mm3(score_of(h), k_hi[rows, j, col(mt)], k_lo[rows, j, col(mt)], q_hi[rows, j, q],
                               q_lo[rows, j, q], h < 4, False, skip_group_check=True)
                last.then_inc(score_done, 1)

            def centre(i):
                pe.wait_ge(max_done, i + 1)
                for h in range(HEADS):
                    last = nc.tensor.matmul(score_of(h), neg_ident[:], m_bf[:], start=False, stop=True,
                                            skip_group_check=True)
                last.then_inc(centred, 1)

            def values(i, part_no):
                mt, half = i % NT, i // NT
                if i == 0:
                    pe.wait_ge(v_lo_made, NT)
                    pe.wait_ge(ct_ready, 1)
                if i == NT:
                    pe.wait_ge(att_lo_made, PAIRS)
                pe.wait_ge(p_lo_made, 2 * i + part_no + 1)
                q = slice(half * HN, (half + 1) * HN)
                for h in range(4 * part_no, 4 * part_no + 4):
                    goal = ps[:, h // 2, q]
                    mm3(goal, vz_hi[:, mt, h, :], vz_lo[:, mt, h, :], p_hi[:, h, :], p_lo[:, h, :],
                        mt == 0 and h % 2 == 0, False)
                    for vz in (vz_hi, vz_lo):
                        last = nc.tensor.matmul(goal, vz[:, mt, h, :], maskc[:, mt, q], start=False,
                                                stop=mt == NT - 1 and h % 2 == 1 and vz is vz_lo)
                last.then_inc(pv_done, 1)

            for i in range(2):
                scores(i)
                centre(i)
            for i in range(STEPS):
                if i + 2 < STEPS:
                    scores(i + 2)
                values(i, 0)
                if i + 2 < STEPS:
                    centre(i + 2)
                values(i, 1)

            pe.wait_ge(att_lo_made, 2 * PAIRS)
            w = weights(WO)
            for t in range(NT):
                rows_tile(4, t, w, wo_done)

            def count_transposes(src, bank, done):
                for s in range(NT):
                    for t in range(NT):
                        last = nc.tensor.transpose(ps[:, bank + s, col(t)], f32(src[:, t, col(s)]), ident[:])
                    last.then_inc(done, 1)

            count_transposes(ct_hi, 0, c_tr)

            for t in range(NT):
                pe.wait_ge(h_ready, t + 1)
                transposes(4, t)
            for j in range(DT):
                pe.wait_ge(c_hi_made, j + 1)
            hi, lo = weights(W1A)
            for half in range(2):
                pe.wait_ge(tr_lo, tr_no(T1, 2 * half + 1))
                n = slice(half * HN, (half + 1) * HN)
                for j in range(DT):
                    for k in range(DT):
                        last = mm3(ps[:, j, n], hi[:, k, col(j)], lo[:, k, col(j)], T_hi[:, k, n], T_lo[:, k, n],
                                   half == 0 and k == 0, k == DT - 1, skip_group_check=True)
                    if half:
                        last.then_inc(ff_done, 1)
            hi, lo = weights(W1B)
            for j in range(DT, FT):
                for k in range(DT):
                    last = mm3(ps[:, j, :], hi[:, k, col(j - DT)], lo[:, k, col(j - DT)],
                               T_hi[:, k, :], T_lo[:, k, :], k == 0, k == DT - 1)
                last.then_inc(ff_done, 1)
            for half in range(2):
                hi, lo = weights(W2A + half)
                pe.wait_ge(ff_lo_made, DT * (half + 1))
                for t in range(NT):
                    for k in range(DT):
                        f = half * DT + k
                        last = mm3(ps[:, t, :], ff_hi[:, f, col(t)], ff_lo[:, f, col(t)], hi[:, k, :],
                                   lo[:, k, :], f == 0, f == FT - 1)
                    last.then_inc(w2_done if half else w2_half_done, 1)
                if half == 0:
                    with pe.If(slow > 0):
                        pe.wait_ge(ff_lo_made, FT)
                        count_transposes(ct_lo, 4, c_lo_tr)
                        pe.wait_ge(c_lo_made, 1)
                    pe.wait_ge(diag_made, NT)
                    pe.wait_ge(ones_made, 1)
                    for t in range(NT):
                        last = nc.tensor.matmul(ps[:, 4, col(t)], ones[:], tmp[:, t, 0:P], start=True, stop=True)
                    last.then_inc(deg_done, 1)

            pe.wait_ge(deg_made, 1)
            w = weights(WN)
            for t in range(NT):
                pe.wait_ge(ln_out, ln_out_no(LN3, t))
                transposes(4, t)
                if t >= 1:
                    pe.wait_ge(tr_lo, tr_no(T3, t - 1))
                    pe.wait_ge(y2_read, t)
                    rows_tile(0, t - 1, w, beta_done)
            pe.wait_ge(tr_lo, tr_no(T3, NT - 1))
            pe.wait_ge(y2_read, NT)
            rows_tile(0, NT - 1, w, beta_done)
            w = weights(WC)
            for t in range(NT):
                rows_tile(4, t, w, alpha_done)
            pe.wait_ge(beta_lo_made, NT)
            sums_over_edges(0, ct_hi, ct_lo, R_hi, R_lo, beta_lo_made, 0, gamma_done)

            pe.wait_ge(alpha_added, NT)
            for k in range(NT):
                pe.wait_ge(ln_out, ln_out_no(LN4, k))
                transposes(0, k)
                pe.wait_ge(hr_lo_made, k + 1)
                for j in range(DT):
                    goal = ps[:, 4 + j, :]
                    nc.tensor.matmul(goal, R_hi[:, k, col(j)], c_hi[:, k, :], start=k == 0, stop=False)
                    last = nc.tensor.matmul(goal, R_lo[:, k, col(j)], c_hi[:, k, :], start=False, stop=k == NT - 1)
                    if k == NT - 1:
                        last.then_inc(agg_done, 1)
                if k == NT - 2:
                    with pe.If(slow > 0):
                        for j in range(DT):
                            for kk in range(NT - 1):
                                nc.tensor.matmul(ps[:, 4 + j, :], R_hi[:, kk, col(j)], c_lo[:, kk, :],
                                                 start=False, stop=False, skip_group_check=True)
                        pe.wait_ge(hr_lo_made, NT)
                        for j in range(DT):
                            nc.tensor.matmul(ps[:, 4 + j, :], R_hi[:, NT - 1, col(j)], c_lo[:, NT - 1, :],
                                             start=False, stop=False, skip_group_check=True)
            pe.wait_ge(tr_lo, tr_no(T4, NT - 1))
            pe.wait_ge(gate_split, 1)
            for t in range(NT):
                for k in range(DT):
                    last = mm3(ps[:, 3, t * EXPERTS:(t + 1) * EXPERTS], T_hi[:, k, col(t)], T_lo[:, k, col(t)],
                               gw_hi[:, k, :], gw_lo[:, k, :], k == 0, k == DT - 1)
            last.then_inc(logits_done, 1)

            for e in range(EXPERTS):
                for n, (a_hi, a_lo) in enumerate(((T_hi, T_lo), (agg_hi, agg_lo))):
                    hi, lo = weights(FIRST_EXPERT + 4 * e + n)
                    if n == 0 and e >= 1:
                        pe.wait_ge(own_made, NT * e)
                    for j in range(DT):
                        if n == 0 and e == 0 and j == 3:
                            pe.wait_ge(logits_out, 1)
                        if n == 1 and e == 0 and j == 0:
                            pe.wait_ge(agg_lo_made, DT)
                        for k in range(DT):
                            last = mm3(ps[:, j, :], hi[:, k, col(j)], lo[:, k, col(j)], a_hi[:, k, :],
                                       a_lo[:, k, :], n == 0 and k == 0, n == 1 and k == DT - 1)
                        last.then_inc(hid_done if n else hid_half_done, 1)
                hi, lo = weights(FIRST_EXPERT + 4 * e + 2)
                if e >= 1:
                    pe.wait_ge(expert_sum, NT * e)
                for k in range(DT):
                    pe.wait_ge(hid_lo_made, DT * e + k + 1)
                    for t in range(NT):
                        last = mm3(ps[:, 4 + t, :], hid_hi[:, k, col(t)], hid_lo[:, k, col(t)], hi[:, k, :],
                                   lo[:, k, :], k == 0, k == DT - 1)
                        if k == DT - 1:
                            last.then_inc(z_done, 1)
                hi, lo = weights(FIRST_EXPERT + 4 * e + 3)
                for t in range(NT):
                    for k in range(DT):
                        last = mm3(ps[:, t, :], hid_hi[:, k, col(t)], hid_lo[:, k, col(t)], hi[:, k, :],
                                   lo[:, k, :], k == 0, k == DT - 1)
                    last.then_inc(own_done, 1)
                pe.wait_ge(z_lo_made, NT * (e + 1))
                sums_over_edges(4, c_hi, c_lo, z_hi, z_lo, z_lo_made, NT * e, near_done)

            pe.wait_ge(own_made, NT * EXPERTS)
            w = weights(W_LAST)
            for t in range(NT):
                pe.wait_ge(ln_out, ln_out_no(LN5, t))
                transposes(0, t)
                if t >= 1:
                    pe.wait_ge(tr_lo, tr_no(T5, t - 1))
                    pe.wait_ge(expert_sum, NT * (EXPERTS - 1) + t)
                    rows_tile(4, t - 1, w, H_done)
            pe.wait_ge(tr_lo, tr_no(T5, NT - 1))
            rows_tile(4, NT - 1, w, H_done)
            sums_over_edges(0, c_hi, c_lo, R_hi, R_lo, H_lo_made, 0, last_done)


_INS = ["x", "src", "dst",
        *(f"L0_gnn_{n}" for n in ("Wq", "bq", "Wk", "bk", "Wv", "bv", "Wo", "bo", "W1", "b1", "W2", "b2", "g1",
                                  "be1", "g2", "be2")),
        "L1_gnn_wc", "L1_gnn_wn", "L1_gnn_bias",
        *(f"L2_gnn_{n}" for n in ("gate_W", "gate_b", "Wl", "bl", "Wr")), "L3_gnn_W", "L3_gnn_b"]


def kernel(**inputs):
    import concourse.bacc as bacc
    from concourse.bass_utils import run_bass_kernel_spmd

    nc = bacc.Bacc("TRN2", target_bir_lowering=False, num_devices=1)
    arrays, d = {}, {}
    for name in _INS:
        a = np.ascontiguousarray(inputs[name])
        arrays[f"in_{name}"] = a
        d[name] = nc.dram_tensor(f"in_{name}", a.shape, mybir.dt.from_np(a.dtype), kind="ExternalInput").ap()
    out = nc.dram_tensor("out", arrays["in_x"].shape, F32, kind="ExternalOutput").ap()
    build(nc, d, out)
    r = run_bass_kernel_spmd(nc, [arrays], core_ids=[0])
    return r.results[0]["out"]
```

```python
from contextlib import ExitStack

import numpy as np

import concourse.bass as bass
from concourse import mybir
from concourse.alu_op_type import AluOpType as ALU

ACT = mybir.ActivationFunctionType
F32 = mybir.dt.float32
F32R = mybir.dt.float32r
F16 = mybir.dt.float16
BF16 = mybir.dt.bfloat16
I32 = mybir.dt.int32
AX_X = mybir.AxisListType.X

P = 128
EPS = 1e-5
TOP_K = 2


def build(nc, d, out):
    N, D = d["x"].shape
    E = d["src"].shape[0]
    NT = N // P
    DT = D // P
    FT = 2 * D // P
    CH = E // P
    HEADS = 8
    HD = D // HEADS
    PAIRS = HEADS // 2
    EXPERTS = d["L2_gnn_gate_W"].shape[1]
    SCALE = float(HD) ** -0.5
    HN = N // 2
    STEPS = 2 * NT
    HALF = N // 2
    DIGIT = 6
    POOL_HEADS = 2
    UN = 8
    UW = 4
    ACT_CHUNKS = 4
    RING = 32
    SEGMENTS = CH // RING
    FAR = 2.0 ** 100
    W_SCALE = 2.0 ** 9
    assert N == D == 512 and NT == DT == 4 and HD == 64 and CH % RING == 0 and RING % UN == 0

    at = [-(-nc.sbuf_base // 32) * 32]

    def region(size):
        start = at[0]
        at[0] += size
        return start

    def place(name, shape, dt, offset):
        return nc.alloc_sbuf_tensor_at(name, shape, dt, offset=offset)

    MAT = NT * D * 4
    rW, rX, rH, rT, rCT, rQK, rVZ, rEP, rM = (region(k * MAT) for k in (6, 1, 1, 2, 2, 4, 4, 3, 1))
    rB, rBL, rS = region(4 * D * 4), region(2 * D * 4), region(2048 + 1280)

    stage = [place(f"w_stage{i}", [P, 4, D], F32, rW + i * MAT) for i in range(2)]
    w_hi = [place(f"w_hi{i}", [P, 4, D], F32R, rW + (2 + i) * MAT) for i in range(2)]
    w_lo = [place(f"w_lo{i}", [P, 4, D], F32R, rW + (4 + i) * MAT) for i in range(2)]
    x_sb = place("x_sb", [P, NT, D], F32, rX)
    h_sb = place("h_sb", [P, NT, D], F32, rH)
    T_hi = place("T_hi", [P, DT, N], F32R, rT)
    T_lo = place("T_lo", [P, DT, N], F32R, rT + MAT)
    ct_hi = place("ct_hi", [P, NT, N], F32R, rCT)
    ct_lo = place("ct_lo", [P, NT, N], F32R, rCT + MAT)
    q_hi = place("q_hi", [P, PAIRS, N], F32R, rQK)
    q_lo = place("q_lo", [P, PAIRS, N], F32R, rQK + MAT)
    k_hi = place("k_hi", [P, PAIRS, N], F32R, rQK + 2 * MAT)
    k_lo = place("k_lo", [P, PAIRS, N], F32R, rQK + 3 * MAT)
    ff_hi = place("ff_hi", [P, FT, N], F32R, rQK)
    ff_lo = place("ff_lo", [P, FT, N], F32R, rQK + 2 * MAT)
    R_hi = place("R_hi", [P, NT, D], F32R, rQK)
    R_lo = place("R_lo", [P, NT, D], F32R, rQK + MAT)
    agg_hi = place("agg_hi", [P, DT, N], F32R, rQK + 2 * MAT)
    agg_lo = place("agg_lo", [P, DT, N], F32R, rQK + 3 * MAT)
    VZ = 3 * HD
    vz_hi = place("vz_hi", [P, NT, PAIRS, VZ], F32R, rVZ)
    vz_lo = place("vz_lo", [P, NT, PAIRS, VZ], F32R, rVZ + NT * PAIRS * VZ * 4)
    e_two = [place("e_sb0", [P, HEADS, HN], F32, rVZ + 2 * NT * PAIRS * VZ * 4),
             place("e_sb1", [P, HEADS, HN], F32, rEP)]
    c_hi = place("c_hi", [P, NT, N], F32R, rVZ)
    c_lo = place("c_lo", [P, NT, N], F32R, rVZ + MAT)
    hid_hi = place("hid_hi", [P, DT, N], F32R, rVZ + 2 * MAT)
    hid_lo = place("hid_lo", [P, DT, N], F32R, rVZ + 3 * MAT)
    tmp = place("tmp", [P, NT, D], F32, rEP)
    p_hi = place("p_hi", [P, HEADS, HN], F32R, rEP + MAT)
    p_lo = place("p_lo", [P, HEADS, HN], F32R, rEP + 2 * MAT)
    z_hi = place("z_hi", [P, NT, D], F32R, rEP + MAT)
    z_lo = place("z_lo", [P, NT, D], F32R, rEP + 2 * MAT)
    no_edge = place("no_edge", [P, NT, N], BF16, rM)
    part = place("part", [P, NT, D], F32, rM)
    one_dst = place("one_dst", [P, RING, HALF], F16, rVZ)
    one_src = place("one_src", [P, RING, HALF], F16, rVZ + RING * HALF * 2)
    all_dst = place("all_dst", [P, UW, N], F16, rEP)
    all_src = place("all_src", [P, UW, N], F16, rEP + UW * N * 2)
    edge_i = place("edge_i", [P, 2, CH], I32, rEP + MAT)
    edge_f = place("edge_f", [P, 2, CH], F32, rEP + MAT + 1024)
    upper = place("upper", [P, 2, CH], F32, rEP + MAT + 2048)
    edge_m = place("edge_m", [P, 2, CH], F32, rEP + MAT + 3072)
    edge_w = place("edge_w", [P, CH], F32, rEP + MAT + 4096)
    iota_n = place("iota_n", [P, N], F16, rEP + MAT + 4608)
    packed = place("packed", [P, 2, HALF], I32, rEP + MAT + 5632)
    distance = place("distance", [P, ACT_CHUNKS, HALF], F16, rEP + 2 * MAT)
    edge_neg = place("edge_neg", [P, CH], F32, rEP + 2 * MAT + 2048)
    checked = place("checked", [P, 2], F32, rEP + MAT + 7680)
    slow_flag = place("slow_flag", [P, 1], I32, rEP + MAT + 7712)
    zeros = place("zeros", [P, N], F16, rEP)
    digits = place("digits", [P, NT, N], I32, rEP + 2 * MAT)
    row = [place(f"row{i}", [P, D], F32, rB + i * D * 4) for i in range(4)]
    row_bl = [place(f"row_bl{i}", [P, D], F32, rBL + i * D * 4) for i in range(2)]
    inv_in_row = place("inv_in_row", [P, N], F32, rS)
    rsum = place("rsum", [P, 2, HN], F32, rS)
    small = [rS + 2048]

    def little(name, shape, dt=F32):
        start = small[0]
        size = int(np.prod(shape[1:])) * (2 if dt == BF16 else 4)
        small[0] += -(-size // 32) * 32
        return place(name, shape, dt, start)

    qk_bias = little("qk_bias", [P, 2, DT])
    bq, bk = qk_bias[:, 0, :], qk_bias[:, 1, :]
    b1 = little("b1", [P, FT])
    bl0 = little("bl0", [P, EXPERTS, DT])
    gate_b = little("gate_b", [P, EXPERTS])
    gate_w = little("gate_w", [P, DT, EXPERTS])
    gw_hi = little("gw_hi", [P, DT, EXPERTS], F32R)
    gw_lo = little("gw_lo", [P, DT, EXPERTS], F32R)
    scalars = little("scalars", [P, 2])
    one_col, half_neg = scalars[:, 0:1], scalars[:, 1:2]
    stats = little("stats", [P, 6])
    moments = little("moments", [P, 6 * NT, 2])
    vareps = little("vareps", [P, 6 * NT])
    rstd = little("rstd", [P, 6 * NT])
    shift = little("shift", [P, 6 * NT])
    in_deg = little("in_deg", [P, NT])
    inv_in = little("inv_in", [P, NT])
    isd = little("isd", [P, NT])
    out_deg = little("out_deg", [P, NT])
    inv_out = little("inv_out", [P, NT])
    no_edge_nan = little("no_edge_nan", [P, NT])
    G1 = [P, NT, EXPERTS]
    logit = little("logit", G1)
    gmax = little("gmax", [P, NT])
    gate = little("gate", G1)
    gsum = little("gsum", [P, NT])
    rank = little("rank", G1)
    beats = little("beats", [P, NT])
    sbuf_end = small[0]
    at[0] = -(-sbuf_end // 32) * 32
    ident = place("ident", [P, P], F32, region(P * 4))
    m_bf = place("m_bf", [P, HN], BF16, rBL)
    neg_ident = place("neg_ident", [P, P], BF16, rBL + HN * 2)
    m_half = place("m_half", [P, 2, HN], F32, rBL + 1024)
    ones = place("ones", [P, P], F32, rM)
    assert at[0] <= nc.sbuf_usable_end, (at[0], nc.sbuf_usable_end)

    def matrix(a, rows=slice(0, D), cols=slice(0, D)):
        return a[rows, cols].rearrange("(t p) n -> p t n", p=P)

    w1, w2 = d["L0_gnn_W1"], d["L0_gnn_W2"]
    units = [matrix(d[f"L0_gnn_{n}"]) for n in ("Wq", "Wk", "Wv", "Wo")]
    units += [matrix(w1, cols=slice(j * D, (j + 1) * D)) for j in range(2)]
    units += [matrix(w2, rows=slice(j * D, (j + 1) * D)) for j in range(2)]
    units += [matrix(d["L1_gnn_wn"]), matrix(d["L1_gnn_wc"])]
    FIRST_EXPERT = len(units)
    for e in range(EXPERTS):
        wl, wr = d["L2_gnn_Wl"], d["L2_gnn_Wr"]
        units += [matrix(a[e, layer]) for a, layer in ((wr, 0), (wl, 0), (wl, 1), (wr, 1))]
    units.append(matrix(d["L3_gnn_W"]))
    (WQ, WK, WV, WO, W1A, W1B, W2A, W2B, WN, WC) = range(FIRST_EXPERT)
    W_LAST = len(units) - 1

    rows_in = [("L0_gnn_bv", 0), ("L0_gnn_bo", 1), ("L0_gnn_g1", 2), ("L0_gnn_be1", 3),
               ("L0_gnn_b2", 0), ("L0_gnn_g2", 1), ("L0_gnn_be2", 2), ("L1_gnn_bias", 3),
               ("L3_gnn_b", 0)]
    BV, BO, GAMMA1, BETA1, B2, GAMMA2, BETA2, BIAS1, B3 = range(len(rows_in))

    LN0, LN1, LN2, LN3, LN4, LN5 = range(6)
    ln_order = [(LN0, t) for t in range(NT)] + [(LN1, t) for t in range(NT)]
    ln_order += [(LN2, 0)] + [x for t in range(1, NT) for x in ((LN2, t), (LN3, t - 1))] + [(LN3, NT - 1)]
    ln_order += [(k, t) for k in (LN4, LN5) for t in range(NT)]

    def ln_no(k, t):
        return ln_order.index((k, t)) + 1

    out_order = [(k, t) for k in (LN0, LN3, LN4, LN5) for t in range(NT)]

    def ln_out_no(k, t):
        return out_order.index((k, t)) + 1

    T0, T1, T3, T4, T5 = range(5)

    def tr_no(k, t):
        return NT * k + t + 1

    ctx = ExitStack()
    with ctx:
        ps = ctx.enter_context(nc.psum_tensor("ps", [P, 8, 512], F32))

        def sem(name):
            return ctx.enter_context(nc.semaphore(name))

        x_in = [sem(f"x_in{t}") for t in range(NT)]
        edges_in = sem("edges_in")
        cols_in = sem("cols_in")
        row_in = [sem(f"row_in{i}") for i in range(4)]
        bl_in = [sem(f"bl_in{i}") for i in range(2)]
        stage_in = [sem(f"stage_in{i}") for i in range(2)]
        hi_made = sem("hi_made")
        lo_made = sem("lo_made")
        wq_rest_made = sem("wq_rest_made")
        consts = sem("consts")
        neg_made = sem("neg_made")
        onehot = sem("onehot")
        onehot_act = sem("onehot_act")
        distance_made = sem("distance_made")
        onehot_used = sem("onehot_used")
        digits_made = sem("digits_made")
        ct_hi_made = sem("ct_hi_made")
        total_ask = sem("total_ask")
        total_done = sem("total_done")
        flag_made = sem("flag_made")
        all_onehot = sem("all_onehot")
        all_used = sem("all_used")
        all_copied = sem("all_copied")
        ct_ready = sem("ct_ready")
        rinv_made, prob_pool = sem("rinv_made"), sem("prob_pool")
        dve = sem("dve")
        pool = sem("pool")
        ln_var = sem("ln_var")
        ln_rstd = sem("ln_rstd")
        ln_scale = sem("ln_scale")
        ln_out = sem("ln_out")
        h_ready = sem("h_ready")
        tr_done = sem("tr_done")
        tr_hi = sem("tr_hi")
        tr_lo = sem("tr_lo")
        vz_zero = sem("vz_zero")
        q_done, q_hi_made, q_lo_made = sem("q_done"), sem("q_hi_made"), sem("q_lo_made")
        k_done, k_hi_made, k_lo_made = sem("k_done"), sem("k_hi_made"), sem("k_lo_made")
        v_done, v_sum, v_hi_made, v_lo_made = sem("v_done"), sem("v_sum"), sem("v_hi_made"), sem("v_lo_made")
        ones_made = sem("ones_made")
        zero_made = sem("zero_made")
        diag_made = sem("diag_made")
        score_done, max_done, centred = sem("score_done"), sem("max_done"), sem("centred")
        exp_done, prob_done, p_hi_made, p_lo_made = sem("exp_done"), sem("prob_done"), sem("p_hi_made"), sem("p_lo_made")
        pv_done = sem("pv_done")
        att_hi_made, att_lo_made = sem("att_hi_made"), sem("att_lo_made")
        bo_added, b2_added, be2_added, bias1_added = sem("bo_added"), sem("b2_added"), sem("be2_added"), sem("bias1_added")
        wo_done = sem("wo_done")
        c_tr, c_hi_made, c_lo_tr, c_lo_made = sem("c_tr"), sem("c_hi_made"), sem("c_lo_tr"), sem("c_lo_made")
        ff_done, ff_hi_made, ff_lo_made = sem("ff_done"), sem("ff_hi_made"), sem("ff_lo_made")
        w2_half_done, w2_done = sem("w2_half_done"), sem("w2_done")
        y2_read = sem("y2_read")
        beta_done, beta_hi_made, beta_lo_made = sem("beta_done"), sem("beta_hi_made"), sem("beta_lo_made")
        alpha_done, alpha_added = sem("alpha_done"), sem("alpha_added")
        gamma_done, x2_made = sem("gamma_done"), sem("x2_made")
        deg_done, deg_made = sem("deg_done"), sem("deg_made")
        pow_ask, pow_made = sem("pow_ask"), sem("pow_made")
        hr_hi_made, hr_lo_made = sem("hr_hi_made"), sem("hr_lo_made")
        gate_split, logits_done, logits_out = sem("gate_split"), sem("logits_done"), sem("logits_out")
        gexp_ask, gexp_done = sem("gexp_ask"), sem("gexp_done")
        agg_done, agg_sum, agg_hi_made, agg_lo_made = sem("agg_done"), sem("agg_sum"), sem("agg_hi_made"), sem("agg_lo_made")
        hid_half_done = sem("hid_half_done")
        hid_done, hid_hi_made, hid_lo_made = sem("hid_done"), sem("hid_hi_made"), sem("hid_lo_made")
        z_done, z_hi_made, z_lo_made = sem("z_done"), sem("z_hi_made"), sem("z_lo_made")
        own_done, own_made = sem("own_done"), sem("own_made")
        near_done, expert_sum, expert_out = sem("near_done"), sem("expert_sum"), sem("expert_out")
        x3_made = sem("x3_made")
        H_done, H_made, H_hi_made, H_lo_made = sem("H_done"), sem("H_made"), sem("H_hi_made"), sem("H_lo_made")
        last_done, last_sum, last_relu, x4_made = sem("last_done"), sem("last_sum"), sem("last_relu"), sem("x4_made")
        stored = sem("stored")

        block = ctx.enter_context(nc.Block())

        w_spent = [(q_done, DT), (k_done, DT), (v_done, NT), (wo_done, NT), (ff_done, DT), (ff_done, FT),
                   (w2_half_done, NT), (w2_done, NT), (beta_done, NT), (alpha_done, NT)]
        for e in range(EXPERTS):
            w_spent += [(done, 4 * (e + 1)) for done in (hid_half_done, hid_done, z_done, own_done)]

        def k_bank(j):
            return (4, 5, 6, 0)[j]

        def f32(t):
            return t.bitcast(F32)

        SLOT_BANK = (4, 6, 2)

        def slot_bank(i, g):
            return SLOT_BANK[(2 * i + g) % 3]

        def score_of(i, h):
            half = h // 2 % 2
            return ps[:, slot_bank(i, h // 4) + h % 2, half * HN:(half + 1) * HN]

        def group_scores(i, g):
            bank = slot_bank(i, g)
            return ps[:, bank:bank + 2, :].rearrange("p b (w n) -> p w b n", w=2)

        def scores_by_column(bank, banks):
            return ps[:, bank:bank + banks, :].rearrange("p b (w n) -> p n b w", w=2)

        def attended():
            return ps[:, 0:2, :].rearrange("p b (w n) -> p (b w) n", w=2)

        def probabilities(engine, i, heads):
            e = e_two[i % 2][:, heads]
            return engine.tensor_tensor(e, e, rsum[:, i % 2:i % 2 + 1, :].to_broadcast(list(e.shape)), ALU.mult)

        @block.sync
        def _(sp):
            for t in range(NT):
                sp.dma_start(x_sb[:, t, :], d["x"][t * P:(t + 1) * P, :]).then_inc(x_in[t], 16)
            sp.dma_start(edge_i[:, 0, :], d["src"].rearrange("(p c) -> p c", p=P)).then_inc(edges_in, 16)
            sp.dma_start(edge_i[:, 1, :], d["dst"].rearrange("(p c) -> p c", p=P)).then_inc(edges_in, 16)

            row_free = {B2: (v_sum, NT), GAMMA2: (bo_added, NT), BETA2: (h_ready, NT), BIAS1: (h_ready, NT),
                        B3: (b2_added, NT)}

            def load_row(i):
                name, slot = rows_in[i]
                if i in row_free:
                    sp.wait_ge(*row_free[i])
                sp.dma_start(row[slot][:], d[name].unsqueeze(0).to_broadcast([P, D])).then_inc(row_in[slot], 16)

            def load_bl(e):
                if e >= 2:
                    sp.wait_ge(own_made, NT * (e - 1))
                sp.dma_start(row_bl[e % 2][:], d["L2_gnn_bl"][e, 1].unsqueeze(0).to_broadcast([P, D]))\
                  .then_inc(bl_in[e % 2], 16)

            def load_columns():
                with nc.allow_non_contiguous_dma("small per-partition vectors"):
                    for dst, src in ((bq, d["L0_gnn_bq"].rearrange("(j p) -> p j", p=P)),
                                     (bk, d["L0_gnn_bk"].rearrange("(j p) -> p j", p=P)),
                                     (b1[:], d["L0_gnn_b1"].rearrange("(j p) -> p j", p=P)),
                                     (gate_w[:], d["L2_gnn_gate_W"].rearrange("(t p) e -> p t e", p=P)),
                                     (gate_b[:], d["L2_gnn_gate_b"].unsqueeze(0).to_broadcast([P, EXPERTS]))):
                        sp.dma_start(dst, src).then_inc(cols_in, 16)
                    for e in range(EXPERTS):
                        sp.dma_start(bl0[:, e, :], d["L2_gnn_bl"][e, 0].rearrange("(j p) -> p j", p=P))\
                           .then_inc(cols_in, 16)

            ahead = {WQ: [BV], WK: [BO, GAMMA1], WV: [BETA1], W1B: [B2, GAMMA2], W2A: [BETA2, BIAS1],
                     FIRST_EXPERT + 1: [B3]}
            for u, src in enumerate(units):
                if u >= 2:
                    sp.wait_ge(lo_made, u - 1)
                if u == 2:
                    sp.wait_ge(wq_rest_made, 1)
                sp.dma_start(stage[u % 2][:], src).then_inc(stage_in[u % 2], 16)
                if u == WK:
                    load_columns()
                for i in ahead.get(u, []):
                    load_row(i)
                if u in (WN, WC):
                    load_bl(u - WN)
                if u in (FIRST_EXPERT + 9, FIRST_EXPERT + 13):
                    load_bl((u - FIRST_EXPERT - 1) // 4)
            for t in range(NT):
                sp.wait_ge(x4_made, t + 1)
                sp.dma_start(out[t * P:(t + 1) * P, :], x_sb[:, t, :]).then_inc(stored, 16)
            sp.wait_ge(stored, 16 * NT)

        @block.gpsimd
        def _(gp):
            gp.iota(iota_n[:], pattern=[[1, N]], base=0, channel_multiplier=0,
                    allow_small_or_imprecise_dtypes=True).then_inc(consts, 1)
            gp.memset(ident[:], 0.0).then_inc(pool, 1)
            gp.memset(half_neg, -0.5).then_inc(consts, 1)
            gp.memset(one_col, 1.0).then_inc(consts, 1)
            gp.memset(zeros[:], 0.0).then_inc(zero_made, 1)
            gp.wait_ge(pool, 1)
            gp.affine_select(out=ident[:], in_=ident[:], compare_op=ALU.not_equal, fill=1.0, base=0,
                             pattern=[[-1, P]], channel_multiplier=1).then_inc(consts, 1)
            gp.wait_ge(consts, 4)

            def split_lo(u):
                gp.wait_ge(hi_made, u + 1)
                if u >= 2:
                    gp.wait_ge(*w_spent[u - 2])
                s = u % 2
                first = gp.tensor_tensor(w_lo[s][:, 0:2], stage[s][:, 0:2], f32(w_hi[s][:, 0:2]), ALU.subtract)
                if u == WQ:
                    first.then_inc(lo_made, 1)
                    return
                gp.tensor_tensor(w_lo[s][:, 2:4], stage[s][:, 2:4], f32(w_hi[s][:, 2:4]), ALU.subtract)\
                  .then_inc(lo_made, 1)

            def rstd_of(k):
                for t in range(NT):
                    power(ln_no(k, t))

            def power(n):
                gp.wait_ge(ln_var, n)
                gp.tensor_tensor(rstd[:, n - 1:n], vareps[:, n - 1:n], half_neg, ALU.pow).then_inc(ln_rstd, 1)

            def add_row(i, t, target, done):
                slot = rows_in[i][1]
                if t == 0:
                    gp.wait_ge(row_in[slot], 16 * (1 + sum(s == slot for _, s in rows_in[:i])))
                ins = gp.tensor_tensor(target[:, t, :], target[:, t, :], row[slot][:], ALU.add)
                ins.then_inc(done, 1)

            def split_p_lo(i):
                for g in range(2):
                    gp.wait_ge(p_hi_made, 2 * i + g + 1)
                    if i >= 1:
                        gp.wait_ge(pv_done, 2 * i + g - 1)
                    heads = slice(g * HEADS // 2, (g + 1) * HEADS // 2)
                    gp.tensor_tensor(p_lo[:, heads], e_two[i % 2][:, heads], f32(p_hi[:, heads]),
                                     ALU.subtract).then_inc(p_lo_made, 1)

            rstd_of(LN0)
            split_lo(WQ)
            split_lo(WK)
            gp.wait_ge(tr_done, tr_no(T0, NT - 1))
            for t in range(NT):
                add_row(BO, t, h_sb, bo_added)
            split_lo(WV)
            gp.wait_ge(onehot_used, CH // UN)
            gp.memset(f32(vz_hi[:, :, :, HD:2 * HD]), 0.0).then_inc(vz_zero, 1)
            gp.memset(f32(vz_lo[:, :, :, HD:2 * HD]), 0.0).then_inc(vz_zero, 1)
            split_lo(WO)
            for i in range(STEPS):
                gp.wait_ge(rinv_made, i + 1)
                probabilities(gp, i, slice(HEADS - POOL_HEADS, HEADS)).then_inc(prob_pool, 1)
                split_p_lo(i)
                if i == 1:
                    split_lo(W1A)
            rstd_of(LN1)
            for t in range(NT):
                gp.wait_ge(tr_done, tr_no(T1, t))
                add_row(B2, t, h_sb, b2_added)
            gp.memset(ones[:], 1.0).then_inc(ones_made, 1)
            split_lo(W1B)
            for t in range(NT):
                add_row(BETA2, t, x_sb, be2_added)
            split_lo(W2A)
            split_lo(W2B)
            split_lo(WN)
            for k, t in ln_order[2 * NT:4 * NT]:
                power(ln_no(k, t))
            split_lo(WC)
            for t in range(NT):
                gp.wait_ge(ln_out, ln_out_no(LN3, t))
                add_row(BIAS1, t, x_sb, bias1_added)
            gp.wait_ge(pow_ask, 1)
            gp.tensor_tensor(isd[:], isd[:], half_neg.to_broadcast([P, NT]), ALU.pow).then_inc(pow_made, 1)
            split_lo(FIRST_EXPERT)
            rstd_of(LN4)
            for u in range(FIRST_EXPERT + 1, W_LAST + 1):
                split_lo(u)
            rstd_of(LN5)

        @block.scalar
        def _(act):
            def split_hi(u):
                act.wait_ge(stage_in[u % 2], 16 * (u // 2 + 1))
                if u >= 2:
                    act.wait_ge(*w_spent[u - 2])
                nc.scalar.activation(w_hi[u % 2][:], stage[u % 2][:], ACT.Copy).then_inc(hi_made, 1)

            def normalise(k, t, dst, src, func):
                n = ln_no(k, t)
                act.wait_ge(ln_scale, ln_out_no(k, t))
                nc.scalar.activation(dst[:, t, :], src[:, t, :], func, scale=rstd[:, n - 1:n],
                                     bias=shift[:, n - 1:n]).then_inc(ln_out, 1)

            def transposed_hi(k, bank, only=None):
                for t in range(NT) if only is None else [only]:
                    act.wait_ge(tr_done, tr_no(k, t))
                    nc.scalar.activation(T_hi[:, :, t * P:(t + 1) * P],
                                         ps[:, bank + t, :].rearrange("p (k n) -> p k n", k=DT),
                                         ACT.Copy).then_inc(tr_hi, 1)

            for t in range(NT):
                normalise(LN0, t, h_sb, x_sb, ACT.Relu)
            split_hi(WQ)
            def packed_one_hots(first, count):
                with act.Fori(0, count // UN) as g:
                    turn = g + first // UN
                    if first >= RING:
                        act.wait_ge(onehot_used, g + (first - RING) // UN + 1)
                    act.wait_ge(onehot_act, turn + 1)
                    for s in range(ACT_CHUNKS):
                        c = g * UN + (first + UN - ACT_CHUNKS + s)
                        last = nc.scalar.activation(distance[:, s, :], iota_n[:, 0:HALF], ACT.Abs,
                                                    bias=edge_neg[:, bass.ds(c, 1)])
                    last.then_inc(distance_made, 1)
                    act.wait_ge(distance_made, turn + 1)
                    slot = g * UN + (first % RING + UN - ACT_CHUNKS)
                    nc.scalar.activation(one_dst[:, bass.ds(slot, ACT_CHUNKS), :], distance[:], ACT.Relu, scale=-1.0,
                                         bias=one_col).then_inc(onehot_act, 1)

            transposed_hi(T0, 0)
            split_hi(WK)
            act.wait_ge(consts, 4)
            packed_one_hots(0, RING)
            act.wait_ge(cols_in, 16 * (5 + EXPERTS))
            for j in range(PAIRS):
                act.wait_ge(q_done, j + 1)
                nc.scalar.activation(q_hi[:, j, :], ps[:, j, :], ACT.Identity, bias=bq[:, j:j + 1])\
                  .then_inc(q_hi_made, 1)
            split_hi(WV)
            packed_one_hots(RING, RING)
            for j in range(PAIRS):
                act.wait_ge(k_done, j + 1)
                nc.scalar.activation(k_hi[:, j, :], ps[:, k_bank(j), :], ACT.Identity, bias=bk[:, j:j + 1])\
                  .then_inc(k_hi_made, 1)
            split_hi(WO)
            packed_one_hots(2 * RING, RING)
            packed_one_hots(3 * RING, RING)
            act.wait_ge(digits_made, 1)
            nc.scalar.activation(ct_hi[:], digits[:], ACT.Copy).then_inc(ct_hi_made, 1)
            for t in range(NT):
                act.wait_ge(v_sum, t + 1)
                nc.scalar.activation(vz_hi[:, t].rearrange("p j (w c) -> p j w c", w=3)[:, :, 0:3:2, :],
                                     tmp[:, t, :].rearrange("p (j w c) -> p j w c", j=PAIRS, w=2), ACT.Copy)\
                  .then_inc(v_hi_made, 1)
            split_hi(W1A)

            def exponentials(i):
                if i == 1:
                    act.wait_ge(v_lo_made, NT)
                for g in range(2):
                    if i >= 2:
                        act.wait_ge(p_lo_made, 2 * i + g - 3)
                    act.wait_ge(centred, 2 * i + g + 1)
                    heads = e_two[i % 2][:, g * HEADS // 2:(g + 1) * HEADS // 2]
                    nc.scalar.activation(heads.rearrange("p (w b) n -> p w b n", w=2), group_scores(i, g), ACT.Exp,
                                         scale=SCALE).then_inc(exp_done, 1)

            def attended_hi(half):
                act.wait_ge(pv_done, 2 * NT * (half + 1))
                nc.scalar.activation(T_hi[:, :, half * HN:(half + 1) * HN], attended(), ACT.Copy)\
                  .then_inc(att_hi_made, 1)

            exponentials(0)
            for i in range(STEPS):
                if i + 1 < STEPS:
                    exponentials(i + 1)
                for g in range(2):
                    act.wait_ge(prob_done, 2 * i + g + 1)
                    if g:
                        act.wait_ge(prob_pool, i + 1)
                    if i >= 1:
                        act.wait_ge(pv_done, 2 * i + g - 1)
                    heads = slice(g * HEADS // 2, (g + 1) * HEADS // 2)
                    nc.scalar.activation(p_hi[:, heads], e_two[i % 2][:, heads], ACT.Copy).then_inc(p_hi_made, 1)
                if i == NT:
                    attended_hi(0)
            attended_hi(1)
            for t in range(NT):
                act.wait_ge(c_tr, t + 1)
                nc.scalar.activation(c_hi[:, t, :], ps[:, t, :], ACT.Copy).then_inc(c_hi_made, 1)
            split_hi(W1B)
            transposed_hi(T1, 4)
            for j in range(FT):
                if j == DT:
                    split_hi(W2A)
                act.wait_ge(ff_done, j + 1)
                nc.scalar.activation(ff_hi[:, j, :], ps[:, j, :], ACT.Relu, bias=b1[:, j:j + 1])\
                  .then_inc(ff_hi_made, 1)
            split_hi(W2B)
            split_hi(WN)
            for t in range(NT):
                normalise(LN3, t, h_sb, x_sb, ACT.Relu)
                if t >= 1:
                    transposed_hi(T3, 4, t - 1)
            split_hi(WC)
            transposed_hi(T3, 4, NT - 1)
            for t in range(NT):
                act.wait_ge(beta_done, t + 1)
                nc.scalar.activation(R_hi[:, t, :], ps[:, t, :], ACT.Copy).then_inc(beta_hi_made, 1)
            split_hi(FIRST_EXPERT)
            split_hi(FIRST_EXPERT + 1)
            act.wait_ge(gamma_done, NT)
            for t in range(NT):
                normalise(LN4, t, h_sb, x_sb, ACT.Relu)
                act.wait_ge(ln_out, ln_out_no(LN4, t))
                nc.scalar.activation(R_hi[:, t, :], h_sb[:, t, :], ACT.Copy).then_inc(hr_hi_made, 1)
                if t >= 1:
                    transposed_hi(T4, 0, t - 1)
            transposed_hi(T4, 0, NT - 1)
            for j in range(DT):
                act.wait_ge(agg_sum, j + 1)
                nc.scalar.activation(agg_hi[:, j, :], tmp[:, j, :], ACT.Copy).then_inc(agg_hi_made, 1)
            act.wait_ge(gexp_ask, 1)
            nc.scalar.activation(gate[:], logit[:], ACT.Exp).then_inc(gexp_done, 1)
            for e in range(EXPERTS):
                u = FIRST_EXPERT + 4 * e
                split_hi(u + 2)
                for j in range(DT):
                    act.wait_ge(hid_done, DT * e + j + 1)
                    nc.scalar.activation(hid_hi[:, j, :], ps[:, j, :], ACT.Relu, bias=bl0[:, e, j:j + 1])\
                      .then_inc(hid_hi_made, 1)
                split_hi(u + 3)
                for t in range(NT):
                    act.wait_ge(z_done, NT * e + t + 1)
                    nc.scalar.activation(z_hi[:, t, :], ps[:, 4 + t, :], ACT.Copy).then_inc(z_hi_made, 1)
                split_hi(u + 4)
                if e < EXPERTS - 1:
                    split_hi(u + 5)
                for t in range(NT):
                    act.wait_ge(expert_sum, NT * e + t + 1)
                    nc.scalar.activation(part[:, t, :], part[:, t, :], ACT.Relu, scale=gate[:, t, e:e + 1])\
                      .then_inc(expert_out, 1)
            for t in range(NT):
                normalise(LN5, t, h_sb, x_sb, ACT.Relu)
                if t >= 1:
                    transposed_hi(T5, 0, t - 1)
            transposed_hi(T5, 0, NT - 1)
            for t in range(NT):
                act.wait_ge(H_made, t + 1)
                nc.scalar.activation(R_hi[:, t, :], tmp[:, t, :], ACT.Copy).then_inc(H_hi_made, 1)
            for t in range(NT):
                act.wait_ge(last_sum, t + 1)
                nc.scalar.activation(tmp[:, t, :], tmp[:, t, :], ACT.Relu, scale=isd[:, t:t + 1])\
                  .then_inc(last_relu, 1)

        @block.vector
        def _(v):
            order = [0]

            def link(ins):
                order[0] += 1
                ins.then_inc(dve, 1)
                v.wait_ge(dve, order[0])

            def norm_stats(k, t, src):
                n = ln_no(k, t)
                link(nc.vector.bn_stats(stats[:], src[:, t, :]))
                link(nc.vector.bn_aggr(moments[:, n - 1, :], stats[:]))
                nc.vector.tensor_scalar(vareps[:, n - 1:n], moments[:, n - 1, 1:2], EPS, None, ALU.add)\
                  .then_inc(ln_var, 1)

            def norm_shift(k, t):
                n = ln_no(k, t)
                v.wait_ge(ln_rstd, n)
                nc.vector.scalar_tensor_tensor(shift[:, n - 1:n], moments[:, n - 1, 0:1], -1.0, rstd[:, n - 1:n],
                                               ALU.mult, ALU.mult).then_inc(ln_scale, 1)

            def norm_scaled(k, t, gain, goal, base):
                n = ln_no(k, t)
                link(nc.vector.scalar_tensor_tensor(h_sb[:, t, :], h_sb[:, t, :], moments[:, n - 1, 0:1], gain[:],
                                                    ALU.subtract, ALU.mult))
                v.wait_ge(ln_rstd, n)
                return nc.vector.scalar_tensor_tensor(goal, h_sb[:, t, :], rstd[:, n - 1:n], base, ALU.mult, ALU.add)

            def wait_row(i):
                slot = rows_in[i][1]
                v.wait_ge(row_in[slot], 16 * (1 + sum(s == slot for _, s in rows_in[:i])))
                return row[slot]

            def transposed_lo(k, bank, t):
                v.wait_ge(tr_hi, tr_no(k, t))
                cols = slice(t * P, (t + 1) * P)
                nc.vector.tensor_tensor(T_lo[:, :, cols], ps[:, bank + t, :].rearrange("p (k n) -> p k n", k=DT),
                                        f32(T_hi[:, :, cols]), ALU.subtract).then_inc(tr_lo, 1)

            for t in range(NT):
                v.wait_ge(x_in[t], 16)
                norm_stats(LN0, t, x_sb)
                if t >= 1:
                    norm_shift(LN0, t - 1)
            norm_shift(LN0, NT - 1)

            v.wait_ge(edges_in, 32)
            link(nc.vector.tensor_copy(edge_f[:], edge_i[:]))
            link(nc.vector.tensor_scalar(upper[:], edge_f[:], float(HALF), None, ALU.is_ge))
            link(nc.vector.scalar_tensor_tensor(edge_m[:], upper[:], -float(HALF), edge_f[:], ALU.mult, ALU.add))
            link(nc.vector.tensor_scalar(upper[:, 0, :], upper[:, 0, :], 4.0 ** DIGIT - 1, 1.0, ALU.mult, ALU.add))
            link(nc.vector.tensor_scalar(upper[:, 1, :], upper[:, 1, :], (2.0 ** DIGIT - 1) / W_SCALE, 1 / W_SCALE,
                                         ALU.mult, ALU.add))
            link(nc.vector.tensor_tensor(edge_w[:], upper[:, 0, :], upper[:, 1, :], ALU.mult))
            nc.vector.tensor_scalar(edge_neg[:], edge_m[:, 1, :], -1.0, None, ALU.mult).then_inc(onehot_act, 1)
            v.wait_ge(consts, 4)
            nc.vector.tensor_scalar(neg_ident[:], ident[:], -1.0, None, ALU.mult).then_inc(neg_made, 1)

            def packed_one_hots(first, count):
                with v.Fori(0, count // UN) as g:
                    if first >= RING:
                        v.wait_ge(onehot_used, g + (first - RING) // UN + 1)
                    for s in range(UN):
                        c = g * UN + (first + s)
                        slot = g * UN + (first % RING + s)
                        if s < UN - ACT_CHUNKS:
                            nc.vector.tensor_scalar(one_dst[:, bass.ds(slot, 1), :].squeeze(1), iota_n[:, 0:HALF],
                                                    edge_m[:, 1, bass.ds(c, 1)], None, ALU.is_equal)
                        last = nc.vector.tensor_scalar(one_src[:, bass.ds(slot, 1), :].squeeze(1), iota_n[:, 0:HALF],
                                                       edge_m[:, 0, bass.ds(c, 1)], edge_w[:, bass.ds(c, 1)],
                                                       ALU.is_equal, ALU.mult)
                    last.then_inc(onehot, 1)

            packed_one_hots(0, UN)
            v.wait_ge(hi_made, 1)
            nc.vector.tensor_tensor(w_lo[0][:, 2:4], stage[0][:, 2:4], f32(w_hi[0][:, 2:4]), ALU.subtract)\
              .then_inc(wq_rest_made, 1)
            for t in range(NT):
                transposed_lo(T0, 0, t)
            packed_one_hots(UN, RING // 2 - UN)
            packed_one_hots(RING // 2, RING // 2)
            v.wait_ge(cols_in, 16 * (5 + EXPERTS))
            for j in range(PAIRS):
                v.wait_ge(q_hi_made, j + 1)
                nc.vector.scalar_tensor_tensor(q_lo[:, j, :], ps[:, j, :], bq[:, j:j + 1], f32(q_hi[:, j, :]),
                                               ALU.add, ALU.subtract).then_inc(q_lo_made, 1)
            packed_one_hots(RING, RING)
            packed_one_hots(2 * RING, RING)
            for j in range(PAIRS):
                v.wait_ge(k_hi_made, j + 1)
                nc.vector.scalar_tensor_tensor(k_lo[:, j, :], ps[:, k_bank(j), :], bk[:, j:j + 1],
                                               f32(k_hi[:, j, :]), ALU.add, ALU.subtract).then_inc(k_lo_made, 1)
            packed_one_hots(3 * RING, RING)

            v.wait_ge(onehot_used, CH // UN)
            link(nc.vector.tensor_scalar(packed[:], ps[:, 7, :].rearrange("p (m n) -> p m n", m=2), W_SCALE, 2.0 ** 24,
                                         ALU.mult, ALU.min))
            for src_up in range(2):
                for dst_up in range(2):
                    shift_by = DIGIT * (dst_up + 2 * src_up)
                    last = nc.vector.tensor_scalar(
                        digits[:, 2 * dst_up:2 * dst_up + 2, src_up * HALF:(src_up + 1) * HALF], packed[:], shift_by,
                        2 ** DIGIT - 1 if shift_by < 3 * DIGIT else 2 ** 24 - 1, ALU.logical_shift_right,
                        ALU.bitwise_and)
            last.then_inc(digits_made, 1)
            v.wait_ge(digits_made, 1)
            link(nc.vector.tensor_reduce(in_deg[:], digits[:], AX_X, ALU.add))
            link(nc.vector.tensor_reduce(checked[:, 0:1], in_deg[:], AX_X, ALU.add))
            link(nc.vector.tensor_reduce(checked[:, 1:2], ps[:, 7, :], AX_X, ALU.max))
            link(nc.vector.tensor_scalar(checked[:, 1:2], checked[:, 1:2], 2.0 ** 24 / W_SCALE, -(2.0 ** 24), ALU.is_ge,
                                         ALU.mult))
            nc.vector.tensor_tensor(checked[:, 0:1], checked[:, 0:1], checked[:, 1:2], ALU.add).then_inc(total_ask, 1)
            nc.vector.tensor_scalar(no_edge[:], digits[:], 0.0, FAR, ALU.is_equal, ALU.mult)
            v.wait_ge(total_done, 1)
            nc.vector.tensor_scalar(slow_flag[0:1, :], ps[0:1, 7, 0:1], float(E), None, ALU.not_equal)\
              .then_inc(flag_made, 1)
            v.wait_ge(flag_made, 1)
            slow = v.value_load(slow_flag[0:1, 0:1], min_val=0, max_val=1)
            v.wait_ge(ct_hi_made, 1)
            with v.If(slow > 0):
                def whole_one_hots(s, c):
                    nc.vector.tensor_scalar(all_dst[:, s, :], iota_n[:], edge_f[:, 1, bass.ds(c, 1)], None,
                                            ALU.is_equal)
                    nc.vector.tensor_scalar(all_src[:, s, :], iota_n[:], edge_f[:, 0, bass.ds(c, 1)], None,
                                            ALU.is_equal).then_inc(all_onehot, 1)

                for s in range(UW):
                    whole_one_hots(s, s)
                with v.Fori(1, CH // UW) as g:
                    for s in range(UW):
                        v.wait_ge(all_used, g * UW + (s + 1 - UW))
                        whole_one_hots(s, g * UW + s)
                v.wait_ge(all_used, CH)
                nc.vector.tensor_copy(ct_hi[:], ps[:, 4:8, :]).then_inc(all_copied, 1)
                v.wait_ge(all_copied, 1)
                nc.vector.tensor_tensor(ct_lo[:], ps[:, 4:8, :], f32(ct_hi[:]), ALU.subtract)
                nc.vector.tensor_reduce(in_deg[:], ps[:, 4:8, :], AX_X, ALU.add)
                nc.vector.tensor_scalar(no_edge[:], ps[:, 4:8, :], 0.0, FAR, ALU.is_equal, ALU.mult)\
                  .then_inc(all_copied, 1)
                v.wait_ge(all_copied, 2)
            link(nc.vector.tensor_scalar(inv_in[:], in_deg[:], 1.0, None, ALU.max))
            nc.vector.reciprocal(inv_in[:], inv_in[:]).then_inc(ct_ready, 1)

            bv_row = wait_row(BV)
            for t in range(NT):
                v.wait_ge(v_done, t + 1)
                nc.vector.tensor_tensor(tmp[:, t, :], ps[:, t, :], bv_row[:], ALU.add).then_inc(v_sum, 1)

            def maxima(i):
                v.wait_ge(score_done, i + 1)
                if i >= 1:
                    v.wait_ge(centred, 2 * i)
                low, high = sorted(slot_bank(i, g) for g in range(2))
                if high == low + 2:
                    nc.vector.tensor_reduce(m_bf[:], scores_by_column(low, 4), mybir.AxisListType.XY, ALU.max)\
                      .then_inc(max_done, 1)
                else:
                    nc.vector.tensor_reduce(m_half[:, 0], scores_by_column(low, 2), mybir.AxisListType.XY, ALU.max)
                    link(nc.vector.tensor_reduce(m_half[:, 1], scores_by_column(high, 2), mybir.AxisListType.XY,
                                                 ALU.max))
                    nc.vector.tensor_tensor(m_bf[:], m_half[:, 0], m_half[:, 1], ALU.max).then_inc(max_done, 1)

            def attended_lo(half):
                cols = slice(half * HN, (half + 1) * HN)
                v.wait_ge(att_hi_made, half + 1)
                nc.vector.tensor_tensor(T_lo[:, :, cols], attended(), f32(T_hi[:, :, cols]),
                                        ALU.subtract).then_inc(att_lo_made, 1)

            maxima(0)
            for t in range(NT):
                v.wait_ge(v_hi_made, t + 1)
                hi, lo = (vz[:, t].rearrange("p j (w c) -> p j w c", w=3)[:, :, 0:3:2, :] for vz in (vz_hi, vz_lo))
                nc.vector.tensor_tensor(lo, tmp[:, t, :].rearrange("p (j w c) -> p j w c", j=PAIRS, w=2), f32(hi),
                                        ALU.subtract).then_inc(v_lo_made, 1)
            for i in range(STEPS):
                e = e_two[i % 2]
                if i + 1 < STEPS:
                    maxima(i + 1)
                if i == NT + 1:
                    attended_lo(0)
                v.wait_ge(exp_done, 2 * (i + 1))
                r = rsum[:, i % 2, :]
                if i >= 2:
                    v.wait_ge(prob_done, 2 * (i - 1))
                    v.wait_ge(prob_pool, i - 1)
                link(nc.vector.tensor_reduce(r, e[:].rearrange("p h n -> p n h"), AX_X, ALU.add))
                nc.vector.reciprocal(r, r).then_inc(rinv_made, 1)
                v.wait_ge(rinv_made, i + 1)
                probabilities(nc.vector, i, slice(0, HEADS // 2)).then_inc(prob_done, 1)
                probabilities(nc.vector, i, slice(HEADS // 2, HEADS - POOL_HEADS)).then_inc(prob_done, 1)

            g1_row, be1_row = wait_row(GAMMA1), wait_row(BETA1)

            def h1_start(t):
                v.wait_ge(wo_done, t + 1)
                v.wait_ge(bo_added, t + 1)
                link(nc.vector.tensor_tensor(h_sb[:, t, :], ps[:, 4 + t, :], h_sb[:, t, :], ALU.add))
                norm_stats(LN1, t, h_sb)

            def h1_finish(t):
                norm_scaled(LN1, t, g1_row, h_sb[:, t, :], be1_row[:]).then_inc(h_ready, 1)

            h1_start(0)
            h1_start(1)
            attended_lo(1)
            h1_finish(0)
            h1_start(2)
            h1_finish(1)
            h1_start(3)
            h1_finish(2)
            transposed_lo(T1, 4, 0)
            h1_finish(3)
            for t in range(1, NT):
                transposed_lo(T1, 4, t)

            v.wait_ge(c_hi_made, NT)
            link(nc.vector.tensor_reduce(out_deg[:], f32(c_hi[:]), AX_X, ALU.add))
            for j in range(DT):
                v.wait_ge(ff_hi_made, j + 1)
                link(nc.vector.tensor_scalar(tmp[:, j, :], ps[:, j, :], b1[:, j:j + 1], 0.0, ALU.add, ALU.max))
                nc.vector.tensor_tensor(ff_lo[:, j, :], tmp[:, j, :], f32(ff_hi[:, j, :]),
                                        ALU.subtract).then_inc(ff_lo_made, 1)
            v.wait_ge(ff_lo_made, DT)
            for j in range(DT, FT):
                v.wait_ge(ff_hi_made, j + 1)
                link(nc.vector.tensor_scalar(tmp[:, j - DT, :], ps[:, j, :], b1[:, j:j + 1], 0.0, ALU.add, ALU.max))
                nc.vector.tensor_tensor(ff_lo[:, j, :], tmp[:, j - DT, :], f32(ff_hi[:, j, :]),
                                        ALU.subtract).then_inc(ff_lo_made, 1)
            with v.If(slow > 0):
                v.wait_ge(c_lo_tr, NT)
                nc.vector.tensor_copy(c_lo[:], ps[:, 4:8, :]).then_inc(c_lo_made, 1)
                v.wait_ge(c_lo_made, 1)
                nc.vector.tensor_reduce(inv_out[:], f32(c_lo[:]), AX_X, ALU.add).then_inc(c_lo_made, 1)
                v.wait_ge(c_lo_made, 2)
                nc.vector.tensor_tensor(out_deg[:], out_deg[:], inv_out[:], ALU.add).then_inc(c_lo_made, 1)
                v.wait_ge(c_lo_made, 3)
            link(nc.vector.reciprocal(no_edge_nan[:], out_deg[:]))
            link(nc.vector.tensor_scalar(no_edge_nan[:], no_edge_nan[:], 0.0, None, ALU.mult))
            link(nc.vector.tensor_scalar(out_deg[:], out_deg[:], 1.0, None, ALU.max))
            link(nc.vector.reciprocal(inv_out[:], out_deg[:]))
            nc.vector.tensor_scalar(isd[:], in_deg[:], 1.0, None, ALU.add).then_inc(pow_ask, 1)
            v.wait_ge(ff_lo_made, FT)
            for t in range(NT):
                nc.vector.tensor_scalar(tmp[:, t, 0:P], ident[:], inv_in[:, t:t + 1], None, ALU.mult)\
                  .then_inc(diag_made, 1)
            v.wait_ge(deg_done, 1)
            nc.vector.tensor_copy(inv_in_row[:], ps[:, 4, :]).then_inc(deg_made, 1)

            g2_row = wait_row(GAMMA2)

            def x1_finish(t):
                v.wait_ge(be2_added, t + 1)
                link(norm_scaled(LN2, t, g2_row, x_sb[:, t, :], x_sb[:, t, :]))
                norm_stats(LN3, t, x_sb)

            for t in range(NT):
                v.wait_ge(w2_done, t + 1)
                v.wait_ge(b2_added, t + 1)
                ins = nc.vector.tensor_tensor(h_sb[:, t, :], ps[:, t, :], h_sb[:, t, :], ALU.add)
                ins.then_inc(y2_read, 1)
                v.wait_ge(y2_read, t + 1)
                norm_stats(LN2, t, h_sb)
                if t >= 2:
                    norm_shift(LN3, t - 2)
                if t >= 1:
                    x1_finish(t - 1)
            norm_shift(LN3, NT - 2)
            transposed_lo(T3, 4, 0)
            x1_finish(NT - 1)
            norm_shift(LN3, NT - 1)
            for t in range(1, NT):
                transposed_lo(T3, 4, t)

            for t in range(NT):
                v.wait_ge(beta_hi_made, t + 1)
                nc.vector.tensor_tensor(R_lo[:, t, :], ps[:, t, :], f32(R_hi[:, t, :]), ALU.subtract)\
                  .then_inc(beta_lo_made, 1)
            v.wait_ge(cols_in, 16 * (5 + EXPERTS))
            link(nc.vector.tensor_copy(gw_hi[:], gate_w[:]))
            nc.vector.tensor_tensor(gw_lo[:], gate_w[:], f32(gw_hi[:]), ALU.subtract).then_inc(gate_split, 1)
            for t in range(NT):
                v.wait_ge(alpha_done, t + 1)
                v.wait_ge(bias1_added, t + 1)
                nc.vector.tensor_tensor(x_sb[:, t, :], ps[:, 4 + t, :], x_sb[:, t, :], ALU.add)\
                  .then_inc(alpha_added, 1)
            v.wait_ge(alpha_added, NT)

            def row_lo(t):
                v.wait_ge(hr_hi_made, t + 1)
                nc.vector.tensor_tensor(R_lo[:, t, :], h_sb[:, t, :], f32(R_hi[:, t, :]), ALU.subtract)\
                  .then_inc(hr_lo_made, 1)

            for t in range(NT + 3):
                if t < NT:
                    v.wait_ge(gamma_done, t + 1)
                    ins = nc.vector.scalar_tensor_tensor(x_sb[:, t, :], ps[:, t, :], inv_out[:, t:t + 1],
                                                         x_sb[:, t, :], ALU.mult, ALU.add)
                    ins.then_inc(x2_made, 1)
                    v.wait_ge(x2_made, t + 1)
                    norm_stats(LN4, t, x_sb)
                if 1 <= t <= NT:
                    norm_shift(LN4, t - 1)
                if 2 <= t < NT + 2:
                    row_lo(t - 2)
                if t >= 3:
                    transposed_lo(T4, 0, t - 3)

            for j in range(DT):
                v.wait_ge(agg_done, j + 1)
                nc.vector.tensor_tensor(tmp[:, j, :], ps[:, 4 + j, :], inv_in_row[:], ALU.mult).then_inc(agg_sum, 1)
                v.wait_ge(agg_hi_made, j + 1)
                nc.vector.tensor_tensor(agg_lo[:, j, :], tmp[:, j, :], f32(agg_hi[:, j, :]), ALU.subtract)\
                  .then_inc(agg_lo_made, 1)

            def over_experts(a):
                return a[:].unsqueeze(2).to_broadcast([P, NT, EXPERTS])

            v.wait_ge(logits_done, 1)
            ins = nc.vector.tensor_tensor(logit[:], ps[:, 3, 0:NT * EXPERTS].rearrange("p (t e) -> p t e", t=NT),
                                          gate_b[:].unsqueeze(1).to_broadcast([P, NT, EXPERTS]), ALU.add)
            ins.then_inc(logits_out, 1)
            v.wait_ge(logits_out, 1)
            link(nc.vector.tensor_reduce(gmax[:], logit[:], AX_X, ALU.max))
            nc.vector.tensor_tensor(logit[:], logit[:], over_experts(gmax), ALU.subtract).then_inc(gexp_ask, 1)
            v.wait_ge(gexp_done, 1)
            link(nc.vector.tensor_reduce(gsum[:], gate[:], AX_X, ALU.add))
            link(nc.vector.reciprocal(gsum[:], gsum[:]))
            link(nc.vector.tensor_tensor(gate[:], gate[:], over_experts(gsum), ALU.mult))
            for e in range(EXPERTS):
                others = [o for o in range(EXPERTS) if o != e]
                for o in others:
                    goal = rank[:, :, e] if o == others[0] else beats[:]
                    link(nc.vector.tensor_tensor(goal, gate[:, :, o], gate[:, :, e],
                                                 ALU.is_ge if o < e else ALU.is_gt))
                    if o != others[0]:
                        link(nc.vector.tensor_tensor(rank[:, :, e], rank[:, :, e], beats[:], ALU.add))
            link(nc.vector.scalar_tensor_tensor(gate[:], rank[:], TOP_K - 0.5, gate[:], ALU.is_lt, ALU.mult))

            for e in range(EXPERTS):
                if e == 0:
                    v.wait_ge(agg_lo_made, DT)
                else:
                    v.wait_ge(hid_lo_made, DT * e)
                for j in range(DT):
                    v.wait_ge(hid_hi_made, DT * e + j + 1)
                    link(nc.vector.tensor_scalar(tmp[:, j, :], ps[:, j, :], bl0[:, e, j:j + 1], 0.0,
                                                 ALU.add, ALU.max))
                    nc.vector.tensor_tensor(hid_lo[:, j, :], tmp[:, j, :], f32(hid_hi[:, j, :]), ALU.subtract)\
                      .then_inc(hid_lo_made, 1)
                for t in range(NT):
                    v.wait_ge(z_hi_made, NT * e + t + 1)
                    nc.vector.tensor_tensor(z_lo[:, t, :], ps[:, 4 + t, :], f32(z_hi[:, t, :]), ALU.subtract)\
                      .then_inc(z_lo_made, 1)
                v.wait_ge(bl_in[e % 2], 16 * (e // 2 + 1))
                if e >= 1:
                    v.wait_ge(x3_made, NT * e)
                for t in range(NT):
                    v.wait_ge(own_done, NT * e + t + 1)
                    nc.vector.tensor_tensor(part[:, t, :], ps[:, t, :], row_bl[e % 2][:], ALU.add)\
                      .then_inc(own_made, 1)
                v.wait_ge(own_made, NT * (e + 1))

                def add_expert(t):
                    v.wait_ge(expert_out, NT * e + t + 1)
                    ins = nc.vector.tensor_tensor(x_sb[:, t, :], x_sb[:, t, :], part[:, t, :], ALU.add)
                    ins.then_inc(x3_made, 1)
                    if e == EXPERTS - 1:
                        v.wait_ge(x3_made, NT * e + t + 1)
                        norm_stats(LN5, t, x_sb)

                for t in range(NT):
                    v.wait_ge(near_done, NT * e + t + 1)
                    nc.vector.scalar_tensor_tensor(part[:, t, :], ps[:, 4 + t, :], inv_in[:, t:t + 1], part[:, t, :],
                                                   ALU.mult, ALU.add).then_inc(expert_sum, 1)
                    if t >= 1:
                        add_expert(t - 1)
                    if e == EXPERTS - 1 and t >= 2:
                        norm_shift(LN5, t - 2)
                add_expert(NT - 1)
            norm_shift(LN5, NT - 2)
            norm_shift(LN5, NT - 1)
            for t in range(NT):
                transposed_lo(T5, 0, t)

            b3_row = wait_row(B3)
            v.wait_ge(pow_made, 1)
            for t in range(NT):
                v.wait_ge(H_done, t + 1)
                link(nc.vector.tensor_tensor(tmp[:, t, :], ps[:, 4 + t, :], b3_row[:], ALU.add))
                nc.vector.tensor_scalar(tmp[:, t, :], tmp[:, t, :], isd[:, t:t + 1], None, ALU.mult)\
                  .then_inc(H_made, 1)
                v.wait_ge(H_hi_made, t + 1)
                nc.vector.tensor_tensor(R_lo[:, t, :], tmp[:, t, :], f32(R_hi[:, t, :]), ALU.subtract)\
                  .then_inc(H_lo_made, 1)
            v.wait_ge(H_lo_made, NT)

            def finish(t):
                v.wait_ge(last_relu, t + 1)
                nc.vector.scalar_tensor_tensor(x_sb[:, t, :], tmp[:, t, :], no_edge_nan[:, t:t + 1], x_sb[:, t, :],
                                               ALU.add, ALU.add).then_inc(x4_made, 1)

            for t in range(NT):
                v.wait_ge(last_done, t + 1)
                nc.vector.tensor_tensor(tmp[:, t, :], ps[:, t, :], tmp[:, t, :], ALU.add).then_inc(last_sum, 1)
                if t >= 1:
                    finish(t - 1)
            finish(NT - 1)

        @block.tensor
        def _(pe):
            def mm3(goal, a_hi, a_lo, b_hi, b_lo, start, stop, **kw):
                nc.tensor.matmul(goal, a_hi, b_hi, start=start, stop=False, **kw)
                nc.tensor.matmul(goal, a_hi, b_lo, start=False, stop=False, **kw)
                return nc.tensor.matmul(goal, a_lo, b_hi, start=False, stop=stop, **kw)

            def weights(u):
                pe.wait_ge(lo_made, u + 1)
                return w_hi[u % 2], w_lo[u % 2]

            def col(t):
                return slice(t * P, (t + 1) * P)

            def transposes(bank, t):
                for j in range(DT):
                    last = nc.tensor.transpose(ps[:, bank + t, col(j)], h_sb[:, t, col(j)], ident[:])
                last.then_inc(tr_done, 1)

            def rows_tile(bank, t, w, done):
                for k in range(DT):
                    last = mm3(ps[:, bank + t, :], T_hi[:, k, col(t)], T_lo[:, k, col(t)], w[0][:, k, :],
                               w[1][:, k, :], k == 0, k == DT - 1)
                last.then_inc(done, 1)

            def sums_over_edges(bank, counts_hi, counts_lo, r_hi, r_lo, ready, value, together, done):
                def products(k, t):
                    goal = ps[:, bank + t, :]
                    nc.tensor.matmul(goal, counts_hi[:, k, col(t)], r_hi[:, k, :], start=k == 0, stop=False)
                    return nc.tensor.matmul(goal, counts_hi[:, k, col(t)], r_lo[:, k, :], start=False,
                                            stop=k == NT - 1)

                for k in range(together):
                    pe.wait_ge(ready, value + k + 1)
                    for t in range(NT):
                        products(k, t)
                    if k == 0:
                        with pe.If(slow > 0):
                            pe.wait_ge(ready, value + NT)
                            for t in range(NT):
                                for kk in range(NT):
                                    nc.tensor.matmul(ps[:, bank + t, :], counts_lo[:, kk, col(t)], r_hi[:, kk, :],
                                                     start=False, stop=False, skip_group_check=True)
                pe.wait_ge(ready, value + NT)
                for t in range(NT):
                    for k in range(together, NT):
                        last = products(k, t)
                    last.then_inc(done, 1)

            def count_segment(n):
                with pe.Fori(0, RING // UN) as g:
                    pe.wait_ge(onehot, g + (n * (RING // UN) + 1))
                    pe.wait_ge(onehot_act, g + (n * (RING // UN) + 2))
                    for s in range(UN):
                        rows = one_src[:, bass.ds(g * UN + s, 1), :].squeeze(1)
                        for m in range(2):
                            cols = one_dst[:, bass.ds(g * UN + s, 1), m * P:(m + 1) * P].squeeze(1)
                            last = nc.tensor.matmul(ps[:, 7, m * HALF:(m + 1) * HALF], cols, rows,
                                                    start=False, stop=False, skip_group_check=True)
                    last.then_inc(onehot_used, 1)

            for t in range(NT):
                pe.wait_ge(ln_out, ln_out_no(LN0, t))
                pe.wait_ge(consts, 4)
                transposes(0, t)
            pe.wait_ge(zero_made, 1)
            nc.tensor.matmul(ps[:, 7, :], zeros[:, 0:P], zeros[:], start=True, stop=False, skip_group_check=True)
            pe.wait_ge(tr_lo, tr_no(T0, NT - 1))
            hi, lo = weights(WQ)
            pe.wait_ge(wq_rest_made, 1)
            for j in range(DT):
                for k in range(DT):
                    last = mm3(ps[:, j, :], hi[:, k, col(j)], lo[:, k, col(j)], T_hi[:, k, :], T_lo[:, k, :],
                               k == 0, k == DT - 1)
                last.then_inc(q_done, 1)
            count_segment(0)
            hi, lo = weights(WK)
            for j in range(DT):
                if k_bank(j) == 0:
                    pe.wait_ge(q_lo_made, 1)
                for k in range(DT):
                    last = mm3(ps[:, k_bank(j), :], hi[:, k, col(j)], lo[:, k, col(j)], T_hi[:, k, :], T_lo[:, k, :],
                               k == 0, k == DT - 1)
                last.then_inc(k_done, 1)
            count_segment(1)
            count_segment(2)
            pe.wait_ge(q_lo_made, PAIRS)
            pe.wait_ge(k_lo_made, PAIRS)
            w = weights(WV)
            for t in range(NT // 2):
                rows_tile(0, t, w, v_done)
            count_segment(3)
            for t in range(NT // 2, NT):
                rows_tile(0, t, w, v_done)
            pe.wait_ge(total_ask, 1)
            nc.tensor.matmul(ps[0:1, 7, 0:1], checked[:, 0:1], one_col, start=True, stop=True).then_inc(total_done, 1)
            pe.wait_ge(flag_made, 1)
            slow = pe.value_load(slow_flag[0:1, 0:1], min_val=0, max_val=1)
            with pe.If(slow > 0):
                def count(slot, value, start):
                    pe.wait_ge(all_onehot, value)
                    for t in range(NT):
                        last = nc.tensor.matmul(ps[:, 4 + t, :], all_dst[:, slot, col(t)], all_src[:, slot, :],
                                                start=start, stop=False, skip_group_check=True)
                    last.then_inc(all_used, 1)

                for s in range(UW):
                    count(s, s + 1, s == 0)
                with pe.Fori(1, CH // UW) as g:
                    for s in range(UW):
                        count(s, g * UW + (s + 1), False)
                pe.wait_ge(all_copied, 2)

            def twice(a):
                return a.unsqueeze(1).to_broadcast([P, 2, HN])

            def scores(i, g):
                mt, half, n = i % NT, i // NT, 2 * i + g
                if n == 0:
                    pe.wait_ge(neg_made, 1)
                    pe.wait_ge(ct_ready, 1)
                elif n == 2:
                    pe.wait_ge(v_sum, NT)
                elif n > 2:
                    pe.wait_ge(exp_done, n - 2)
                q = slice(half * HN, (half + 1) * HN)
                for b in range(2):
                    nc.tensor.matmul(ps[:, slot_bank(i, g) + b, :], neg_ident[:], twice(no_edge[:, mt, q]),
                                     start=True, stop=False, skip_group_check=True)
                for h in range(4 * g, 4 * g + 4):
                    rows, j = slice(HD * (h % 2), HD * (h % 2 + 1)), h // 2
                    last = mm3(score_of(i, h), k_hi[rows, j, col(mt)], k_lo[rows, j, col(mt)], q_hi[rows, j, q],
                               q_lo[rows, j, q], False, False, skip_group_check=True)
                if g:
                    last.then_inc(score_done, 1)

            def centre(i, g):
                pe.wait_ge(max_done, i + 1)
                for b in range(2):
                    last = nc.tensor.matmul(ps[:, slot_bank(i, g) + b, :], neg_ident[:], twice(m_bf[:]), start=False,
                                            stop=True, skip_group_check=True)
                last.then_inc(centred, 1)

            def values(i, part_no):
                mt = i % NT
                if i == 0:
                    pe.wait_ge(v_lo_made, NT)
                    pe.wait_ge(vz_zero, 2)
                if i == NT:
                    pe.wait_ge(att_lo_made, 1)
                pe.wait_ge(p_lo_made, 2 * i + part_no + 1)
                for h in range(4 * part_no, 4 * part_no + 4):
                    cols = slice(HD * (h % 2), HD * (h % 2) + P)
                    goal = ps[:, h // 4, (h // 2 % 2) * HN:(h // 2 % 2 + 1) * HN]
                    last = mm3(goal, vz_hi[:, mt, h // 2, cols], vz_lo[:, mt, h // 2, cols], p_hi[:, h, :],
                               p_lo[:, h, :], mt == 0 and h % 4 == 0, mt == NT - 1 and h % 4 == 3,
                               skip_group_check=True)
                last.then_inc(pv_done, 1)

            scores(0, 0)
            scores(0, 1)
            scores(1, 0)
            for i in range(STEPS):
                centre(i, 0)
                centre(i, 1)
                if i >= 2:
                    values(i - 2, 0)
                if i + 1 < STEPS:
                    scores(i + 1, 1)
                if i >= 2:
                    values(i - 2, 1)
                if i + 2 < STEPS:
                    scores(i + 2, 0)
            values(STEPS - 2, 0)
            values(STEPS - 2, 1)

            pe.wait_ge(exp_done, 2 * STEPS)
            w = weights(WO)
            for t in range(NT // 2):
                rows_tile(4, t, w, wo_done)
            values(STEPS - 1, 0)
            values(STEPS - 1, 1)
            pe.wait_ge(att_lo_made, 2)
            for t in range(NT // 2, NT):
                rows_tile(4, t, w, wo_done)

            def count_transposes(src, bank, done):
                for s in range(NT):
                    for t in range(NT):
                        last = nc.tensor.transpose(ps[:, bank + s, col(t)], f32(src[:, t, col(s)]), ident[:])
                    last.then_inc(done, 1)

            count_transposes(ct_hi, 0, c_tr)

            for t in range(NT):
                pe.wait_ge(h_ready, t + 1)
                transposes(4, t)
            for j in range(DT):
                pe.wait_ge(c_hi_made, j + 1)
            hi, lo = weights(W1A)
            for half in range(2):
                pe.wait_ge(tr_lo, tr_no(T1, 2 * half + 1))
                n = slice(half * HN, (half + 1) * HN)
                for j in range(DT):
                    for k in range(DT):
                        last = mm3(ps[:, j, n], hi[:, k, col(j)], lo[:, k, col(j)], T_hi[:, k, n], T_lo[:, k, n],
                                   half == 0 and k == 0, k == DT - 1, skip_group_check=True)
                    if half:
                        last.then_inc(ff_done, 1)
            hi, lo = weights(W1B)
            for j in range(DT, FT):
                for k in range(DT):
                    last = mm3(ps[:, j, :], hi[:, k, col(j - DT)], lo[:, k, col(j - DT)],
                               T_hi[:, k, :], T_lo[:, k, :], k == 0, k == DT - 1)
                last.then_inc(ff_done, 1)
            for half in range(2):
                hi, lo = weights(W2A + half)
                pe.wait_ge(ff_lo_made, DT * (half + 1))
                for t in range(NT):
                    for k in range(DT):
                        f = half * DT + k
                        last = mm3(ps[:, t, :], ff_hi[:, f, col(t)], ff_lo[:, f, col(t)], hi[:, k, :],
                                   lo[:, k, :], f == 0, f == FT - 1)
                    last.then_inc(w2_done if half else w2_half_done, 1)
                if half == 0:
                    with pe.If(slow > 0):
                        pe.wait_ge(ff_lo_made, FT)
                        count_transposes(ct_lo, 4, c_lo_tr)
                        pe.wait_ge(c_lo_made, 1)
                    pe.wait_ge(diag_made, NT)
                    pe.wait_ge(ones_made, 1)
                    for t in range(NT):
                        last = nc.tensor.matmul(ps[:, 4, col(t)], ones[:], tmp[:, t, 0:P], start=True, stop=True)
                    last.then_inc(deg_done, 1)

            pe.wait_ge(deg_made, 1)
            w = weights(WN)
            for t in range(NT):
                pe.wait_ge(ln_out, ln_out_no(LN3, t))
                transposes(4, t)
                if t >= 1:
                    pe.wait_ge(tr_lo, tr_no(T3, t - 1))
                    pe.wait_ge(y2_read, t)
                    rows_tile(0, t - 1, w, beta_done)
            pe.wait_ge(tr_lo, tr_no(T3, NT - 1))
            pe.wait_ge(y2_read, NT)
            rows_tile(0, NT - 1, w, beta_done)
            w = weights(WC)
            for t in range(NT):
                rows_tile(4, t, w, alpha_done)
            pe.wait_ge(beta_lo_made, NT)
            sums_over_edges(0, ct_hi, ct_lo, R_hi, R_lo, beta_lo_made, 0, 1, gamma_done)

            pe.wait_ge(alpha_added, NT)
            for k in range(NT):
                pe.wait_ge(ln_out, ln_out_no(LN4, k))
                transposes(0, k)
                pe.wait_ge(hr_lo_made, k + 1)
                for j in range(DT):
                    goal = ps[:, 4 + j, :]
                    nc.tensor.matmul(goal, R_hi[:, k, col(j)], c_hi[:, k, :], start=k == 0, stop=False)
                    last = nc.tensor.matmul(goal, R_lo[:, k, col(j)], c_hi[:, k, :], start=False, stop=k == NT - 1)
                    if k == NT - 1:
                        last.then_inc(agg_done, 1)
                if k == NT - 2:
                    with pe.If(slow > 0):
                        for j in range(DT):
                            for kk in range(NT - 1):
                                nc.tensor.matmul(ps[:, 4 + j, :], R_hi[:, kk, col(j)], c_lo[:, kk, :],
                                                 start=False, stop=False, skip_group_check=True)
                        pe.wait_ge(hr_lo_made, NT)
                        for j in range(DT):
                            nc.tensor.matmul(ps[:, 4 + j, :], R_hi[:, NT - 1, col(j)], c_lo[:, NT - 1, :],
                                             start=False, stop=False, skip_group_check=True)
            pe.wait_ge(tr_lo, tr_no(T4, NT - 1))
            pe.wait_ge(gate_split, 1)
            for t in range(NT):
                for k in range(DT):
                    last = mm3(ps[:, 3, t * EXPERTS:(t + 1) * EXPERTS], T_hi[:, k, col(t)], T_lo[:, k, col(t)],
                               gw_hi[:, k, :], gw_lo[:, k, :], k == 0, k == DT - 1)
            last.then_inc(logits_done, 1)

            for e in range(EXPERTS):
                for n, (a_hi, a_lo) in enumerate(((T_hi, T_lo), (agg_hi, agg_lo))):
                    hi, lo = weights(FIRST_EXPERT + 4 * e + n)
                    if n == 0 and e >= 1:
                        pe.wait_ge(own_made, NT * e)
                    for j in range(DT):
                        if n == 0 and e == 0 and j == 3:
                            pe.wait_ge(logits_out, 1)
                        if n == 1 and e == 0 and j == 0:
                            pe.wait_ge(agg_lo_made, DT)
                        for k in range(DT):
                            last = mm3(ps[:, j, :], hi[:, k, col(j)], lo[:, k, col(j)], a_hi[:, k, :],
                                       a_lo[:, k, :], n == 0 and k == 0, n == 1 and k == DT - 1)
                        last.then_inc(hid_done if n else hid_half_done, 1)
                hi, lo = weights(FIRST_EXPERT + 4 * e + 2)
                if e >= 1:
                    pe.wait_ge(expert_sum, NT * e)
                for k in range(DT):
                    pe.wait_ge(hid_lo_made, DT * e + k + 1)
                    for t in range(NT):
                        last = mm3(ps[:, 4 + t, :], hid_hi[:, k, col(t)], hid_lo[:, k, col(t)], hi[:, k, :],
                                   lo[:, k, :], k == 0, k == DT - 1)
                        if k == DT - 1:
                            last.then_inc(z_done, 1)
                hi, lo = weights(FIRST_EXPERT + 4 * e + 3)
                for t in range(NT):
                    for k in range(DT):
                        last = mm3(ps[:, t, :], hid_hi[:, k, col(t)], hid_lo[:, k, col(t)], hi[:, k, :],
                                   lo[:, k, :], k == 0, k == DT - 1)
                    last.then_inc(own_done, 1)
                pe.wait_ge(z_lo_made, NT * (e + 1))
                sums_over_edges(4, c_hi, c_lo, z_hi, z_lo, z_lo_made, NT * e, 1, near_done)

            pe.wait_ge(own_made, NT * EXPERTS)
            w = weights(W_LAST)
            for t in range(NT):
                pe.wait_ge(ln_out, ln_out_no(LN5, t))
                transposes(0, t)
                if t >= 1:
                    pe.wait_ge(tr_lo, tr_no(T5, t - 1))
                    pe.wait_ge(expert_sum, NT * (EXPERTS - 1) + t)
                    rows_tile(4, t - 1, w, H_done)
            pe.wait_ge(tr_lo, tr_no(T5, NT - 1))
            rows_tile(4, NT - 1, w, H_done)
            sums_over_edges(0, c_hi, c_lo, R_hi, R_lo, H_lo_made, 0, 2, last_done)


_INS = ["x", "src", "dst",
        *(f"L0_gnn_{n}" for n in ("Wq", "bq", "Wk", "bk", "Wv", "bv", "Wo", "bo", "W1", "b1", "W2", "b2", "g1",
                                  "be1", "g2", "be2")),
        "L1_gnn_wc", "L1_gnn_wn", "L1_gnn_bias",
        *(f"L2_gnn_{n}" for n in ("gate_W", "gate_b", "Wl", "bl", "Wr")), "L3_gnn_W", "L3_gnn_b"]


def kernel(**inputs):
    import concourse.bacc as bacc
    from concourse.bass_utils import run_bass_kernel_spmd

    nc = bacc.Bacc("TRN2", target_bir_lowering=False, num_devices=1)
    arrays, d = {}, {}
    for name in _INS:
        a = np.ascontiguousarray(inputs[name])
        arrays[f"in_{name}"] = a
        d[name] = nc.dram_tensor(f"in_{name}", a.shape, mybir.dt.from_np(a.dtype), kind="ExternalInput").ap()
    out = nc.dram_tensor("out", arrays["in_x"].shape, F32, kind="ExternalOutput").ap()
    build(nc, d, out)
    r = run_bass_kernel_spmd(nc, [arrays], core_ids=[0])
    return r.results[0]["out"]
```
